# Optimizing a Trainium2 kernel written in Bass

```python
import numpy as np
import jax
import jax.numpy as jnp

def _softmax(x, axis=-1):
    return jax.nn.softmax(x, axis=axis)

def _gelu(x):
    return jax.nn.gelu(x, approximate=True)

def _silu(x):
    return jax.nn.silu(x)

def _sigmoid(x):
    return jax.nn.sigmoid(x)

def _layernorm(x, axis=-1, eps=1e-05):
    m = jnp.mean(x, axis=axis, keepdims=True)
    v = jnp.var(x, axis=axis, keepdims=True)
    return (x - m) / jnp.sqrt(v + eps)

def _scatter_add(tgt, idx, src, axis=0):
    return tgt.at[idx].add(src)

def _segment_sum(src, seg, n):
    return jax.ops.segment_sum(src, seg, n)
kernel_name = 'mk_xattn_ffn_d1_seqx_r4_3d6867'

def setup_inputs(seed: int=0):
    np.random.seed(seed)
    _w = jnp.asarray

    def _rec_inputs():
        import jax
        import jax.numpy as jnp
        _rk = jax.random.key(seed)
        x = 7.22e-05 + 1 * jax.random.normal(jax.random.fold_in(_rk, 1), (8, 512, 256), jnp.float32)
        _lenS = 512 - jax.random.randint(jax.random.fold_in(_rk, 7), (8,), 0, max(1, 512 // 4) + 1, jnp.int32)
        _lenS2 = 512 - jax.random.randint(jax.random.fold_in(_rk, 8), (8,), 0, max(1, 512 // 4) + 1, jnp.int32)
        _ctx_1024P = jax.random.normal(jax.random.fold_in(_rk, 11), (8, 16, 256), jnp.float32)
        _ctx_1024c = jax.random.dirichlet(jax.random.fold_in(_rk, 511), 0.3 * jnp.ones((16,), jnp.float32), (8, 512))
        _ctx_1024t = jnp.einsum('bsk,bkd->bsd', _ctx_1024c, _ctx_1024P)
        _ctx_1024t = _ctx_1024t * jax.lax.rsqrt(jnp.mean(jnp.square(_ctx_1024t)) + 1e-12) * 0.953939
        ctx_1024 = -0.000514642 + 1.00011 * (_ctx_1024t + 0.3 * jax.random.normal(jax.random.fold_in(_rk, 611), (8, 512, 256), jnp.float32))
        return (x, ctx_1024)
    x, ctx_1024 = _rec_inputs()

    def _L0_xattn_setup():
        import jax, jax.numpy as jnp
        import numpy as np
        B, L_ENC, L_DEC, D = (16, 128, 128, 256)
        key = jax.random.key(seed)
        k1, k2, k3, k4, k5, k6 = jax.random.split(key, 6)
        encoder_hc = jax.random.normal(k1, (B, L_ENC, D), dtype=jnp.float32)
        decoder_hq = jax.random.normal(k2, (B, L_DEC, D), dtype=jnp.float32)
        w_sim = jax.random.normal(k3, (3 * D,), dtype=jnp.float32) * 0.02
        b_sim = jax.random.normal(k4, (1,), dtype=jnp.float32) * 0.02
        W_qv = jax.random.normal(k5, (4 * D, D), dtype=jnp.float32) * 0.02
        b_qv = jax.random.normal(k6, (D,), dtype=jnp.float32) * 0.02
        return {'encoder_hc': encoder_hc, 'decoder_hq': decoder_hq, 'w_sim': w_sim, 'b_sim': b_sim, 'W_qv': W_qv, 'b_qv': b_qv}
    _L0_xattn_all = _L0_xattn_setup()
    _L0_xattn_in = {k: v for k, v in _L0_xattn_all.items() if k in ('w_sim', 'b_sim', 'W_qv', 'b_qv')}
    del _L0_xattn_all

    def _L0_ffn_setup():
        import jax, jax.numpy as jnp
        import numpy as np
        QK_SCALE = 10.0
        NEG_INF = -1000000000.0

        def layernorm(x, g, b, eps=1e-05):
            mu = jnp.mean(x, axis=-1, keepdims=True)
            var = jnp.var(x, axis=-1, keepdims=True)
            return (x - mu) * jax.lax.rsqrt(var + eps) * g + b

        def l2norm(x, eps=1e-12):
            return x / jnp.sqrt(jnp.sum(x * x, axis=-1, keepdims=True) + eps)
        key = jax.random.key(seed)
        ks = jax.random.split(key, 10)
        B, S, D, H, DH, E, FF = (2, 256, 256, 16, 64, 8, 1024)
        sd = lambda fan: 1.0 / np.sqrt(fan)
        return {'x': jax.random.normal(ks[0], (B, S, D), jnp.float32), 'ln_g': jnp.ones((D,), jnp.float32), 'ln_b': jnp.zeros((D,), jnp.float32), 'Wq': jax.random.normal(ks[1], (D, H * DH), jnp.float32) * sd(D), 'Wk': jax.random.normal(ks[2], (D, H * DH), jnp.float32) * sd(D), 'Wv': jax.random.normal(ks[3], (D, H * DH), jnp.float32) * sd(D), 'q_scale': jnp.ones((H, 1, DH), jnp.float32), 'k_scale': jnp.ones((H, 1, DH), jnp.float32), 'Wo': jax.random.normal(ks[4], (H * DH, D), jnp.float32) * sd(H * DH), 'gate_w': jax.random.normal(ks[5], (D, E), jnp.float32) * sd(D), 'gate_b': jnp.zeros((E,), jnp.float32), 'w1': jax.random.normal(ks[6], (E, D, FF), jnp.float32) * sd(D), 'b1': jnp.zeros((E, FF), jnp.float32), 'w2': jax.random.normal(ks[7], (E, FF, D), jnp.float32) * sd(FF), 'b2': jnp.zeros((E, D), jnp.float32)}
    _L0_ffn_all = _L0_ffn_setup()
    _L0_ffn_in = {k: v for k, v in _L0_ffn_all.items() if k in ('ln_g', 'ln_b', 'Wq', 'Wk', 'Wv', 'q_scale', 'k_scale', 'Wo', 'gate_w', 'gate_b', 'w1', 'b1', 'w2', 'b2')}
    del _L0_ffn_all
    return {'x': x, 'ctx_1024': ctx_1024, 'L0_xattn_w_sim': _L0_xattn_in['w_sim'], 'L0_xattn_b_sim': _L0_xattn_in['b_sim'], 'L0_xattn_W_qv': _L0_xattn_in['W_qv'], 'L0_xattn_b_qv': _L0_xattn_in['b_qv'], 'L0_ffn_ln_g': _L0_ffn_in['ln_g'], 'L0_ffn_ln_b': _L0_ffn_in['ln_b'], 'L0_ffn_Wq': _L0_ffn_in['Wq'], 'L0_ffn_Wk': _L0_ffn_in['Wk'], 'L0_ffn_Wv': _L0_ffn_in['Wv'], 'L0_ffn_q_scale': _L0_ffn_in['q_scale'], 'L0_ffn_k_scale': _L0_ffn_in['k_scale'], 'L0_ffn_Wo': _L0_ffn_in['Wo'], 'L0_ffn_gate_w': _L0_ffn_in['gate_w'], 'L0_ffn_gate_b': _L0_ffn_in['gate_b'], 'L0_ffn_w1': _L0_ffn_in['w1'], 'L0_ffn_b1': _L0_ffn_in['b1'], 'L0_ffn_w2': _L0_ffn_in['w2'], 'L0_ffn_b2': _L0_ffn_in['b2']}

def reference(x, ctx_1024, L0_xattn_w_sim, L0_xattn_b_sim, L0_xattn_W_qv, L0_xattn_b_qv, L0_ffn_ln_g, L0_ffn_ln_b, L0_ffn_Wq, L0_ffn_Wk, L0_ffn_Wv, L0_ffn_q_scale, L0_ffn_k_scale, L0_ffn_Wo, L0_ffn_gate_w, L0_ffn_gate_b, L0_ffn_w1, L0_ffn_b1, L0_ffn_w2, L0_ffn_b2):
    import jax
    import jax.numpy as jnp

    def _L0_xattn_ref(encoder_hc, decoder_hq, w_sim, b_sim, W_qv, b_qv):
        import jax, jax.numpy as jnp
        import numpy as np
        B, L_ENC, L_DEC, D = (16, 128, 128, 256)
        d = encoder_hc.shape[-1]
        w1, w2, w3 = (w_sim[:d], w_sim[d:2 * d], w_sim[2 * d:])
        Sim = (encoder_hc @ w1)[:, :, None] + (decoder_hq @ w2)[:, None, :] + jnp.einsum('bid,bjd->bij', encoder_hc * w3, decoder_hq) + b_sim[0]
        A = jax.nn.softmax(Sim, axis=2)
        hq_hat = jnp.einsum('bij,bjd->bid', A, decoder_hq)
        Batt = jax.nn.softmax(jnp.max(Sim, axis=2), axis=1)
        hc_bar = jnp.einsum('bi,bid->bd', Batt, encoder_hc)[:, None, :]
        hc_hat = jnp.broadcast_to(hc_bar, encoder_hc.shape)
        feats = jnp.concatenate([encoder_hc, hq_hat, encoder_hc * hq_hat, encoder_hc * hc_hat], axis=-1)
        hcq = feats @ W_qv + b_qv
        return hcq

    def _L0_ffn_ref(x, ln_g, ln_b, Wq, Wk, Wv, q_scale, k_scale, Wo, gate_w, gate_b, w1, b1, w2, b2):
        import jax, jax.numpy as jnp
        import numpy as np
        QK_SCALE = 10.0
        NEG_INF = -1000000000.0

        def layernorm(x, g, b, eps=1e-05):
            mu = jnp.mean(x, axis=-1, keepdims=True)
            var = jnp.var(x, axis=-1, keepdims=True)
            return (x - mu) * jax.lax.rsqrt(var + eps) * g + b

        def l2norm(x, eps=1e-12):
            return x / jnp.sqrt(jnp.sum(x * x, axis=-1, keepdims=True) + eps)
        B, S, D = x.shape
        H = q_scale.shape[0]
        DH = q_scale.shape[-1]
        h = layernorm(x, ln_g, ln_b)
        q = (h @ Wq).reshape(B, S, H, DH).transpose(0, 2, 1, 3)
        k = (h @ Wk).reshape(B, S, H, DH).transpose(0, 2, 1, 3)
        v = (h @ Wv).reshape(B, S, H, DH).transpose(0, 2, 1, 3)
        q = l2norm(q) * q_scale
        k = l2norm(k) * k_scale
        logits = jnp.einsum('bhid,bhjd->bhij', q, k) * QK_SCALE
        causal = jnp.tril(jnp.ones((S, S), bool))
        logits = jnp.where(causal, logits, NEG_INF)
        attn = jax.nn.softmax(logits, axis=-1)
        out = jnp.einsum('bhij,bhjd->bhid', attn, v)
        out = out.transpose(0, 2, 1, 3).reshape(B, S, H * DH) @ Wo
        h = layernorm(out, ln_g, ln_b)
        gate = jax.nn.softmax(h @ gate_w + gate_b, axis=-1)
        hid = jax.nn.gelu(jnp.einsum('bsd,edf->bsef', h, w1) + b1)
        exp_out = jnp.einsum('bsef,efd->bsed', hid, w2) + b2
        moe = jnp.einsum('bse,bsed->bsd', gate, exp_out)
        return layernorm(moe, ln_g, ln_b)
    x = x + _L0_xattn_ref(_layernorm(x, axis=-1), ctx_1024, L0_xattn_w_sim, L0_xattn_b_sim, L0_xattn_W_qv, L0_xattn_b_qv)
    x = x + _L0_ffn_ref(_layernorm(x, axis=-1), L0_ffn_ln_g, L0_ffn_ln_b, L0_ffn_Wq, L0_ffn_Wk, L0_ffn_Wv, L0_ffn_q_scale, L0_ffn_k_scale, L0_ffn_Wo, L0_ffn_gate_w, L0_ffn_gate_b, L0_ffn_w1, L0_ffn_b1, L0_ffn_w2, L0_ffn_b2)
    return x

_drawn_inputs = setup_inputs


def setup_inputs(seed=0):
    import zlib

    import numpy as np

    out = dict(_drawn_inputs(seed))
    spreads = {'L0_ffn_ln_g': (1.0, 0.2),
     'L0_ffn_ln_b': (0.0, 0.1),
     'L0_ffn_q_scale': (1.0, 0.2),
     'L0_ffn_k_scale': (1.0, 0.2),
     'L0_ffn_gate_b': (0.0, 0.1),
     'L0_ffn_b1': (0.0, 0.1),
     'L0_ffn_b2': (0.0, 0.1)}
    factors = {}
    for name, (base, spread) in spreads.items():
        noise = np.random.default_rng([zlib.crc32(name.encode()), seed]).standard_normal(out[name].shape)
        drawn = base * np.exp(spread * noise) if base else spread * noise
        out[name] = jnp.asarray(drawn.astype(out[name].dtype))
    for name, factor in factors.items():
        out[name] = (out[name] * factor).astype(out[name].dtype)
    return out
```

```python
from contextlib import ExitStack

import concourse.bass as bass
from concourse import mybir

f32 = mybir.dt.float32
f32r = mybir.dt.float32r
bf16 = mybir.dt.bfloat16
ALU = mybir.AluOpType
ACT = mybir.ActivationFunctionType
AX = mybir.AxisListType

P = 128
CHUNKS, ROWS, D = 8, 512, 256
TT = ROWS // P
KT = D // P
HEADS, DH = 16, 64
PAIRS = HEADS // 2
E, FF = 8, 1024
EPS = 1e-5
QK_SCALE = 10.0
MASKED = -1e30

COL_WSIM, COL_G, COL_B, COL_QS, COL_KS, COL_B1 = 0, 6, 8, 10, 18, 26
N_COLS = COL_B1 + E * FF // P


def setup_phase(nc, T, w_sim, ln_g, ln_b, q_scale, k_scale, gate_w, gate_b, b1):
    ident, ones, neg_half, columns = T["ident"], T["ones"], T["neg_half"], T["columns"]
    ctx = ExitStack()
    with ctx:
        rows = ctx.enter_context(nc.sbuf_tensor("param_rows", [N_COLS, P], f32))
        cols_ps = ctx.enter_context(nc.psum_tensor("psum_columns", [P, 512], f32))
        sem = lambda name: ctx.enter_context(nc.semaphore(name))
        rows_loaded, gate_loaded = sem("rows_loaded"), sem("gate_loaded")
        ident_zero, ident_done, consts_done = sem("ident_zero"), sem("ident_done"), sem("consts_done")
        cols_ready, cols_done = sem("cols_ready"), sem("cols_done")
        block = ctx.enter_context(nc.Block())

        @block.sync
        def _(sp):
            for at, src, n in ((COL_WSIM, w_sim, 6), (COL_G, ln_g, 2), (COL_B, ln_b, 2)):
                sp.dma_start(rows[at:at + n, :], src.rearrange("(r p) -> r p", p=P)).then_inc(rows_loaded, 16)
            for at, src in ((COL_QS, q_scale), (COL_KS, k_scale)):
                sp.dma_start(rows[at:at + PAIRS, :], src.rearrange("(r h) a d -> r (h a d)", h=2)).then_inc(rows_loaded, 16)
            sp.dma_start(rows[COL_B1:N_COLS, :], b1.rearrange("e (f p) -> (e f) p", p=P)).then_inc(rows_loaded, 16)

        @block.gpsimd
        def _(pool):
            nc.gpsimd.memset(ident[:, :], 0.0).then_inc(ident_zero, 1)
            nc.gpsimd.memset(ones[:, :], 1.0).then_inc(consts_done, 1)
            nc.gpsimd.memset(neg_half[:, :], -0.5).then_inc(consts_done, 1)
            nc.gpsimd.memset(T["mask"][:, :], 0.0).then_inc(ident_zero, 1)
            pool.wait_ge(ident_zero, 2)
            nc.gpsimd.affine_select(out=T["mask"][:, :], in_=T["mask"][:, :], compare_op=ALU.is_ge, fill=MASKED,
                                    base=0, pattern=[[-1, P]], channel_multiplier=1).then_inc(ident_done, 1)
            nc.gpsimd.affine_select(out=ident[:, :], in_=ident[:, :], compare_op=ALU.not_equal, fill=1.0,
                                    base=0, pattern=[[-1, P]], channel_multiplier=1).then_inc(ident_done, 1)

        @block.scalar
        def _(act):
            act.dma_start(T["gate_w"][:, :, :], gate_w.rearrange("(k p) e -> p k e", p=P)).then_inc(gate_loaded, 16)
            act.dma_start(T["gate_b"][:, :], gate_b.unsqueeze(0)).then_inc(gate_loaded, 16)
            act.wait_ge(gate_loaded, 32)

        @block.tensor
        def _(pe):
            pe.wait_ge(rows_loaded, 96)
            pe.wait_ge(ident_done, 2)
            nc.tensor.transpose(cols_ps[:, 0:N_COLS], rows[:, :], ident[0:N_COLS, 0:N_COLS]).then_inc(cols_ready, 1)

        @block.vector
        def _(dve):
            dve.wait_ge(cols_ready, 1)
            nc.vector.tensor_copy(columns[:, :], cols_ps[:, 0:N_COLS]).then_inc(cols_done, 1)
            dve.wait_ge(cols_done, 1)
            nc.vector.scalar_tensor_tensor(out=T["qk_scale"][:, :], in0=columns[:, COL_QS:COL_QS + PAIRS],
                                           scalar=QK_SCALE, in1=columns[:, COL_KS:COL_KS + PAIRS],
                                           op0=ALU.mult, op1=ALU.mult).then_inc(cols_done, 1)
            dve.wait_ge(ident_done, 2)
            nc.vector.tensor_copy(T["ident_b"][:, :], ident[:, :]).then_inc(cols_done, 1)
            dve.wait_ge(consts_done, 2)


def cross_attention_phase(nc, T, x, context, W_qv, b_qv, b_sim, Wq, Wk, Wv, Wo, x1_dram):
    ident, ones, neg_half, columns = T["ident"], T["ones"], T["neg_half"], T["columns"]
    hT_all, self_raw = T["hT_all"], T["self_raw"]

    ctx = ExitStack()
    with ctx:
        sb = lambda name, shape, dt=f32: ctx.enter_context(nc.sbuf_tensor(name, shape, dt))
        pair = lambda name, shape: (sb(name + "_hi", shape, f32r), sb(name + "_lo", shape, f32r))
        sem = lambda name: ctx.enter_context(nc.semaphore(name))

        xb = [sb(f"x_biased{i}", [P, TT, D]) for i in range(2)]
        encT = [sb(f"encT{i}", [P, KT, ROWS]) for i in range(2)]
        enc_s = [pair(f"encT_s{i}", [P, KT, ROWS]) for i in range(2)]
        xr = sb("x_raw", [P, TT, D])
        enc = sb("enc", [P, TT, D])
        cx = sb("cx", [P, TT, D])
        cx_s = pair("cx_s", [P, TT, D])
        cxT_s = pair("cxT_s", [P, KT, ROWS])
        ep = sb("ep", [P, KT, ROWS])
        ep_s = pair("ep_s", [P, KT, ROWS])
        prob = sb("prob", [P, TT, ROWS])
        probT_s = pair("probT_s", [P, TT, ROWS])
        hq_s = pair("hq_s", [P, KT, ROWS])
        prod = sb("prod", [P, KT, ROWS])
        prod_s = pair("prod_s", [P, KT, ROWS])
        w_enc = sb("w_enc", [P, KT, D])
        w_bar = sb("w_bar", [P, KT, D])
        w_mid_s = pair("w_mid_s", [P, 2 * KT, D])
        w_mix = sb("w_mix", [P, KT, D])
        w_mix_s = pair("w_mix_s", [P, KT, D])
        x1 = sb("x1_chunk", [P, TT, D])
        h = ep[:, :, :].rearrange("p k n -> p (k n)").rearrange("p (t d) -> p t d", d=D)
        bn = sb("bn", [P, TT, 6])
        mv = sb("mv", [P, TT, 2])
        veps = sb("veps", [P, TT])
        rstd = sb("rstd", [P, TT])
        bn1 = sb("bn1", [P, TT, 6])
        mv1 = sb("mv1", [P, TT, 2])
        veps1 = sb("veps1", [P, TT])
        rstd1 = sb("rstd1", [P, TT])
        rowmax = sb("rowmax", [P, TT])
        nrowmax = sb("nrowmax", [P, TT])
        rowsum = sb("rowsum", [P, TT])
        rinv = sb("rinv", [P, TT])
        mx = sb("mx", [P, TT])
        mcol = sb("mcol", [P, 1])
        gmax = sb("gmax", [1, 1])
        ngmax = sb("ngmax", [P, 1])
        bexp = sb("bexp", [P, TT])
        binv = sb("binv", [P, 1])
        hc = sb("hc", [P, KT])
        bqv_rows = sb("bqv_rows", [P, D])
        bsim = sb("bsim", [P, 1])
        w_stage = prob[:, 0:2, :].rearrange("p a b -> p (a b)").rearrange("p (k d) -> p k d", d=D)

        TR = ctx.enter_context(nc.psum_tensor("psum_transposed", [P, 2, 512], f32))
        S = ctx.enter_context(nc.psum_tensor("psum_scores", [P, 2, 512], f32))
        HQ = ctx.enter_context(nc.psum_tensor("psum_hq", [P, 2, 512], f32))
        X = ctx.enter_context(nc.psum_tensor("psum_x1", [P, 2, 512], f32))
        BATT = S[:, 0, :]

        bias_loaded = sem("bias_loaded")
        cx_loaded, w_loaded, qkv_loaded = sem("cx_loaded"), sem("wqv_loaded"), sem("qkv_loaded")
        x_loaded = sem("x_loaded")
        wmid_hi, wmid_split = sem("wmid_hi"), sem("wmid_split")
        enc_stats, enc_mv, enc_var, enc_rstd, enc_done, xb_done = map(
            sem, ("enc_stats", "enc_mv", "enc_var", "enc_rstd", "enc_done", "xb_done"))
        encT_ready, encT_copied, ep_copied, enc_hi, enc_split, ep_hi, ep_split = map(
            sem, ("encT_ready", "encT_copied", "ep_copied", "enc_hi", "enc_split", "ep_hi", "ep_split"))
        cxT_ready, cxT_hi, cxT_split, cx_hi, cx_split = map(
            sem, ("cxT_ready", "cxT_hi", "cxT_split", "cx_hi", "cx_split"))
        hq_ready, hq_hi, hq_split, prod_done, prod_hi, prod_split = map(
            sem, ("hq_ready", "hq_hi", "hq_split", "prod_done", "prod_hi", "prod_split"))
        s_ready, max_done, nmax_done, exp_done, rinv_done, prob_done = map(
            sem, ("s_ready", "max_done", "nmax_done", "exp_done", "rinv_done", "prob_done"))
        pT_ready, pT_hi, pT_split = map(sem, ("pT_ready", "pT_hi", "pT_split"))
        r_ready, mx_done, mcol_done, mcolT_ready, gmax_done, gmax_spread, ngmax_done, bexp_done = map(
            sem, ("r_ready", "mx_done", "mcol_done", "mcolT_ready", "gmax_done", "gmax_spread", "ngmax_done", "bexp_done"))
        hc_ready, binv_done, hc_done, wmix_done, wmix_hi, wmix_split = map(
            sem, ("hc_ready", "binv_done", "hc_done", "wmix_done", "wmix_hi", "wmix_split"))
        x1_ready, x1_done, x1_stats, x1_mv, x1_var, x1_rstd, h_done, hT_ready, hT_done, x1_stored = map(
            sem, ("x1_ready", "x1_done", "x1_stats", "x1_mv", "x1_var", "x1_rstd", "h_done", "hT_ready", "hT_done", "x1_stored"))
        block = ctx.enter_context(nc.Block())

        def steps(engine, step):
            step(None, 0, 1, 1)
            with engine.Fori(0, (CHUNKS - 2) // 2) as i:
                for odd in range(2):
                    m = engine.snap(i * 2 + odd)
                    step(m, m + 1, m + 2, odd)
            step(CHUNKS - 2, CHUNKS - 1, None, 0)
            step(CHUNKS - 1, None, None, 1)

        @block.sync
        def _(sp):
            def load(q):
                sp.wait_ge(enc_done, q)
                sp.wait_ge(xb_done, q)
                sp.dma_start(xr[:, :, :], x[bass.ds(q, 1), :, :].rearrange("c (t p) d -> p (c t) d", p=P)).then_inc(x_loaded, 16)
                sp.wait_ge(cxT_ready, q * 2)
                sp.wait_ge(cx_split, q)
                sp.dma_start(cx[:, :, :], context[bass.ds(q, 1), :, :].rearrange("c (t p) d -> p (c t) d", p=P)).then_inc(cx_loaded, 16)

            with sp.Fori(0, CHUNKS) as q:
                load(q)

        @block.gpsimd
        def _(pool):
            def prepare(q):
                pool.wait_ge(enc_var, q + 1)
                nc.gpsimd.tensor_tensor(rstd[:, :], veps[:, :], neg_half[:, 0:TT], ALU.pow).then_inc(enc_rstd, 1)

            def with_bias(q, odd, first):
                pool.wait_ge(x_loaded, q * 16 + 16)
                if not first:
                    pool.wait_ge(x1_done, q * 4 - 4)
                nc.gpsimd.tensor_tensor(xb[odd][:, :, :], xr[:, :, :],
                                        bqv_rows[:, :].unsqueeze(1).to_broadcast([P, TT, D]), ALU.add).then_inc(xb_done, 1)

            def step(m, n, q, odd):
                if n is not None:
                    pool.wait_ge(cx_hi, n + 1)
                    nc.gpsimd.tensor_tensor(cx_s[1][:, :, :], cx[:, :, :], cx_s[0][:, :, :].bitcast(f32),
                                            ALU.subtract).then_inc(cx_split, 1)
                if m is not None:
                    for k in range(KT):
                        pool.wait_ge(prod_hi, m * 2 + (k + 1))
                        nc.gpsimd.tensor_tensor(prod_s[1][:, k, :], prod[:, k, :], prod_s[0][:, k, :].bitcast(f32),
                                                ALU.subtract).then_inc(prod_split, 1)
                if q is not None:
                    prepare(q)
                if m is not None:
                    pool.wait_ge(x1_var, m + 1)
                    nc.gpsimd.tensor_tensor(rstd1[:, :], veps1[:, :], neg_half[:, 0:TT], ALU.pow).then_inc(x1_rstd, 1)
                    pool.dma_start(x1_dram[bass.ds(m, 1), :, :, :].rearrange("c t p d -> p (c t) d"),
                                   x1[:, :, :]).then_inc(x1_stored, 16)
                if q is not None:
                    with_bias(q, odd, m is None)

            prepare(0)
            pool.wait_ge(bias_loaded, 32)
            with_bias(0, 0, True)
            steps(nc.gpsimd, step)
            pool.wait_ge(x1_stored, 16 * CHUNKS)

        @block.scalar
        def _(act):
            act.dma_start(w_enc[:, :, :], W_qv[0:D, :].rearrange("(k p) d -> p k d", p=P)).then_inc(w_loaded, 16)
            act.dma_start(w_bar[:, :, :], W_qv[3 * D:4 * D, :].rearrange("(k p) d -> p k d", p=P)).then_inc(w_loaded, 16)
            act.dma_start(w_stage, W_qv[D:3 * D, :].rearrange("(k p) d -> p k d", p=P)).then_inc(w_loaded, 16)
            act.wait_ge(w_loaded, 48)
            act.dma_start(bqv_rows[:, :], b_qv.unsqueeze(0).to_broadcast([P, D])).then_inc(bias_loaded, 16)
            act.dma_start(bsim[:, :], b_sim.unsqueeze(0).to_broadcast([P, 1])).then_inc(bias_loaded, 16)
            nc.scalar.activation(w_mid_s[0][:, :, :], w_stage, ACT.Copy).then_inc(wmid_hi, 1)
            for i, w in enumerate((Wq, Wk, Wv)):
                act.dma_start(self_raw[:, i * KT:(i + 1) * KT, :], w.rearrange("(k p) n -> p k n", p=P)).then_inc(qkv_loaded, 16)
            act.dma_start(self_raw[:, 3 * KT:, :].rearrange("p a b -> p (a b)").rearrange("p (k d) -> p k d", d=D),
                          Wo.rearrange("(k p) d -> p k d", p=P)).then_inc(qkv_loaded, 16)

            def step(m, n, q, odd):
                if n is not None:
                    for k in range(KT):
                        act.wait_ge(encT_ready, n * 2 + (k + 1))
                        act.wait_ge(x1_ready, n * 4 - 4 if m is not None else 0)
                        act.wait_ge(prod_done, n * 2 - 2 if m is not None else 0)
                        nc.scalar.activation(encT[1 - odd][:, k, :], TR[:, k, :], ACT.Copy).then_inc(encT_copied, 1)
                        act.wait_ge(ep_split, n * 2)
                        act.wait_ge(hT_ready, n * 2 - 2 if m is not None else 0)
                        nc.scalar.activation(ep[:, k, :], TR[:, k, :], ACT.Identity,
                                             scale=columns[:, COL_WSIM + 4 + k:COL_WSIM + 5 + k],
                                             bias=columns[:, COL_WSIM + 2 + k:COL_WSIM + 3 + k]).then_inc(ep_copied, 1)
                    for k in range(KT):
                        act.wait_ge(cxT_ready, n * 2 + (k + 1))
                        act.wait_ge(s_ready, n * 4)
                        nc.scalar.activation(cxT_s[0][:, k, :], TR[:, k, :], ACT.Copy).then_inc(cxT_hi, 1)
                def context_hi():
                    act.wait_ge(cx_loaded, n * 16 + 16)
                    act.wait_ge(hq_ready, n * 2)
                    nc.scalar.activation(cx_s[0][:, :, :], cx[:, :, :], ACT.Copy).then_inc(cx_hi, 1)

                if m is not None:
                    for k in range(KT):
                        act.wait_ge(hq_ready, m * 2 + (k + 1))
                        act.wait_ge(x1_ready, m * 4)
                        nc.scalar.activation(hq_s[0][:, k, :], HQ[:, k, :], ACT.Copy).then_inc(hq_hi, 1)
                        act.wait_ge(prod_done, m * 2 + (k + 1))
                        nc.scalar.activation(prod_s[0][:, k, :], prod[:, k, :], ACT.Copy).then_inc(prod_hi, 1)
                if n is not None:
                    context_hi()
                    for t in range(TT):
                        act.wait_ge(nmax_done, n * 4 + (t + 1))
                        act.wait_ge(pT_ready, n * 4)
                        nc.scalar.activation(prob[:, t, :], S[:, t % 2, :], ACT.Exp, bias=nrowmax[:, t:t + 1],
                                             accum_out=rowsum[:, t:t + 1]).then_inc(exp_done, 1)
                    act.wait_ge(ngmax_done, n + 1)
                    act.wait_ge(hc_ready, n)
                    nc.scalar.activation(bexp[:, :], mx[:, :], ACT.Exp, bias=ngmax[:, 0:1]).then_inc(bexp_done, 1)
                    act.wait_ge(wmix_done, n + 1)
                    act.wait_ge(x1_ready, n * 4)
                    nc.scalar.activation(w_mix_s[0][:, :, :], w_mix[:, :, :], ACT.Copy).then_inc(wmix_hi, 1)
                    for t in range(TT):
                        act.wait_ge(pT_ready, n * 4 + (t + 1))
                        act.wait_ge(hq_ready, n * 2)
                        nc.scalar.activation(probT_s[0][:, :, t * P:(t + 1) * P],
                                             TR[:, t % 2, :].rearrange("p (j i) -> p j i", i=P), ACT.Copy).then_inc(pT_hi, 1)
                if m is not None:
                    for k in range(KT):
                        act.wait_ge(hT_ready, m * 2 + (k + 1))
                        nc.scalar.activation(hT_all[:, bass.ds(m, 1), k, :], TR[:, k, :].unsqueeze(1), ACT.Identity,
                                             scale=columns[:, COL_G + k:COL_G + k + 1],
                                             bias=columns[:, COL_B + k:COL_B + k + 1]).then_inc(hT_done, 1)

            steps(nc.scalar, step)
            act.wait_ge(qkv_loaded, 64)

        @block.vector
        def _(dve):
            def stats(q):
                dve.wait_ge(x_loaded, q * 16 + 16)
                for t in range(TT):
                    ins = nc.vector.bn_stats(bn[:, t, :], xr[:, t, :])
                ins.then_inc(enc_stats, 1)
                dve.wait_ge(enc_stats, q + 1)

            def variance(q):
                for t in range(TT):
                    ins = nc.vector.bn_aggr(mv[:, t, :], bn[:, t, :])
                ins.then_inc(enc_mv, 1)
                dve.wait_ge(enc_mv, q + 1)
                dve.wait_ge(enc_rstd, q)
                nc.vector.tensor_scalar_add(veps[:, :], mv[:, :, 1], EPS).then_inc(enc_var, 1)

            def normalise(q):
                dve.wait_ge(enc_rstd, q + 1)
                dve.wait_ge(hc_ready, q)
                dve.wait_ge(encT_ready, q * 2)
                for t in range(TT):
                    ins = nc.vector.tensor_scalar(enc[:, t, :], xr[:, t, :], mv[:, t, 0:1], rstd[:, t:t + 1],
                                                  ALU.subtract, ALU.mult)
                ins.then_inc(enc_done, 1)

            def x1_tile(m, t, odd):
                dve.wait_ge(x1_ready, m * 4 + (t + 1))
                if t == 0:
                    dve.wait_ge(xb_done, m + 1)
                    dve.wait_ge(x1_stored, m * 16)
                    dve.wait_ge(h_done, m)
                nc.vector.tensor_tensor(x1[:, t, :], X[:, t % 2, 0:D], xb[odd][:, t, :], ALU.add).then_inc(x1_done, 1)

            def step(m, n, q, odd):
                even = 1 - odd
                if n is not None:
                    for k in range(KT):
                        dve.wait_ge(ep_copied, n * 2 + (k + 1))
                        dve.wait_ge(s_ready, n * 4)
                        nc.vector.tensor_copy(ep_s[0][:, k, :], ep[:, k, :]).then_inc(ep_hi, 1)
                        nc.vector.tensor_copy(enc_s[even][0][:, k, :], encT[even][:, k, :]).then_inc(enc_hi, 1)
                        dve.wait_ge(ep_hi, n * 2 + (k + 1))
                        nc.vector.tensor_tensor(ep_s[1][:, k, :], ep[:, k, :], ep_s[0][:, k, :].bitcast(f32),
                                                ALU.subtract).then_inc(ep_split, 1)
                        dve.wait_ge(enc_hi, n * 2 + (k + 1))
                        nc.vector.tensor_tensor(enc_s[even][1][:, k, :], encT[even][:, k, :], enc_s[even][0][:, k, :].bitcast(f32),
                                                ALU.subtract).then_inc(enc_split, 1)
                    for k in range(KT):
                        dve.wait_ge(cxT_hi, n * 2 + (k + 1))
                        nc.vector.tensor_tensor(cxT_s[1][:, k, :], TR[:, k, :], cxT_s[0][:, k, :].bitcast(f32),
                                                ALU.subtract).then_inc(cxT_split, 1)
                if m is not None:
                    for k in range(KT):
                        dve.wait_ge(prod_split, m * 2)
                        dve.wait_ge(hq_hi, m * 2 + (k + 1))
                        nc.vector.tensor_tensor(prod[:, k, :], HQ[:, k, :], encT[odd][:, k, :], ALU.mult).then_inc(prod_done, 1)
                        nc.vector.tensor_tensor(hq_s[1][:, k, :], HQ[:, k, :], hq_s[0][:, k, :].bitcast(f32),
                                                ALU.subtract).then_inc(hq_split, 1)
                if n is not None:
                    for t in range(TT + 1):
                        if t < TT:
                            dve.wait_ge(s_ready, n * 4 + (t + 1))
                            nc.vector.reduce_max(rowmax[:, t:t + 1], S[:, t % 2, :], AX.X).then_inc(max_done, 1)
                            dve.wait_ge(max_done, n * 4 + (t + 1))
                            nc.vector.tensor_scalar(nrowmax[:, t:t + 1], rowmax[:, t:t + 1], -1.0, None, ALU.mult).then_inc(nmax_done, 1)
                        if t:
                            u = t - 1
                            dve.wait_ge(exp_done, n * 4 + (u + 1))
                            nc.vector.reciprocal(rinv[:, u:u + 1], rowsum[:, u:u + 1]).then_inc(rinv_done, 1)
                            dve.wait_ge(rinv_done, n * 4 + (u + 1))
                            nc.vector.tensor_scalar(prob[:, u, :], prob[:, u, :], rinv[:, u:u + 1], None, ALU.mult).then_inc(prob_done, 1)
                if q is not None:
                    stats(q)
                if m is not None:
                    x1_tile(m, 0, odd)
                if q is not None:
                    variance(q)
                if n is not None:
                    dve.wait_ge(r_ready, n + 1)
                    dve.wait_ge(bexp_done, n)
                    nc.vector.scalar_tensor_tensor(out=mx[:, :], in0=BATT[:, 0:TT], scalar=bsim[:, 0:1], in1=rowmax[:, :],
                                                   op0=ALU.add, op1=ALU.add).then_inc(mx_done, 1)
                    dve.wait_ge(mx_done, n + 1)
                    nc.vector.reduce_max(mcol[:, :], mx[:, :], AX.X).then_inc(mcol_done, 1)
                if m is not None:
                    x1_tile(m, 1, odd)
                if n is not None:
                    dve.wait_ge(mcolT_ready, n + 1)
                    nc.vector.reduce_max(gmax[:, :], BATT[0:1, 8:8 + P], AX.X).then_inc(gmax_done, 1)
                if m is not None:
                    x1_tile(m, 2, odd)
                if n is not None:
                    dve.wait_ge(gmax_spread, n + 1)
                    nc.vector.tensor_scalar(ngmax[:, :], BATT[:, 144:145], -1.0, None, ALU.mult).then_inc(ngmax_done, 1)
                if m is not None:
                    x1_tile(m, 3, odd)
                    dve.wait_ge(x1_done, m * 4 + 4)
                    for t in range(TT):
                        ins = nc.vector.bn_stats(bn1[:, t, :], x1[:, t, :])
                    ins.then_inc(x1_stats, 1)
                    dve.wait_ge(x1_stats, m + 1)
                if n is not None:
                    dve.wait_ge(hc_ready, n + 1)
                    nc.vector.reciprocal(binv[:, :], BATT[:, 152:153]).then_inc(binv_done, 1)
                if m is not None:
                    for t in range(TT):
                        ins = nc.vector.bn_aggr(mv1[:, t, :], bn1[:, t, :])
                    ins.then_inc(x1_mv, 1)
                    dve.wait_ge(x1_mv, m + 1)
                    nc.vector.tensor_scalar(veps1[:, :], mv1[:, :, 1], 1.0 + EPS, EPS * EPS, ALU.mult, ALU.add).then_inc(x1_var, 1)
                if n is not None:
                    dve.wait_ge(binv_done, n + 1)
                    nc.vector.tensor_scalar(hc[:, :], BATT[:, 148:150], binv[:, 0:1], None, ALU.mult).then_inc(hc_done, 1)
                    dve.wait_ge(hc_done, n + 1)
                    dve.wait_ge(w_loaded, 48)
                    dve.wait_ge(wmix_split, n)
                    for k in range(KT):
                        ins = nc.vector.scalar_tensor_tensor(out=w_mix[:, k, :], in0=w_bar[:, k, :], scalar=hc[:, k:k + 1],
                                                             in1=w_enc[:, k, :], op0=ALU.mult, op1=ALU.add)
                    ins.then_inc(wmix_done, 1)
                    dve.wait_ge(wmix_hi, n + 1)
                    nc.vector.tensor_tensor(w_mix_s[1][:, :, :], w_mix[:, :, :], w_mix_s[0][:, :, :].bitcast(f32),
                                            ALU.subtract).then_inc(wmix_split, 1)
                    for t in range(TT):
                        dve.wait_ge(pT_hi, n * 4 + (t + 1))
                        here = slice(t * P, (t + 1) * P)
                        nc.vector.tensor_tensor(probT_s[1][:, :, here], TR[:, t % 2, :].rearrange("p (j i) -> p j i", i=P),
                                                probT_s[0][:, :, here].bitcast(f32), ALU.subtract).then_inc(pT_split, 1)
                if m is not None:
                    dve.wait_ge(x1_rstd, m + 1)
                    dve.wait_ge(hT_ready, m * 2)
                    for t in range(TT):
                        ins = nc.vector.tensor_scalar(h[:, t, :], x1[:, t, :], mv1[:, t, 0:1], rstd1[:, t:t + 1],
                                                      ALU.subtract, ALU.mult)
                    ins.then_inc(h_done, 1)
                if q is not None:
                    normalise(q)

            dve.wait_ge(bias_loaded, 32)
            stats(0)
            variance(0)
            dve.wait_ge(wmid_hi, 1)
            nc.vector.tensor_tensor(w_mid_s[1][:, :, :], w_stage, w_mid_s[0][:, :, :].bitcast(f32),
                                    ALU.subtract).then_inc(wmid_split, 1)
            normalise(0)
            steps(nc.vector, step)

        @block.tensor
        def _(pe):
            THREE = ((0, 0), (1, 0), (0, 1))

            def transposes(bank, sources):
                for i, src in enumerate(sources):
                    ins = nc.tensor.transpose(TR[:, bank, i * P:(i + 1) * P], src, ident[:, :])
                return ins

            def products(out, ks, lhs, rhs):
                steps = [(a, b, k) for a, b in THREE for k in ks]
                for i, (a, b, k) in enumerate(steps):
                    ins = nc.tensor.matmul(out, lhs(a, k), rhs(b, k), start=i == 0, stop=i == len(steps) - 1)
                return ins

            def features(m, t, odd):
                pe.wait_ge(x1_done, m * 4 + max(t - 1, 0))
                here = slice(t * P, (t + 1) * P)
                groups = ([(enc_s[odd], k, w_mix_s, k) for k in range(KT)] + [(hq_s, k, w_mid_s, k) for k in range(KT)]
                          + [(prod_s, k, w_mid_s, KT + k) for k in range(KT)])
                products(X[:, t % 2, 0:D], range(3 * KT),
                         lambda a, i: groups[i][0][a][:, groups[i][1], here],
                         lambda b, i: groups[i][2][b][:, groups[i][3], :]).then_inc(x1_ready, 1)

            def step(m, n, q, odd):
                even = 1 - odd
                if n is not None:
                    pe.wait_ge(enc_done, n + 1)
                    pe.wait_ge(hT_done, n * 2 - 2 if m is not None else 0)
                    pe.wait_ge(pT_split, n * 4)
                    for k in range(KT):
                        transposes(k, [enc[:, t, k * P:(k + 1) * P] for t in range(TT)]).then_inc(encT_ready, 1)
                    pe.wait_ge(cx_loaded, n * 16 + 16)
                    for k in range(KT):
                        pe.wait_ge(encT_copied, n * 2 + (k + 1))
                        pe.wait_ge(ep_copied, n * 2 + (k + 1))
                        transposes(k, [cx[:, t, k * P:(k + 1) * P] for t in range(TT)]).then_inc(cxT_ready, 1)
                if m is not None:
                    pe.wait_ge(cx_split, m + 1)
                    pe.wait_ge(pT_split, m * 4 + 4)
                    pe.wait_ge(hq_split, m * 2)
                    for k in range(KT):
                        cols = slice(k * P, (k + 1) * P)
                        products(HQ[:, k, :], range(TT), lambda a, j: cx_s[a][:, j, cols],
                                 lambda b, j: probT_s[b][:, j, :]).then_inc(hq_ready, 1)
                if n is not None:
                    pe.wait_ge(ep_split, n * 2 + 2)
                    pe.wait_ge(cxT_split, n * 2 + 2)
                    pe.wait_ge(hc_done, n)
                    for t in range(TT):
                        if t < 2:
                            pe.wait_ge(exp_done, n * 4)
                        else:
                            pe.wait_ge(exp_done, n * 4 + (t - 1))
                        here = slice(t * P, (t + 1) * P)
                        products(S[:, t % 2, :], range(KT), lambda a, k: ep_s[a][:, k, here],
                                 lambda b, k: cxT_s[b][:, k, :]).then_inc(s_ready, 1)
                if m is not None:
                    pe.wait_ge(enc_split, m * 2 + 2)
                    pe.wait_ge(hq_split, m * 2 + 2)
                    pe.wait_ge(prod_split, m * 2 + 2)
                    pe.wait_ge(wmix_split, m + 1)
                    pe.wait_ge(wmid_split, 1)
                    features(m, 0, odd)
                if n is not None:
                    pe.wait_ge(exp_done, n * 4 + 3)
                    for t in range(TT):
                        for k in range(KT):
                            ins = nc.tensor.matmul(BATT[:, t:t + 1], encT[even][:, k, t * P:(t + 1) * P],
                                                   columns[:, COL_WSIM + k:COL_WSIM + k + 1], start=k == 0, stop=k == KT - 1)
                    ins.then_inc(r_ready, 1)
                if m is not None:
                    features(m, 1, odd)
                if n is not None:
                    pe.wait_ge(mcol_done, n + 1)
                    nc.tensor.transpose(BATT[0:1, 8:8 + P], mcol[:, :], ident[:, :]).then_inc(mcolT_ready, 1)
                if m is not None:
                    features(m, 2, odd)
                if n is not None:
                    pe.wait_ge(gmax_done, n + 1)
                    nc.tensor.matmul(BATT[:, 144:145], ones[0:1, :], gmax[:, :], start=True, stop=True).then_inc(gmax_spread, 1)
                if m is not None:
                    features(m, 3, odd)
                if n is not None:
                    pe.wait_ge(bexp_done, n + 1)
                    for k in range(KT):
                        for t in range(TT):
                            nc.tensor.matmul(BATT[:, 148 + k:149 + k], enc[:, t, k * P:(k + 1) * P], bexp[:, t:t + 1],
                                             start=t == 0, stop=t == TT - 1)
                    for t in range(TT):
                        ins = nc.tensor.matmul(BATT[:, 152:153], ones[:, :], bexp[:, t:t + 1], start=t == 0, stop=t == TT - 1)
                    ins.then_inc(hc_ready, 1)
                    for t in range(TT):
                        pe.wait_ge(prob_done, n * 4 + (t + 1))
                        if t >= 2:
                            pe.wait_ge(pT_split, n * 4 + (t - 1))
                        else:
                            pe.wait_ge(cxT_split, n * 2 + (t + 1))
                        transposes(t % 2, [prob[:, t, j * P:(j + 1) * P] for j in range(TT)]).then_inc(pT_ready, 1)
                if m is not None:
                    pe.wait_ge(h_done, m + 1)
                    pe.wait_ge(pT_split, m * 4 + 8 if n is not None else m * 4 + 4)
                    for k in range(KT):
                        transposes(k, [h[:, t, k * P:(k + 1) * P] for t in range(TT)]).then_inc(hT_ready, 1)

            steps(nc.tensor, step)



def self_attention_phase(nc, T):
    ident, ident_b, mask, ones = T["ident"], T["ident_b"], T["mask"], T["ones"]
    neg_half, columns, qk_scale = T["neg_half"], T["columns"], T["qk_scale"]
    hT_all, gate_all, self_raw = T["hT_all"], T["gate_all"], T["self_raw"]
    PC = 2 * DH
    U = 2 * TT
    BLOCKS = 13
    GROUPS = 4
    order = [(hh, t) for hh in range(2) for t in reversed(range(TT))]

    ctx = ExitStack()
    with ctx:
        sb = lambda name, shape, dt=f32: ctx.enter_context(nc.sbuf_tensor(name, shape, dt))
        split = lambda name, shape: (sb(name + "_hi", shape, f32r), sb(name + "_lo", shape, f32r))
        sem = lambda name: ctx.enter_context(nc.semaphore(name))
        attnT_s = split("attnT_s", [P, PAIRS, ROWS])
        wqkv_s = split("wqkv_s", [P, KT, PAIRS, 3, PC])
        wo_s = split("wo_s", [P, PAIRS, D])
        h_s = split("hT_s", [P, KT, ROWS])
        qT_s = [split(f"qT_s{i}", [P, ROWS]) for i in range(2)]
        kT_s = [split(f"kT_s{i}", [P, ROWS]) for i in range(2)]
        v_s = [split(f"v_s{i}", [P, TT, PC]) for i in range(2)]
        qk = sb("qk", [P, TT, 2, PC])
        qk_sq = sb("qk_sq", [P, TT, 2, PC])
        prob = sb("prob_b", [P, 2, ROWS])
        projected = prob[:, :, :].rearrange("p a b -> p (a b)").rearrange("p (t d) -> p t d", d=D)
        hT_now = prob
        probT_s = [split(f"pT_s{i}", [P, BLOCKS, P]) for i in range(2)]
        ssq = sb("ssq", [P, TT, 2, 2])
        k_rnorm = sb("k_rnorm", [P, TT, 2])
        q_rnorm = [sb(f"q_rnorm{i}", [P, TT, 2]) for i in range(2)]
        q_neg = [sb(f"q_neg{i}", [P, TT, 2]) for i in range(2)]
        rowmax, nrowmax, rowsum, rinv = (sb(n, [P, U]) for n in ("rowmax_b", "nrowmax_b", "rowsum_b", "rinv_b"))
        bn, mv = sb("bn_b", [P, TT, 6]), sb("mv_b", [P, TT, 2])
        veps, rstd = sb("veps_b", [P, TT]), sb("rstd_b", [P, TT])
        g_max, g_sum, g_inv = (sb(n, [P, TT]) for n in ("g_max", "g_sum", "g_inv"))
        g_exp = sb("g_exp", [P, TT, E])

        A = ctx.enter_context(nc.psum_tensor("psum_project", [P, 3, 512], f32))
        S = ctx.enter_context(nc.psum_tensor("psum_logits", [P, 2, 512], f32))
        PT = ctx.enter_context(nc.psum_tensor("psum_probT", [P, 2, 512], f32))
        O = ctx.enter_context(nc.psum_tensor("psum_attn", [P, 512], f32))

        (w_hi, w_split, wo_hi, wo_split, h_hi, h_split) = map(
            sem, ("sw_hi", "sw_split", "wo_hi", "wo_split", "bh_hi", "bh_split"))
        (proj_ready, qk_copied, v_hi, v_split, sq_done, ssq_sum, ssq_done, k_pow, q_pow, q_neg_done, k_done) = map(
            sem, ("proj_ready", "qk_copied", "v_hi", "v_split", "sq_done", "ssq_sum", "ssq_done", "k_pow", "q_pow",
                  "q_neg_done", "k_done"))
        (qT_ready, qT_hi, qT_split, kT_ready, kT_hi, kT_split) = map(
            sem, ("qT_ready", "qT_hi", "qT_split", "kT_ready", "kT_hi", "kT_split"))
        (s_ready, max_done, nmax_done, exp_done, rinv_done, prob_done, pT_ready, pT_hi, pT_split) = map(
            sem, ("bs_ready", "bmax_done", "bnmax_done", "bexp_done_b", "brinv_done", "bprob_done", "bpT_ready",
                  "bpT_hi", "bpT_split"))
        (o_ready, o_hi, o_split, wo_ready, wo_copied) = map(sem, ("o_ready", "o_hi", "o_split", "wo_ready", "wo_copied"))
        (n_stats, n_mv, n_var, n_rstd, n_done, n_ready, hT_done, hT_kept) = map(
            sem, ("n_stats", "n_mv", "n_var", "n_rstd", "n_done", "n_ready", "bhT_done", "hT_kept"))
        (g_ready, g_max_done, g_sub, g_exp_done, g_sum_done, g_inv_done, g_done) = map(
            sem, ("g_ready", "g_max_done", "g_sub", "g_exp_done", "g_sum_done", "g_inv_done", "g_done"))
        block = ctx.enter_context(nc.Block())

        def pairs(engine, begin, pair, finish):
            def chunk(c, last):
                g0 = engine.snap(c * PAIRS) if not last else c * PAIRS
                pair(c, g0, 0, 0, True, True)
                with engine.Fori(0, (PAIRS - 2) // 2) as i:
                    for step in (1, 2):
                        p = engine.snap(i * 2 + step)
                        pair(c, engine.snap(g0 + p), p, step % 2, False, True)
                pair(c, engine.snap(g0 + (PAIRS - 1)), PAIRS - 1, 1, False, False)
                finish(c, last)

            begin()
            with engine.Fori(0, CHUNKS - 1) as c:
                chunk(c, False)
            chunk(CHUNKS - 1, True)

        def done_before(g, u, start):
            return g * U + (max(u - 1, 0) if start else u - 1)

        @block.gpsimd
        def _(pool):
            def squares(g, t):
                pool.wait_ge(ssq_sum, g)
                pool.wait_ge(qk_copied, g * TT + (t + 1))
                nc.gpsimd.tensor_tensor(qk_sq[:, t, :, :], qk[:, t, :, :], qk[:, t, :, :], ALU.mult).then_inc(sq_done, 1)

            def powers_k(g):
                pool.wait_ge(ssq_done, g + 1)
                pool.wait_ge(k_done, g)
                nc.gpsimd.tensor_tensor(k_rnorm[:, :, :], ssq[:, :, 1, :],
                                        neg_half[:, 0:2 * TT].rearrange("p (t h) -> p t h", h=2), ALU.pow).then_inc(k_pow, 1)

            def powers_q(g, odd):
                if not (isinstance(g, int) and g < 2):
                    pool.wait_ge(exp_done, g * U - U)
                nc.gpsimd.tensor_tensor(q_rnorm[odd][:, :, :], ssq[:, :, 0, :],
                                        neg_half[:, 0:2 * TT].rearrange("p (t h) -> p t h", h=2), ALU.pow).then_inc(q_pow, 1)

            def begin():
                for t in range(TT):
                    squares(0, t)
                powers_k(0)
                powers_q(0, 0)

            def pair(c, g, p, odd, start, more):
                nxt = g + 1
                if more:
                    for t in range(TT):
                        squares(nxt, t)
                    powers_k(nxt)
                    powers_q(nxt, 1 - odd)

            def finish(c, last):
                if not last:
                    g = c * PAIRS + PAIRS
                    for t in range(TT):
                        squares(g, t)
                    powers_k(g)
                    powers_q(g, 0)
                pool.wait_ge(n_var, c + 1)
                nc.gpsimd.tensor_tensor(rstd[:, :], veps[:, :], neg_half[:, 0:TT], ALU.pow).then_inc(n_rstd, 1)

            pairs(nc.gpsimd, begin, pair, finish)

        @block.scalar
        def _(act):
            def split_h(c):
                act.wait_ge(proj_ready, c * (PAIRS * TT))
                nc.scalar.activation(h_s[0][:, :, :], hT_all[:, bass.ds(c, 1), :, :].rearrange("p c k n -> p (c k) n"),
                                     ACT.Copy).then_inc(h_hi, 1)

            def from_projection(g, t, odd):
                bank = t % 3
                act.wait_ge(proj_ready, g * TT + (t + 1))
                act.wait_ge(qT_ready, g)
                act.wait_ge(kT_ready, g)
                nc.scalar.activation(qk[:, t, :, :], A[:, bank, 0:2 * PC].rearrange("p (a n) -> p a n", a=2), ACT.Copy).then_inc(qk_copied, 1)
                if not (isinstance(g, int) and g == 0):
                    act.wait_ge(o_ready, g * 2 - 2)
                nc.scalar.activation(v_s[odd][0][:, t, :], A[:, bank, 2 * PC:3 * PC], ACT.Copy).then_inc(v_hi, 1)

            def q_high(g, p, odd):
                act.wait_ge(qT_ready, g + 1)
                if not (isinstance(g, int) and g == 0):
                    act.wait_ge(s_ready, g * U - U)
                nc.scalar.activation(qT_s[odd][0][:, :], A[:, 1, :], ACT.Copy, scale=qk_scale[:, bass.ds(p, 1)]).then_inc(qT_hi, 1)

            def k_high(g, odd):
                act.wait_ge(kT_ready, g + 1)
                nc.scalar.activation(kT_s[odd][0][:, :], A[:, 2, :], ACT.Copy).then_inc(kT_hi, 1)

            def exponentials(g, u, odd, start):
                hh, t = order[u]
                act.wait_ge(q_pow, g + 1)
                act.wait_ge(pT_ready, done_before(g, u, start))
                act.wait_ge(nmax_done, g * U + (u + 1))
                n = (t + 1) * P
                nc.scalar.activation(prob[:, u % 2, 0:n], S[:, u % 2, 0:n], ACT.Exp, bias=nrowmax[:, u:u + 1],
                                     scale=q_rnorm[odd][:, t, hh:hh + 1], accum_out=rowsum[:, u:u + 1]).then_inc(exp_done, 1)

            def probT_high(g, u, start):
                hh, t = order[u]
                act.wait_ge(o_ready, g * 2 if start else g * 2 + (hh - 1))
                act.wait_ge(pT_ready, g * U + (u + 1))
                nc.scalar.activation(probT_s[hh][0][:, t:4 * t + 1:3, :], PT[:, u % 2, 0:(t + 1) * P]
                                     .rearrange("p (j i) -> p j i", i=P), ACT.Copy).then_inc(pT_hi, 1)

            def attn_high(c, g, p, hh):
                act.wait_ge(o_ready, g * 2 + (hh + 1))
                act.wait_ge(wo_ready, c * TT)
                nc.scalar.activation(attnT_s[0][hh * DH:(hh + 1) * DH, bass.ds(p, 1), :], O[0:DH, :].unsqueeze(1),
                                     ACT.Copy).then_inc(o_hi, 1)

            def begin():
                for p in range(PAIRS):
                    for i in range(3):
                        ins = nc.scalar.activation(wqkv_s[0][:, :, p, i, :],
                                                   self_raw[:, i * KT:(i + 1) * KT, p * PC:(p + 1) * PC], ACT.Copy)
                    ins.then_inc(w_hi, 1)
                    if p == 0:
                        split_h(0)
                nc.scalar.activation(wo_s[0][:, :, :], wo_raw, ACT.Copy).then_inc(wo_hi, 1)
                for t in range(TT):
                    from_projection(0, t, 0)
                q_high(0, 0, 0)
                k_high(0, 0)
                exponentials(0, 0, 0, True)

            wo_raw = self_raw[:, 3 * KT:, :].rearrange("p a b -> p (a b)").rearrange("p (k d) -> p k d", d=D)

            def pair(c, g, p, odd, start, more):
                nxt, even = act.snap(g + 1), 1 - odd
                for u in range(U):
                    if u < U - 1:
                        exponentials(g, u + 1, odd, start)
                    if u == 0 and not start:
                        probT_high(act.snap(g - 1), U - 1, False)
                    if u:
                        probT_high(g, u - 1, start)
                    if more:
                        if u == 1:
                            from_projection(nxt, 0, even)
                            from_projection(nxt, 1, even)
                        if u == 2:
                            from_projection(nxt, 2, even)
                        if u == 3:
                            from_projection(nxt, 3, even)
                        if u == 5:
                            q_high(nxt, p + 1, even)
                    if u == 2 and not start:
                        attn_high(c, g - 1, p - 1, 1)
                    if u == 6:
                        attn_high(c, g, p, 0)
                if more:
                    k_high(nxt, even)
                    exponentials(nxt, 0, even, False)

            def finish(c, last):
                g7 = act.snap(c * PAIRS + (PAIRS - 1))
                nxt = act.snap(c * PAIRS + PAIRS)
                probT_high(g7, U - 1, False)
                if not last:
                    split_h(c + 1)
                    for t in range(3):
                        from_projection(nxt, t, 0)
                attn_high(c, g7, PAIRS - 1, 1)
                if not last:
                    from_projection(nxt, 3, 0)
                    q_high(nxt, 0, 0)
                for t in range(TT):
                    act.wait_ge(wo_ready, c * TT + (t + 1))
                    nc.scalar.activation(projected[:, t, :], S[:, t % 2, 0:D], ACT.Copy).then_inc(wo_copied, 1)
                if not last:
                    k_high(nxt, 0)
                act.wait_ge(n_ready, c * KT + KT)
                for k in range(KT):
                    nc.scalar.activation(hT_now[:, k, :], PT[:, k, :], ACT.Identity,
                                         scale=columns[:, COL_G + k:COL_G + k + 1],
                                         bias=columns[:, COL_B + k:COL_B + k + 1]).then_inc(hT_done, 1)
                act.wait_ge(g_sub, c + 1)
                nc.scalar.activation(g_exp[:, :, :], g_exp[:, :, :], ACT.Exp).then_inc(g_exp_done, 1)
                if not last:
                    act.wait_ge(g_ready, c + 1)
                    act.wait_ge(hT_kept, c + 1)
                    exponentials(nxt, 0, 0, True)

            pairs(nc.scalar, begin, pair, finish)

        @block.vector
        def _(dve):
            wo_raw = self_raw[:, 3 * KT:, :].rearrange("p a b -> p (a b)").rearrange("p (k d) -> p k d", d=D)

            def low(out, whole, high):
                return nc.vector.tensor_tensor(out, whole, high.bitcast(f32), ALU.subtract)

            def split_h(c):
                dve.wait_ge(h_hi, c + 1)
                low(h_s[1][:, :, :], hT_all[:, bass.ds(c, 1), :, :].rearrange("p c k n -> p (c k) n"), h_s[0][:, :, :]).then_inc(h_split, 1)

            def v_low(g, t, odd):
                dve.wait_ge(v_hi, g * TT + (t + 1))
                low(v_s[odd][1][:, t, :], A[:, t % 3, 2 * PC:3 * PC], v_s[odd][0][:, t, :]).then_inc(v_split, 1)

            def sum_squares(g):
                dve.wait_ge(k_pow, g)
                dve.wait_ge(q_pow, g)
                dve.wait_ge(sq_done, g * TT + TT)
                nc.vector.reduce_sum(ssq[:, :, :, :], qk_sq[:, :, :, :].rearrange("p t a (h d) -> p (t a h) d", d=DH), AX.X).then_inc(ssq_sum, 1)
                dve.wait_ge(ssq_sum, g + 1)
                nc.vector.tensor_scalar_add(ssq[:, :, :, :], ssq[:, :, :, :], 1e-12).then_inc(ssq_done, 1)

            def key_norms(g):
                dve.wait_ge(k_pow, g + 1)
                here = qk[:, :, 1, :].rearrange("p t (h d) -> p t h d", d=DH)
                nc.vector.tensor_tensor(here, here, k_rnorm[:, :, :].unsqueeze(3).to_broadcast([P, TT, 2, DH]), ALU.mult).then_inc(k_done, 1)

            def negate(g, odd):
                dve.wait_ge(q_pow, g + 1)
                nc.vector.tensor_scalar(q_neg[odd][:, :, :], q_rnorm[odd][:, :, :], -1.0, None, ALU.mult).then_inc(q_neg_done, 1)

            def q_low(g, p, odd):
                dve.wait_ge(qT_hi, g + 1)
                nc.vector.scalar_tensor_tensor(out=qT_s[odd][1][:, :], in0=A[:, 1, :], scalar=qk_scale[:, bass.ds(p, 1)],
                                               in1=qT_s[odd][0][:, :].bitcast(f32), op0=ALU.mult, op1=ALU.subtract).then_inc(qT_split, 1)

            def k_low(g, odd):
                dve.wait_ge(kT_hi, g + 1)
                low(kT_s[odd][1][:, :], A[:, 2, :], kT_s[odd][0][:, :]).then_inc(kT_split, 1)

            def maximum(g, u, odd):
                hh, t = order[u]
                dve.wait_ge(s_ready, g * U + (u + 1))
                nc.vector.reduce_max(rowmax[:, u:u + 1], S[:, u % 2, 0:(t + 1) * P], AX.X).then_inc(max_done, 1)
                dve.wait_ge(q_neg_done, g + 1)
                dve.wait_ge(max_done, g * U + (u + 1))
                nc.vector.tensor_tensor(nrowmax[:, u:u + 1], rowmax[:, u:u + 1], q_neg[odd][:, t, hh:hh + 1], ALU.mult).then_inc(nmax_done, 1)

            def normalise(g, u):
                dve.wait_ge(exp_done, g * U + (u + 1))
                nc.vector.reciprocal(rinv[:, u:u + 1], rowsum[:, u:u + 1]).then_inc(rinv_done, 1)
                dve.wait_ge(rinv_done, g * U + (u + 1))
                here = prob[:, u % 2, 0:(order[u][1] + 1) * P]
                nc.vector.tensor_scalar(here, here, rinv[:, u:u + 1], None, ALU.mult).then_inc(prob_done, 1)

            def probT_low(g, u):
                hh, t = order[u]
                dve.wait_ge(pT_hi, g * U + (u + 1))
                low(probT_s[hh][1][:, t:4 * t + 1:3, :], PT[:, u % 2, 0:(t + 1) * P].rearrange("p (j i) -> p j i", i=P),
                    probT_s[hh][0][:, t:4 * t + 1:3, :]).then_inc(pT_split, 1)

            def attn_low(g, p, hh):
                dve.wait_ge(o_hi, g * 2 + (hh + 1))
                rows = slice(hh * DH, (hh + 1) * DH)
                low(attnT_s[1][rows, bass.ds(p, 1), :], O[0:DH, :].unsqueeze(1), attnT_s[0][rows, bass.ds(p, 1), :]).then_inc(o_split, 1)

            def begin():
                for p in range(PAIRS):
                    dve.wait_ge(w_hi, p + 1)
                    for i in range(3):
                        ins = low(wqkv_s[1][:, :, p, i, :], self_raw[:, i * KT:(i + 1) * KT, p * PC:(p + 1) * PC],
                                  wqkv_s[0][:, :, p, i, :])
                    ins.then_inc(w_split, 1)
                    if p == 0:
                        split_h(0)
                dve.wait_ge(wo_hi, 1)
                low(wo_s[1][:, :, :], wo_raw, wo_s[0][:, :, :]).then_inc(wo_split, 1)
                for t in range(TT):
                    v_low(0, t, 0)
                sum_squares(0)
                q_low(0, 0, 0)
                key_norms(0)
                negate(0, 0)
                k_low(0, 0)
                maximum(0, 0, 0)

            def pair(c, g, p, odd, start, more):
                nxt, even = dve.snap(g + 1), 1 - odd
                for u in range(U):
                    if u < U - 1:
                        maximum(g, u + 1, odd)
                    normalise(g, u)
                    if u == 0 and not start:
                        probT_low(dve.snap(g - 1), U - 1)
                    if u:
                        probT_low(g, u - 1)
                    if more:
                        if u == 1:
                            v_low(nxt, 0, even)
                            v_low(nxt, 1, even)
                        if u == 2:
                            v_low(nxt, 2, even)
                        if u == 3:
                            v_low(nxt, 3, even)
                        if u == 5:
                            sum_squares(nxt)
                        if u == 5:
                            q_low(nxt, p + 1, even)
                        if u == 6:
                            key_norms(nxt)
                            negate(nxt, even)
                    if u == 2 and not start:
                        attn_low(g - 1, p - 1, 1)
                    if u == 6:
                        attn_low(g, p, 0)
                if more:
                    k_low(nxt, even)
                    maximum(nxt, 0, even)

            def finish(c, last):
                g7 = dve.snap(c * PAIRS + (PAIRS - 1))
                nxt = dve.snap(c * PAIRS + PAIRS)
                probT_low(g7, U - 1)
                if not last:
                    split_h(c + 1)
                    for t in range(3):
                        v_low(nxt, t, 0)
                attn_low(g7, PAIRS - 1, 1)
                if not last:
                    v_low(nxt, 3, 0)
                    sum_squares(nxt)
                    q_low(nxt, 0, 0)
                    key_norms(nxt)
                dve.wait_ge(wo_copied, c * TT + TT)
                for t in range(TT):
                    ins = nc.vector.bn_stats(bn[:, t, :], projected[:, t, :])
                ins.then_inc(n_stats, 1)
                dve.wait_ge(n_stats, c + 1)
                if not last:
                    negate(nxt, 0)
                for t in range(TT):
                    ins = nc.vector.bn_aggr(mv[:, t, :], bn[:, t, :])
                ins.then_inc(n_mv, 1)
                dve.wait_ge(n_mv, c + 1)
                nc.vector.tensor_scalar_add(veps[:, :], mv[:, :, 1], EPS).then_inc(n_var, 1)
                if not last:
                    k_low(nxt, 0)
                dve.wait_ge(n_rstd, c + 1)
                for t in range(TT):
                    ins = nc.vector.tensor_scalar(projected[:, t, :], projected[:, t, :], mv[:, t, 0:1], rstd[:, t:t + 1],
                                                  ALU.subtract, ALU.mult)
                ins.then_inc(n_done, 1)
                dve.wait_ge(hT_done, c * KT + KT)
                nc.vector.tensor_copy(hT_all[:, bass.ds(c, 1), :, :].rearrange("p c k n -> p (c k) n"), hT_now[:, :, :]).then_inc(hT_kept, 1)
                dve.wait_ge(g_ready, c + 1)
                logits = O[:, 0:TT * E].rearrange("p (t e) -> p t e", e=E)
                nc.vector.reduce_max(g_max[:, :], logits, AX.X).then_inc(g_max_done, 1)
                dve.wait_ge(g_max_done, c + 1)
                nc.vector.tensor_tensor(g_exp[:, :, :], logits, g_max[:, :].unsqueeze(2).to_broadcast([P, TT, E]), ALU.subtract).then_inc(g_sub, 1)
                dve.wait_ge(g_exp_done, c + 1)
                nc.vector.reduce_sum(g_sum[:, :], g_exp[:, :, :], AX.X).then_inc(g_sum_done, 1)
                dve.wait_ge(g_sum_done, c + 1)
                nc.vector.reciprocal(g_inv[:, :], g_sum[:, :]).then_inc(g_inv_done, 1)
                dve.wait_ge(g_inv_done, c + 1)
                nc.vector.tensor_tensor(gate_all[:, bass.ds(c, 1), :, :].rearrange("p c t e -> p (c t) e"), g_exp[:, :, :],
                                        g_inv[:, :].unsqueeze(2).to_broadcast([P, TT, E]), ALU.mult).then_inc(g_done, 1)
                if not last:
                    maximum(nxt, 0, 0)

            pairs(nc.vector, begin, pair, finish)

        @block.tensor
        def _(pe):
            THREE = ((0, 0), (1, 0), (0, 1))

            def project(c, g, p, t):
                bank = t % 3
                if t == 0:
                    pe.wait_ge(v_split, g * TT)
                if t == 1:
                    pe.wait_ge(qT_split, g)
                if t == 2:
                    pe.wait_ge(kT_split, g)
                if t == 3:
                    pe.wait_ge(v_split, g * TT + 1)
                steps = [(a, b, k) for a, b in THREE for k in range(KT)]
                for i, (a, b, k) in enumerate(steps):
                    ins = nc.tensor.matmul(A[:, bank, 0:3 * PC], h_s[a][:, k, t * P:(t + 1) * P],
                                           wqkv_s[b][:, k, bass.ds(p, 1), :, :].rearrange("p a b c -> p a (b c)"),
                                           start=i == 0, stop=i == len(steps) - 1)
                ins.then_inc(proj_ready, 1)

            def transpose_q(g):
                pe.wait_ge(qk_copied, g * TT + TT)
                pe.wait_ge(v_split, g * TT + 2)
                for t in range(TT):
                    ins = nc.tensor.transpose(A[:, 1, t * P:(t + 1) * P], qk[:, t, 0, :], ident[:, :])
                ins.then_inc(qT_ready, 1)

            def transpose_k(g):
                pe.wait_ge(k_done, g + 1)
                pe.wait_ge(v_split, g * TT + 3)
                for t in range(TT):
                    ins = nc.tensor.transpose(A[:, 2, t * P:(t + 1) * P], qk[:, t, 1, :], ident[:, :])
                ins.then_inc(kT_ready, 1)

            def logits(g, u, odd, start):
                hh, t = order[u]
                if u == 0:
                    pe.wait_ge(qT_split, g + 1)
                    pe.wait_ge(kT_split, g + 1)
                if not (isinstance(g, int) and g == 0 and u < 2):
                    pe.wait_ge(exp_done, done_before(g, u, start))
                rows = slice(hh * DH, (hh + 1) * DH)
                n = (t + 1) * P
                for i, (a, b) in enumerate(THREE):
                    nc.tensor.matmul(S[:, u % 2, 0:n], qT_s[odd][a][rows, t * P:(t + 1) * P], kT_s[odd][b][rows, 0:n],
                                     start=i == 0, stop=False, skip_group_check=True)
                nc.tensor.matmul(S[:, u % 2, t * P:n], ident_b[:, :], mask[:, :], start=False, stop=True,
                                 skip_group_check=True).then_inc(s_ready, 1)

            def transpose_probs(g, u, start):
                t = order[u][1]
                pe.wait_ge(pT_split, done_before(g, u, start))
                pe.wait_ge(prob_done, g * U + (u + 1))
                for j in range(t + 1):
                    ins = nc.tensor.transpose(PT[:, u % 2, j * P:(j + 1) * P], prob[:, u % 2, j * P:(j + 1) * P], ident[:, :])
                ins.then_inc(pT_ready, 1)

            def attend(c, g, hh, odd, start):
                pe.wait_ge(o_split, g * 2 + hh)
                if start:
                    pe.wait_ge(g_sub, c)
                pe.wait_ge(pT_split, g * U + (hh + 1) * TT)
                steps = [(a, b, j) for j in range(TT) for a, b in THREE]
                for i, (a, b, j) in enumerate(steps):
                    probs = probT_s[hh][b][:, 4 * j:3 * j + TT, :].rearrange("p a b -> p (a b)")
                    ins = nc.tensor.matmul(O[0:DH, j * P:ROWS], v_s[odd][a][:, j, hh * DH:(hh + 1) * DH], probs,
                                           start=i == 0, stop=i == len(steps) - 1, skip_group_check=True)
                ins.then_inc(o_ready, 1)

            def begin():
                pe.wait_ge(w_split, 1)
                pe.wait_ge(h_split, 1)
                for t in range(TT):
                    project(0, 0, 0, t)
                transpose_q(0)
                transpose_k(0)
                pe.wait_ge(w_split, PAIRS)
                logits(0, 0, 0, True)
                logits(0, 1, 0, True)

            def pair(c, g, p, odd, start, more):
                nxt, even = pe.snap(g + 1), 1 - odd
                for u in range(U):
                    if u < U - 2:
                        logits(g, u + 2, odd, start)
                    transpose_probs(g, u, start)
                    if more:
                        if u == 0:
                            project(c, nxt, p + 1, 0)
                            project(c, nxt, p + 1, 1)
                        if u in (1, 2):
                            project(c, nxt, p + 1, u + 1)
                        if u == 4:
                            transpose_q(nxt)
                        if u == 7:
                            transpose_k(nxt)
                    if u == 0 and not start:
                        attend(c, g - 1, 1, even, False)
                    if u == 5:
                        attend(c, g, 0, odd, start)
                if more:
                    logits(nxt, 0, even, False)
                    logits(nxt, 1, even, False)

            def finish(c, last):
                g7 = pe.snap(c * PAIRS + (PAIRS - 1))
                nxt = pe.snap(c * PAIRS + PAIRS)
                if not last:
                    pe.wait_ge(h_split, c + 2)
                    for t in range(3):
                        project(c, nxt, 0, t)
                attend(c, g7, 1, 1, False)
                if not last:
                    project(c, nxt, 0, 3)
                    transpose_q(nxt)
                pe.wait_ge(wo_split, 1)
                pe.wait_ge(o_split, c * 16 + 16)
                pe.wait_ge(exp_done, c * 64 + 64)
                for t in range(TT):
                    if t >= 2:
                        pe.wait_ge(wo_copied, c * TT + (t - 1))
                    steps = [(a, b, p) for a, b in THREE for p in range(PAIRS)]
                    for i, (a, b, p) in enumerate(steps):
                        ins = nc.tensor.matmul(S[:, t % 2, 0:D], attnT_s[a][:, p, t * P:(t + 1) * P], wo_s[b][:, p, :],
                                               start=i == 0, stop=i == len(steps) - 1)
                    ins.then_inc(wo_ready, 1)
                if not last:
                    transpose_k(nxt)
                pe.wait_ge(n_done, c + 1)
                pe.wait_ge(pT_split, c * 64 + 64)
                for k in range(KT):
                    for t in range(TT):
                        ins = nc.tensor.transpose(PT[:, k, t * P:(t + 1) * P], projected[:, t, k * P:(k + 1) * P], ident[:, :])
                    ins.then_inc(n_ready, 1)
                pe.wait_ge(hT_done, c * KT + KT)
                for t in range(TT):
                    here = slice(t * P, (t + 1) * P)
                    for k in range(KT):
                        nc.tensor.matmul(O[:, t * E:(t + 1) * E],
                                         hT_now[:, k, here], T["gate_w"][:, k, :], start=k == 0, stop=False)
                    ins = nc.tensor.matmul(O[:, t * E:(t + 1) * E], ones[0:1, :], T["gate_b"][:, :], start=False, stop=True)
                ins.then_inc(g_ready, 1)
                if not last:
                    pe.wait_ge(wo_copied, c * TT + TT)
                    logits(nxt, 0, 0, True)
                    logits(nxt, 1, 0, True)

            pairs(nc.tensor, begin, pair, finish)


def experts_phase(nc, T, ln_g, ln_b, w1, b2, w2, x1_dram, out):
    hT_all, gate_all, columns = T["hT_all"], T["gate_all"], T["columns"]
    ident, neg_half = T["ident"], T["neg_half"]
    moe_sum = hT_all[:, :, :, :].rearrange("p c k n -> p c (k n)").rearrange("p c (t d) -> p c t d", d=D)
    KT, FT = D // P, FF // P
    LAST = E - 1

    ctx = ExitStack()
    with ctx:
        sb = lambda name, shape, dt: ctx.enter_context(nc.sbuf_tensor(name, shape, dt))
        sem = lambda name: ctx.enter_context(nc.semaphore(name))
        h_hi = sb("h2T_hi", [P, CHUNKS, KT, ROWS], f32r)
        h_lo = sb("h2T_lo", [P, CHUNKS, KT, ROWS], f32r)
        W1_COLS = KT * FF
        W_COLS = W1_COLS + FT * D
        w_hi = [sb(f"w_hi{i}", [P, W_COLS], f32r) for i in range(2)]
        w_lo = [sb(f"w_lo{i}", [P, W_COLS], f32r) for i in range(2)]
        w_raw = sb("w_raw", [P, W_COLS], f32)
        g_rows, b_rows = sb("g_rows", [P, D], f32), sb("b_rows", [P, D], f32)
        b2_sb = sb("b2_sb", [E, D], f32)
        hid = sb("hid", [P, 2, ROWS], f32)
        hid_hi = sb("hid_hi", [P, 4, ROWS], f32r)
        hid_lo = sb("hid_lo", [P, 4, ROWS], f32r)
        gT = hid[0:E, :, :]
        x1c = w_raw[:, 0:TT * D].rearrange("p (t d) -> p t d", d=D)
        bn = sb("bn2", [P, TT, 6], f32)
        mv = sb("mv2", [P, TT, 2], f32)
        veps = sb("veps2", [P, TT], f32)
        rstd = sb("rstd2", [P, TT], f32)
        H = ctx.enter_context(nc.psum_tensor("psum_hid", [P, 4, 512], f32))
        O = ctx.enter_context(nc.psum_tensor("psum_out", [P, 4, 2, D], f32))

        w_loaded = sem("w_loaded")
        b2_loaded = sem("b2_loaded")
        norm_loaded = sem("norm_loaded")
        w_hi_done = sem("w_hi_done")
        w_split = sem("w_split")
        h_hi_done = sem("h_hi_done")
        h_split = sem("h_split")
        gT_ready = sem("gT_ready")
        gT_copied = sem("gT_copied")
        bias_ready = sem("bias_ready")
        sum_begun = sem("sum_begun")
        hid_ready = sem("hid_ready")
        gelu_done = sem("gelu_done")
        hid_hi_done = sem("hid_hi_done")
        hid_split = sem("hid_split")
        out_used = sem("out_used")
        sum_done = sem("sum_done")
        x1_loaded = sem("x1_loaded")
        stats_done = sem("stats_done")
        mv_done = sem("mv_done")
        var_done = sem("var_done")
        rstd_done = sem("rstd_done")
        norm_step = sem("norm_step")
        y_done = sem("y_done")
        stored = sem("stored")
        block = ctx.enter_context(nc.Block())

        def experts(engine, run):
            run(0, 0, True, False)
            with engine.Fori(0, (E - 2) // 2) as i:
                for step in (1, 2):
                    run(engine.snap(i * 2 + step), step % 2, False, False)
            run(LAST, LAST % 2, False, True)

        def cell(e, c):
            return e * CHUNKS + c

        @block.sync
        def _(sp):
            def load_weights(e, first):
                if not first:
                    sp.wait_ge(w_split, 8 * e)
                sp.dma_start(w_raw[:, 0:W1_COLS].rearrange("p (k f) -> p k f", k=KT),
                             w1[bass.ds(e, 1), :, :].rearrange("e (k p) f -> p (e k) f", p=P)).then_inc(w_loaded, 16)
                sp.dma_start(w_raw[:, W1_COLS:W_COLS].rearrange("p (k f) -> p k f", k=FT),
                             w2[bass.ds(e, 1), :, :].rearrange("e (k p) f -> p (e k) f", p=P)).then_inc(w_loaded, 16)

            load_weights(0, True)
            sp.dma_start(b2_sb[:, :], b2).then_inc(b2_loaded, 16)
            sp.dma_start(g_rows[:, :], ln_g.unsqueeze(0).to_broadcast([P, D])).then_inc(norm_loaded, 16)
            sp.dma_start(b_rows[:, :], ln_b.unsqueeze(0).to_broadcast([P, D])).then_inc(norm_loaded, 16)
            with sp.Fori(1, E) as e:
                load_weights(e, False)
            for c in range(CHUNKS):
                if c:
                    sp.wait_ge(y_done, c)
                    sp.wait_ge(x1_loaded, 16 * c)
                else:
                    sp.wait_ge(w_split, 8 * E)
                sp.dma_start(x1c[:, :, :], x1_dram[c, :, :, :].rearrange("t p d -> p t d")).then_inc(x1_loaded, 16)
                sp.wait_ge(y_done, c + 1)
                sp.dma_start(out[c, :, :].rearrange("(t p) d -> p t d", p=P), moe_sum[:, c, :, :]).then_inc(stored, 16)
            sp.wait_ge(stored, 16 * CHUNKS)

        @block.gpsimd
        def _(pool):
            for c in range(CHUNKS):
                pool.wait_ge(var_done, c + 1)
                nc.gpsimd.tensor_tensor(rstd[:, :], veps[:, :], neg_half[:, 0:TT], ALU.pow).then_inc(rstd_done, 1)

        @block.scalar
        def _(act):
            act.wait_ge(w_loaded, 32)
            for i in range(8):
                nc.scalar.activation(w_hi[0][:, i * 512:(i + 1) * 512], w_raw[:, i * 512:(i + 1) * 512],
                                     ACT.Copy).then_inc(w_hi_done, 1)
            for c in range(CHUNKS):
                nc.scalar.activation(h_hi[:, c, :, :], hT_all[:, c, :, :], ACT.Copy).then_inc(h_hi_done, 1)
                act.wait_ge(gT_ready, c + 1)
                if c >= 2:
                    act.wait_ge(bias_ready, c - 1)
                nc.scalar.activation(gT[:, c % 2, :], H[0:E, c % 4, :], ACT.Copy).then_inc(gT_copied, 1)
            def gelus(e, c, first):
                base = act.snap(cell(e, c) * FT)
                for f in range(FT):
                    act.wait_ge(hid_ready, base + (f + 1))
                    if not first or f >= 2:
                        act.wait_ge(hid_split, base + (f - 1))
                    nc.scalar.activation(hid[:, f % 2, :], H[:, f % 4, :], ACT.Gelu_apprx_tanh,
                                         bias=columns[:, bass.ds(e * FT + (COL_B1 + f), 1)]).then_inc(gelu_done, 1)

            def run(e, odd, first, last):
                if first:
                    gelus(0, 0, True)
                with nc.scalar.Fori(int(first), CHUNKS) as c:
                    gelus(e, c, False)

            experts(nc.scalar, run)

        @block.vector
        def _(dve):
            def split_weights(e, odd, i):
                cols = bass.ds(i * 512, 512)
                nc.vector.tensor_copy(w_hi[odd][:, cols], w_raw[:, cols]).then_inc(w_hi_done, 1)
                dve.wait_ge(w_hi_done, e * 8 + i + 1)
                nc.vector.tensor_tensor(w_lo[odd][:, cols], w_raw[:, cols], w_hi[odd][:, cols].bitcast(f32),
                                        ALU.subtract).then_inc(w_split, 1)

            for i in range(8):
                dve.wait_ge(w_hi_done, i + 1)
                cols = slice(i * 512, (i + 1) * 512)
                nc.vector.tensor_tensor(w_lo[0][:, cols], w_raw[:, cols], w_hi[0][:, cols].bitcast(f32),
                                        ALU.subtract).then_inc(w_split, 1)
            for c in range(CHUNKS):
                dve.wait_ge(h_hi_done, c + 1)
                nc.vector.tensor_tensor(h_lo[:, c, :, :], hT_all[:, c, :, :], h_hi[:, c, :, :].bitcast(f32),
                                        ALU.subtract).then_inc(h_split, 1)
                dve.wait_ge(bias_ready, c + 1)
                dve.wait_ge(h_split, c + 1)
                nc.vector.tensor_copy(moe_sum[:, c, :, :], O[:, c % 2 * 2:c % 2 * 2 + 2, :, :]
                                      .rearrange("p a b d -> p (a b) d")).then_inc(sum_begun, 1)

            def split_hidden(base, f):
                dve.wait_ge(gelu_done, base + (f + 1))
                nc.vector.tensor_copy(hid_hi[:, f % 4, :], hid[:, f % 2, :]).then_inc(hid_hi_done, 1)
                dve.wait_ge(hid_hi_done, base + (f + 1))
                nc.vector.tensor_tensor(hid_lo[:, f % 4, :], hid[:, f % 2, :], hid_hi[:, f % 4, :].bitcast(f32),
                                        ALU.subtract).then_inc(hid_split, 1)

            def slot_free(base, f, begun):
                if begun or f >= 4:
                    dve.wait_ge(out_used, base + (f - 3))

            def add_chunk(e, c, n, first):
                dve.wait_ge(out_used, (n + 1) * FT)
                if not first:
                    dve.wait_ge(sum_done, n - (CHUNKS - 1))
                half = n % 2 * 2
                for t in range(TT):
                    ins = nc.vector.scalar_tensor_tensor(
                        out=moe_sum[:, bass.ds(c, 1), t, :], in0=O[:, bass.ds(half + t // 2, 1), t % 2, :],
                        scalar=gate_all[:, bass.ds(c, 1), t, bass.ds(e, 1)].rearrange("p a b -> p (a b)"),
                        in1=moe_sum[:, bass.ds(c, 1), t, :], op0=ALU.mult, op1=ALU.add)
                ins.then_inc(sum_done, 1)

            def final_norm(c):
                dve.wait_ge(sum_done, cell(LAST, c) + 1)
                for t in range(TT):
                    ins = nc.vector.bn_stats(bn[:, t, :], moe_sum[:, c, t, :])
                ins.then_inc(stats_done, 1)
                dve.wait_ge(stats_done, c + 1)
                for t in range(TT):
                    ins = nc.vector.bn_aggr(mv[:, t, :], bn[:, t, :])
                ins.then_inc(mv_done, 1)
                dve.wait_ge(mv_done, c + 1)
                nc.vector.tensor_scalar_add(veps[:, :], mv[:, :, 1], EPS).then_inc(var_done, 1)
                dve.wait_ge(rstd_done, c + 1)
                for t in range(TT):
                    ins = nc.vector.tensor_scalar(moe_sum[:, c, t, :], moe_sum[:, c, t, :], mv[:, t, 0:1], rstd[:, t:t + 1],
                                                  ALU.subtract, ALU.mult)
                ins.then_inc(norm_step, 1)
                dve.wait_ge(norm_step, 3 * c + 1)
                dve.wait_ge(norm_loaded, 32)
                nc.vector.tensor_tensor(moe_sum[:, c, :, :], moe_sum[:, c, :, :], g_rows[:, :].unsqueeze(1).to_broadcast([P, TT, D]),
                                        ALU.mult).then_inc(norm_step, 1)
                dve.wait_ge(norm_step, 3 * c + 2)
                nc.vector.tensor_tensor(moe_sum[:, c, :, :], moe_sum[:, c, :, :], b_rows[:, :].unsqueeze(1).to_broadcast([P, TT, D]),
                                        ALU.add).then_inc(norm_step, 1)
                dve.wait_ge(norm_step, 3 * c + 3)
                dve.wait_ge(x1_loaded, 16 * (c + 1))
                nc.vector.tensor_tensor(moe_sum[:, c, :, :], moe_sum[:, c, :, :], x1c[:, :, :], ALU.add).then_inc(y_done, 1)

            def run(e, odd, first, last):
                def chunk(c):
                    base = dve.snap(cell(e, c) * FT)
                    for f in range(FT):
                        slot_free(base, f, True)
                        split_hidden(base, f)
                        if f == 1:
                            add_chunk(e, c - 1, dve.snap(cell(e, c - 1)), first)
                        if f == 4 and not last:
                            split_weights(e + 1, 1 - odd, c)
                        if f == 4 and last:
                            final_norm(c - 1)

                for f in range(FT):
                    slot_free(cell(e, 0) * FT, f, not first)
                    split_hidden(cell(e, 0) * FT, f)
                if last:
                    for c in range(1, CHUNKS):
                        chunk(c)
                else:
                    dve.wait_ge(w_loaded, e * 32 + 64)
                    split_weights(e + 1, 1 - odd, 0)
                    with nc.vector.Fori(1, CHUNKS) as c:
                        chunk(c)
                add_chunk(e, CHUNKS - 1, cell(e, CHUNKS - 1), first)

            experts(nc.vector, run)
            final_norm(CHUNKS - 1)

        @block.tensor
        def _(pe):
            def weights1(odd, half, k, f):
                at = k * FF + f * P
                return (w_hi, w_lo)[half][odd][:, at:at + P]

            def weights2(odd, half, f):
                at = W1_COLS + f * D
                return (w_hi, w_lo)[half][odd][:, at:at + D]

            def up(odd, c, f, base):
                if base is not None:
                    pe.wait_ge(gelu_done, base + (f - 3))
                steps = [(a, b, k) for a, b in ((0, 0), (1, 0), (0, 1)) for k in range(KT)]
                for i, (a, b, k) in enumerate(steps):
                    ins = nc.tensor.matmul(H[:, f % 4, :], weights1(odd, a, k, f),
                                           (h_hi, h_lo)[b][:, bass.ds(c, 1), k, :],
                                           start=i == 0, stop=i == len(steps) - 1)
                ins.then_inc(hid_ready, 1)

            def down(odd, f, n):
                pe.wait_ge(hid_split, n * FT + (f + 1))
                half = n % 2 * 2
                for t in range(TT):
                    for i, (a, b) in enumerate(((0, 0), (1, 0), (0, 1))):
                        tokens = (hid_hi, hid_lo)[a][:, f % 4, t * P:(t + 1) * P]
                        ins = nc.tensor.matmul(O[:, bass.ds(half + t // 2, 1), t % 2, :], tokens, weights2(odd, b, f),
                                               start=f == 0 and i == 0 and t % 2 == 0,
                                               stop=f == FT - 1 and i == 2, skip_group_check=True)
                ins.then_inc(out_used, 1)

            pe.wait_ge(b2_loaded, 16)
            for c in range(CHUNKS):
                if c >= 4:
                    pe.wait_ge(gT_copied, c - 3)
                for t in range(TT):
                    ins = nc.tensor.transpose(H[0:E, c % 4, t * P:(t + 1) * P], gate_all[:, c, t, :], ident[:, :])
                ins.then_inc(gT_ready, 1)
                pe.wait_ge(gT_copied, c + 1)
                if c >= 2:
                    pe.wait_ge(sum_begun, c - 1)
                for t in range(TT):
                    ins = nc.tensor.matmul(O[:, c % 2 * 2 + t // 2, t % 2, :], gT[:, c % 2, t * P:(t + 1) * P],
                                           b2_sb[:, :], start=t % 2 == 0, stop=True, skip_group_check=True)
                ins.then_inc(bias_ready, 1)

            pe.wait_ge(w_split, 8)
            pe.wait_ge(h_split, 2)
            pe.wait_ge(sum_begun, CHUNKS)
            up(0, 0, 0, None)
            up(0, 0, 1, None)

            def run(e, odd, first, last):
                def chunk(c, closing, begun):
                    n = pe.snap(cell(e, c))
                    base = pe.snap(n * FT)
                    for f in range(FT):
                        if f < FT - 2:
                            up(odd, c, f + 2, base if begun or f + 2 >= 4 else None)
                        elif not closing:
                            up(odd, c + 1, f + 2 - FT, base + FT)
                        elif not last:
                            if f == FT - 2:
                                pe.wait_ge(w_split, e * 8 + 16)
                            up(1 - odd, 0, f + 2 - FT, base + FT)
                        if f == 0 and begun:
                            pe.wait_ge(sum_done, n - 1)
                        down(odd, f, n)

                if first:
                    chunk(0, False, False)
                    pe.wait_ge(h_split, CHUNKS)
                with nc.tensor.Fori(int(first), CHUNKS - 1) as c:
                    chunk(c, False, True)
                chunk(CHUNKS - 1, True, True)

            experts(nc.tensor, run)


def xattn_ffn_kernel(nc, x, context, w_sim, b_sim, W_qv, b_qv, ln_g, ln_b, Wq, Wk, Wv, q_scale, k_scale, Wo,
                     gate_w, gate_b, w1, b1, w2, b2, out):
    x1_dram = nc.dram_tensor("x1_kept", (CHUNKS, TT, P, D), f32, kind="Internal").ap()
    with ExitStack() as ctx:
        T = {}
        for name, shape, dt in (("hT_all", [P, CHUNKS, KT, ROWS], f32), ("gate_all", [P, CHUNKS, TT, E], f32),
                                ("columns", [P, N_COLS], f32), ("ident", [P, P], f32), ("ident_b", [P, P], bf16),
                                ("mask", [P, P], bf16), ("ones", [P, P], f32), ("neg_half", [P, 8], f32),
                                ("qk_scale", [P, PAIRS], f32), ("gate_w", [P, KT, E], f32), ("gate_b", [1, E], f32)):
            T[name] = ctx.enter_context(nc.sbuf_tensor(name, shape, dt))
        setup_phase(nc, T, w_sim, ln_g, ln_b, q_scale, k_scale, gate_w, gate_b, b1)
        with nc.sbuf_tensor("self_raw", [P, 3 * KT + 2, HEADS * DH], f32) as self_raw:
            T["self_raw"] = self_raw
            cross_attention_phase(nc, T, x, context, W_qv, b_qv, b_sim, Wq, Wk, Wv, Wo, x1_dram)
        self_attention_phase(nc, T)
        experts_phase(nc, T, ln_g, ln_b, w1, b2, w2, x1_dram, out)


_INS = ['x', 'ctx_1024', 'L0_xattn_w_sim', 'L0_xattn_b_sim', 'L0_xattn_W_qv', 'L0_xattn_b_qv', 'L0_ffn_ln_g',
        'L0_ffn_ln_b', 'L0_ffn_Wq', 'L0_ffn_Wk', 'L0_ffn_Wv', 'L0_ffn_q_scale', 'L0_ffn_k_scale', 'L0_ffn_Wo',
        'L0_ffn_gate_w', 'L0_ffn_gate_b', 'L0_ffn_w1', 'L0_ffn_b1', 'L0_ffn_w2', 'L0_ffn_b2']
_OUTS = [((8, 512, 256), 'float32')]


def kernel(**inputs):
    import numpy as _np
    import concourse.bacc as _bacc
    from concourse import mybir as _mybir
    from concourse.bass_utils import run_bass_kernel_spmd as _run

    nc = _bacc.Bacc("TRN2", target_bir_lowering=False, num_devices=1)
    arrays, args = {}, []
    for name in _INS:
        a = _np.ascontiguousarray(inputs[name])
        arrays[f"in_{name}_dram"] = a
        args.append(nc.dram_tensor(f"in_{name}_dram", a.shape, _mybir.dt.from_np(a.dtype), kind="ExternalInput").ap())
    for i, (shape, dtype) in enumerate(_OUTS):
        dt = _mybir.dt.from_np(_np.dtype(dtype))
        args.append(nc.dram_tensor(f"out_{i}_dram", shape, dt, kind="ExternalOutput").ap())
    xattn_ffn_kernel(nc, *args)
    r = _run(nc, [arrays], core_ids=[0])
    got = tuple(r.results[0][f"out_{i}_dram"] for i in range(len(_OUTS)))
    return got[0]
```

```python
from contextlib import ExitStack

import concourse.bass as bass
from concourse import mybir

f32 = mybir.dt.float32
f32r = mybir.dt.float32r
bf16 = mybir.dt.bfloat16
ALU = mybir.AluOpType
ACT = mybir.ActivationFunctionType
AX = mybir.AxisListType

P = 128
CHUNKS, ROWS, D = 8, 512, 256
TT = ROWS // P
KT = D // P
HEADS, DH = 16, 64
PAIRS = HEADS // 2
E, FF = 8, 1024
EPS = 1e-5
QK_SCALE = 10.0
MASKED = -1e30

COL_WSIM, COL_G, COL_B, COL_QS, COL_KS, COL_B1 = 0, 6, 8, 10, 18, 26
N_COLS = COL_B1 + E * FF // P


def setup_phase(nc, T, w_sim, ln_g, ln_b, q_scale, k_scale, gate_w, gate_b, b1):
    ident, ones, neg_half, columns = T["ident"], T["ones"], T["neg_half"], T["columns"]
    ctx = ExitStack()
    with ctx:
        rows = ctx.enter_context(nc.sbuf_tensor("param_rows", [N_COLS, P], f32))
        cols_ps = ctx.enter_context(nc.psum_tensor("psum_columns", [P, 512], f32))
        sem = lambda name: ctx.enter_context(nc.semaphore(name))
        rows_loaded, gate_loaded = sem("rows_loaded"), sem("gate_loaded")
        ident_zero, ident_done, consts_done = sem("ident_zero"), sem("ident_done"), sem("consts_done")
        cols_ready, cols_done = sem("cols_ready"), sem("cols_done")
        block = ctx.enter_context(nc.Block())

        @block.sync
        def _(sp):
            for at, src, n in ((COL_WSIM, w_sim, 6), (COL_G, ln_g, 2), (COL_B, ln_b, 2)):
                sp.dma_start(rows[at:at + n, :], src.rearrange("(r p) -> r p", p=P)).then_inc(rows_loaded, 16)
            for at, src in ((COL_QS, q_scale), (COL_KS, k_scale)):
                sp.dma_start(rows[at:at + PAIRS, :], src.rearrange("(r h) a d -> r (h a d)", h=2)).then_inc(rows_loaded, 16)
            sp.dma_start(rows[COL_B1:N_COLS, :], b1.rearrange("e (f p) -> (e f) p", p=P)).then_inc(rows_loaded, 16)

        @block.gpsimd
        def _(pool):
            nc.gpsimd.memset(ident[:, :], 0.0).then_inc(ident_zero, 1)
            nc.gpsimd.memset(ones[:, :], 1.0).then_inc(consts_done, 1)
            nc.gpsimd.memset(neg_half[:, :], -0.5).then_inc(consts_done, 1)
            nc.gpsimd.memset(T["mask"][:, :], 0.0).then_inc(ident_zero, 1)
            pool.wait_ge(ident_zero, 2)
            nc.gpsimd.affine_select(out=T["mask"][:, :], in_=T["mask"][:, :], compare_op=ALU.is_ge, fill=MASKED,
                                    base=0, pattern=[[-1, P]], channel_multiplier=1).then_inc(ident_done, 1)
            nc.gpsimd.affine_select(out=ident[:, :], in_=ident[:, :], compare_op=ALU.not_equal, fill=1.0,
                                    base=0, pattern=[[-1, P]], channel_multiplier=1).then_inc(ident_done, 1)

        @block.scalar
        def _(act):
            act.dma_start(T["gate_w"][:, :, :], gate_w.rearrange("(k p) e -> p k e", p=P)).then_inc(gate_loaded, 16)
            act.dma_start(T["gate_b"][:, :], gate_b.unsqueeze(0)).then_inc(gate_loaded, 16)
            act.wait_ge(gate_loaded, 32)

        @block.tensor
        def _(pe):
            pe.wait_ge(rows_loaded, 96)
            pe.wait_ge(ident_done, 2)
            nc.tensor.transpose(cols_ps[:, 0:N_COLS], rows[:, :], ident[0:N_COLS, 0:N_COLS]).then_inc(cols_ready, 1)

        @block.vector
        def _(dve):
            dve.wait_ge(cols_ready, 1)
            nc.vector.tensor_copy(columns[:, :], cols_ps[:, 0:N_COLS]).then_inc(cols_done, 1)
            dve.wait_ge(cols_done, 1)
            nc.vector.scalar_tensor_tensor(out=T["qk_scale"][:, :], in0=columns[:, COL_QS:COL_QS + PAIRS],
                                           scalar=QK_SCALE, in1=columns[:, COL_KS:COL_KS + PAIRS],
                                           op0=ALU.mult, op1=ALU.mult).then_inc(cols_done, 1)
            dve.wait_ge(ident_done, 2)
            nc.vector.tensor_copy(T["ident_b"][:, :], ident[:, :]).then_inc(cols_done, 1)
            dve.wait_ge(consts_done, 2)


def cross_attention_phase(nc, T, x, context, W_qv, b_qv, b_sim, Wq, Wk, Wv, Wo, x1_dram):
    ident, ones, neg_half, columns = T["ident"], T["ones"], T["neg_half"], T["columns"]
    hT_all, self_raw = T["hT_all"], T["self_raw"]

    ctx = ExitStack()
    with ctx:
        sb = lambda name, shape, dt=f32: ctx.enter_context(nc.sbuf_tensor(name, shape, dt))
        pair = lambda name, shape: (sb(name + "_hi", shape, f32r), sb(name + "_lo", shape, f32r))
        sem = lambda name: ctx.enter_context(nc.semaphore(name))

        xb = [sb(f"x_biased{i}", [P, TT, D]) for i in range(2)]
        encT = [sb(f"encT{i}", [P, KT, ROWS]) for i in range(2)]
        enc_s = [pair(f"encT_s{i}", [P, KT, ROWS]) for i in range(2)]
        xr = sb("x_raw", [P, TT, D])
        enc = sb("enc", [P, TT, D])
        cx = sb("cx", [P, TT, D])
        cx_s = pair("cx_s", [P, TT, D])
        cxT_s = pair("cxT_s", [P, KT, ROWS])
        ep = sb("ep", [P, KT, ROWS])
        ep_s = pair("ep_s", [P, KT, ROWS])
        prob = sb("prob", [P, TT, ROWS])
        probT_s = pair("probT_s", [P, TT, ROWS])
        hq_s = pair("hq_s", [P, KT, ROWS])
        prod = sb("prod", [P, KT, ROWS])
        prod_s = pair("prod_s", [P, KT, ROWS])
        w_enc = sb("w_enc", [P, KT, D])
        w_bar = sb("w_bar", [P, KT, D])
        w_mid_s = pair("w_mid_s", [P, 2 * KT, D])
        w_mix = sb("w_mix", [P, KT, D])
        w_mix_s = pair("w_mix_s", [P, KT, D])
        x1 = sb("x1_chunk", [P, TT, D])
        h = ep[:, :, :].rearrange("p k n -> p (k n)").rearrange("p (t d) -> p t d", d=D)
        bn = sb("bn", [P, TT, 6])
        mv = sb("mv", [P, TT, 2])
        veps = sb("veps", [P, TT])
        rstd = sb("rstd", [P, TT])
        bn1 = sb("bn1", [P, TT, 6])
        mv1 = sb("mv1", [P, TT, 2])
        veps1 = sb("veps1", [P, TT])
        rstd1 = sb("rstd1", [P, TT])
        rowmax = sb("rowmax", [P, TT])
        nrowmax = sb("nrowmax", [P, TT])
        rowsum = sb("rowsum", [P, TT])
        rinv = sb("rinv", [P, TT])
        mx = sb("mx", [P, TT])
        mcol = sb("mcol", [P, 1])
        gmax = sb("gmax", [1, 1])
        ngmax = sb("ngmax", [P, 1])
        bexp = sb("bexp", [P, TT])
        binv = sb("binv", [P, 1])
        hc = sb("hc", [P, KT])
        bqv_rows = sb("bqv_rows", [P, D])
        bsim = sb("bsim", [P, 1])
        w_stage = prob[:, 0:2, :].rearrange("p a b -> p (a b)").rearrange("p (k d) -> p k d", d=D)

        TR = ctx.enter_context(nc.psum_tensor("psum_transposed", [P, 2, 512], f32))
        S = ctx.enter_context(nc.psum_tensor("psum_scores", [P, 2, 512], f32))
        HQ = ctx.enter_context(nc.psum_tensor("psum_hq", [P, 2, 512], f32))
        X = ctx.enter_context(nc.psum_tensor("psum_x1", [P, 2, 512], f32))
        BATT = S[:, 0, :]

        bias_loaded = sem("bias_loaded")
        cx_loaded, w_loaded, qkv_loaded = sem("cx_loaded"), sem("wqv_loaded"), sem("qkv_loaded")
        x_loaded = sem("x_loaded")
        wmid_hi, wmid_split = sem("wmid_hi"), sem("wmid_split")
        enc_stats, enc_mv, enc_var, enc_rstd, enc_done, xb_done = map(
            sem, ("enc_stats", "enc_mv", "enc_var", "enc_rstd", "enc_done", "xb_done"))
        encT_ready, encT_copied, ep_copied, enc_hi, enc_split, ep_hi, ep_split = map(
            sem, ("encT_ready", "encT_copied", "ep_copied", "enc_hi", "enc_split", "ep_hi", "ep_split"))
        cxT_ready, cxT_hi, cxT_split, cx_hi, cx_split = map(
            sem, ("cxT_ready", "cxT_hi", "cxT_split", "cx_hi", "cx_split"))
        hq_ready, hq_hi, hq_split, prod_done, prod_hi, prod_split = map(
            sem, ("hq_ready", "hq_hi", "hq_split", "prod_done", "prod_hi", "prod_split"))
        s_ready, max_done, nmax_done, exp_done, rinv_done, prob_done = map(
            sem, ("s_ready", "max_done", "nmax_done", "exp_done", "rinv_done", "prob_done"))
        pT_ready, pT_hi, pT_split = map(sem, ("pT_ready", "pT_hi", "pT_split"))
        r_ready, mx_done, mcol_done, mcolT_ready, gmax_done, gmax_spread, ngmax_done, bexp_done = map(
            sem, ("r_ready", "mx_done", "mcol_done", "mcolT_ready", "gmax_done", "gmax_spread", "ngmax_done", "bexp_done"))
        hc_ready, binv_done, hc_done, wmix_done, wmix_hi, wmix_split = map(
            sem, ("hc_ready", "binv_done", "hc_done", "wmix_done", "wmix_hi", "wmix_split"))
        x1_ready, x1_done, x1_stats, x1_mv, x1_var, x1_rstd, h_done, hT_ready, hT_done, x1_stored = map(
            sem, ("x1_ready", "x1_done", "x1_stats", "x1_mv", "x1_var", "x1_rstd", "h_done", "hT_ready", "hT_done", "x1_stored"))
        block = ctx.enter_context(nc.Block())

        def steps(engine, step):
            step(None, 0, 1, 1)
            with engine.Fori(0, (CHUNKS - 2) // 2) as i:
                for odd in range(2):
                    m = engine.snap(i * 2 + odd)
                    step(m, m + 1, m + 2, odd)
            step(CHUNKS - 2, CHUNKS - 1, None, 0)
            step(CHUNKS - 1, None, None, 1)

        @block.sync
        def _(sp):
            def load(q):
                sp.wait_ge(enc_done, q)
                sp.wait_ge(xb_done, q)
                sp.dma_start(xr[:, :, :], x[bass.ds(q, 1), :, :].rearrange("c (t p) d -> p (c t) d", p=P)).then_inc(x_loaded, 16)
                sp.wait_ge(cxT_ready, q * 2)
                sp.wait_ge(cx_split, q)
                sp.dma_start(cx[:, :, :], context[bass.ds(q, 1), :, :].rearrange("c (t p) d -> p (c t) d", p=P)).then_inc(cx_loaded, 16)

            with sp.Fori(0, CHUNKS) as q:
                load(q)

        @block.gpsimd
        def _(pool):
            def prepare(q):
                pool.wait_ge(enc_var, q + 1)
                nc.gpsimd.tensor_tensor(rstd[:, :], veps[:, :], neg_half[:, 0:TT], ALU.pow).then_inc(enc_rstd, 1)

            def with_bias(q, odd, first):
                pool.wait_ge(x_loaded, q * 16 + 16)
                if not first:
                    pool.wait_ge(x1_done, q * 4 - 4)
                nc.gpsimd.tensor_tensor(xb[odd][:, :, :], xr[:, :, :],
                                        bqv_rows[:, :].unsqueeze(1).to_broadcast([P, TT, D]), ALU.add).then_inc(xb_done, 1)

            def step(m, n, q, odd):
                if n is not None:
                    pool.wait_ge(cx_hi, n + 1)
                    nc.gpsimd.tensor_tensor(cx_s[1][:, :, :], cx[:, :, :], cx_s[0][:, :, :].bitcast(f32),
                                            ALU.subtract).then_inc(cx_split, 1)
                if m is not None:
                    for k in range(KT):
                        pool.wait_ge(prod_hi, m * 2 + (k + 1))
                        nc.gpsimd.tensor_tensor(prod_s[1][:, k, :], prod[:, k, :], prod_s[0][:, k, :].bitcast(f32),
                                                ALU.subtract).then_inc(prod_split, 1)
                if q is not None:
                    prepare(q)
                if m is not None:
                    pool.wait_ge(x1_var, m + 1)
                    nc.gpsimd.tensor_tensor(rstd1[:, :], veps1[:, :], neg_half[:, 0:TT], ALU.pow).then_inc(x1_rstd, 1)
                    pool.dma_start(x1_dram[bass.ds(m, 1), :, :, :].rearrange("c t p d -> p (c t) d"),
                                   x1[:, :, :]).then_inc(x1_stored, 16)
                if q is not None:
                    with_bias(q, odd, m is None)

            prepare(0)
            pool.wait_ge(bias_loaded, 32)
            with_bias(0, 0, True)
            steps(nc.gpsimd, step)
            pool.wait_ge(x1_stored, 16 * CHUNKS)

        @block.scalar
        def _(act):
            act.dma_start(w_enc[:, :, :], W_qv[0:D, :].rearrange("(k p) d -> p k d", p=P)).then_inc(w_loaded, 16)
            act.dma_start(w_bar[:, :, :], W_qv[3 * D:4 * D, :].rearrange("(k p) d -> p k d", p=P)).then_inc(w_loaded, 16)
            act.dma_start(w_stage, W_qv[D:3 * D, :].rearrange("(k p) d -> p k d", p=P)).then_inc(w_loaded, 16)
            act.wait_ge(w_loaded, 48)
            act.dma_start(bqv_rows[:, :], b_qv.unsqueeze(0).to_broadcast([P, D])).then_inc(bias_loaded, 16)
            act.dma_start(bsim[:, :], b_sim.unsqueeze(0).to_broadcast([P, 1])).then_inc(bias_loaded, 16)
            nc.scalar.activation(w_mid_s[0][:, :, :], w_stage, ACT.Copy).then_inc(wmid_hi, 1)
            for i, w in enumerate((Wq, Wk, Wv)):
                act.dma_start(self_raw[:, i * KT:(i + 1) * KT, :], w.rearrange("(k p) n -> p k n", p=P)).then_inc(qkv_loaded, 16)
            act.dma_start(self_raw[:, 3 * KT:, :].rearrange("p a b -> p (a b)").rearrange("p (k d) -> p k d", d=D),
                          Wo.rearrange("(k p) d -> p k d", p=P)).then_inc(qkv_loaded, 16)

            def step(m, n, q, odd):
                if n is not None:
                    for k in range(KT):
                        act.wait_ge(encT_ready, n * 2 + (k + 1))
                        act.wait_ge(x1_ready, n * 4 - 4 if m is not None else 0)
                        act.wait_ge(prod_done, n * 2 - 2 if m is not None else 0)
                        nc.scalar.activation(encT[1 - odd][:, k, :], TR[:, k, :], ACT.Copy).then_inc(encT_copied, 1)
                        act.wait_ge(ep_split, n * 2)
                        act.wait_ge(hT_ready, n * 2 - 2 if m is not None else 0)
                        nc.scalar.activation(ep[:, k, :], TR[:, k, :], ACT.Identity,
                                             scale=columns[:, COL_WSIM + 4 + k:COL_WSIM + 5 + k],
                                             bias=columns[:, COL_WSIM + 2 + k:COL_WSIM + 3 + k]).then_inc(ep_copied, 1)
                    for k in range(KT):
                        act.wait_ge(cxT_ready, n * 2 + (k + 1))
                        act.wait_ge(s_ready, n * 4)
                        nc.scalar.activation(cxT_s[0][:, k, :], TR[:, k, :], ACT.Copy).then_inc(cxT_hi, 1)
                def context_hi():
                    act.wait_ge(cx_loaded, n * 16 + 16)
                    act.wait_ge(hq_ready, n * 2)
                    nc.scalar.activation(cx_s[0][:, :, :], cx[:, :, :], ACT.Copy).then_inc(cx_hi, 1)

                if m is not None:
                    for k in range(KT):
                        act.wait_ge(hq_ready, m * 2 + (k + 1))
                        act.wait_ge(x1_ready, m * 4)
                        nc.scalar.activation(hq_s[0][:, k, :], HQ[:, k, :], ACT.Copy).then_inc(hq_hi, 1)
                        act.wait_ge(prod_done, m * 2 + (k + 1))
                        nc.scalar.activation(prod_s[0][:, k, :], prod[:, k, :], ACT.Copy).then_inc(prod_hi, 1)
                if n is not None:
                    context_hi()
                    for t in range(TT):
                        act.wait_ge(nmax_done, n * 4 + (t + 1))
                        act.wait_ge(pT_ready, n * 4)
                        nc.scalar.activation(prob[:, t, :], S[:, t % 2, :], ACT.Exp, bias=nrowmax[:, t:t + 1],
                                             accum_out=rowsum[:, t:t + 1]).then_inc(exp_done, 1)
                    act.wait_ge(ngmax_done, n + 1)
                    act.wait_ge(hc_ready, n)
                    nc.scalar.activation(bexp[:, :], mx[:, :], ACT.Exp, bias=ngmax[:, 0:1]).then_inc(bexp_done, 1)
                    act.wait_ge(wmix_done, n + 1)
                    act.wait_ge(x1_ready, n * 4)
                    nc.scalar.activation(w_mix_s[0][:, :, :], w_mix[:, :, :], ACT.Copy).then_inc(wmix_hi, 1)
                    for t in range(TT):
                        act.wait_ge(pT_ready, n * 4 + (t + 1))
                        act.wait_ge(hq_ready, n * 2)
                        nc.scalar.activation(probT_s[0][:, :, t * P:(t + 1) * P],
                                             TR[:, t % 2, :].rearrange("p (j i) -> p j i", i=P), ACT.Copy).then_inc(pT_hi, 1)
                if m is not None:
                    for k in range(KT):
                        act.wait_ge(hT_ready, m * 2 + (k + 1))
                        nc.scalar.activation(hT_all[:, bass.ds(m, 1), k, :], TR[:, k, :].unsqueeze(1), ACT.Identity,
                                             scale=columns[:, COL_G + k:COL_G + k + 1],
                                             bias=columns[:, COL_B + k:COL_B + k + 1]).then_inc(hT_done, 1)

            steps(nc.scalar, step)
            act.wait_ge(qkv_loaded, 64)

        @block.vector
        def _(dve):
            def stats(q):
                dve.wait_ge(x_loaded, q * 16 + 16)
                for t in range(TT):
                    ins = nc.vector.bn_stats(bn[:, t, :], xr[:, t, :])
                ins.then_inc(enc_stats, 1)
                dve.wait_ge(enc_stats, q + 1)

            def variance(q):
                for t in range(TT):
                    ins = nc.vector.bn_aggr(mv[:, t, :], bn[:, t, :])
                ins.then_inc(enc_mv, 1)
                dve.wait_ge(enc_mv, q + 1)
                dve.wait_ge(enc_rstd, q)
                nc.vector.tensor_scalar_add(veps[:, :], mv[:, :, 1], EPS).then_inc(enc_var, 1)

            def normalise(q):
                dve.wait_ge(enc_rstd, q + 1)
                dve.wait_ge(hc_ready, q)
                dve.wait_ge(encT_ready, q * 2)
                for t in range(TT):
                    ins = nc.vector.tensor_scalar(enc[:, t, :], xr[:, t, :], mv[:, t, 0:1], rstd[:, t:t + 1],
                                                  ALU.subtract, ALU.mult)
                ins.then_inc(enc_done, 1)

            def x1_tile(m, t, odd):
                dve.wait_ge(x1_ready, m * 4 + (t + 1))
                if t == 0:
                    dve.wait_ge(xb_done, m + 1)
                    dve.wait_ge(x1_stored, m * 16)
                    dve.wait_ge(h_done, m)
                nc.vector.tensor_tensor(x1[:, t, :], X[:, t % 2, 0:D], xb[odd][:, t, :], ALU.add).then_inc(x1_done, 1)

            def step(m, n, q, odd):
                even = 1 - odd
                if n is not None:
                    for k in range(KT):
                        dve.wait_ge(ep_copied, n * 2 + (k + 1))
                        dve.wait_ge(s_ready, n * 4)
                        nc.vector.tensor_copy(ep_s[0][:, k, :], ep[:, k, :]).then_inc(ep_hi, 1)
                        nc.vector.tensor_copy(enc_s[even][0][:, k, :], encT[even][:, k, :]).then_inc(enc_hi, 1)
                        dve.wait_ge(ep_hi, n * 2 + (k + 1))
                        nc.vector.tensor_tensor(ep_s[1][:, k, :], ep[:, k, :], ep_s[0][:, k, :].bitcast(f32),
                                                ALU.subtract).then_inc(ep_split, 1)
                        dve.wait_ge(enc_hi, n * 2 + (k + 1))
                        nc.vector.tensor_tensor(enc_s[even][1][:, k, :], encT[even][:, k, :], enc_s[even][0][:, k, :].bitcast(f32),
                                                ALU.subtract).then_inc(enc_split, 1)
                    for k in range(KT):
                        dve.wait_ge(cxT_hi, n * 2 + (k + 1))
                        nc.vector.tensor_tensor(cxT_s[1][:, k, :], TR[:, k, :], cxT_s[0][:, k, :].bitcast(f32),
                                                ALU.subtract).then_inc(cxT_split, 1)
                if m is not None:
                    for k in range(KT):
                        dve.wait_ge(prod_split, m * 2)
                        dve.wait_ge(hq_hi, m * 2 + (k + 1))
                        nc.vector.tensor_tensor(prod[:, k, :], HQ[:, k, :], encT[odd][:, k, :], ALU.mult).then_inc(prod_done, 1)
                        nc.vector.tensor_tensor(hq_s[1][:, k, :], HQ[:, k, :], hq_s[0][:, k, :].bitcast(f32),
                                                ALU.subtract).then_inc(hq_split, 1)
                if n is not None:
                    for t in range(TT + 1):
                        if t < TT:
                            dve.wait_ge(s_ready, n * 4 + (t + 1))
                            nc.vector.reduce_max(rowmax[:, t:t + 1], S[:, t % 2, :], AX.X).then_inc(max_done, 1)
                            dve.wait_ge(max_done, n * 4 + (t + 1))
                            nc.vector.tensor_scalar(nrowmax[:, t:t + 1], rowmax[:, t:t + 1], -1.0, None, ALU.mult).then_inc(nmax_done, 1)
                        if t:
                            u = t - 1
                            dve.wait_ge(exp_done, n * 4 + (u + 1))
                            nc.vector.reciprocal(rinv[:, u:u + 1], rowsum[:, u:u + 1]).then_inc(rinv_done, 1)
                            dve.wait_ge(rinv_done, n * 4 + (u + 1))
                            nc.vector.tensor_scalar(prob[:, u, :], prob[:, u, :], rinv[:, u:u + 1], None, ALU.mult).then_inc(prob_done, 1)
                if q is not None:
                    stats(q)
                if m is not None:
                    x1_tile(m, 0, odd)
                if q is not None:
                    variance(q)
                if n is not None:
                    dve.wait_ge(r_ready, n + 1)
                    dve.wait_ge(bexp_done, n)
                    nc.vector.scalar_tensor_tensor(out=mx[:, :], in0=BATT[:, 0:TT], scalar=bsim[:, 0:1], in1=rowmax[:, :],
                                                   op0=ALU.add, op1=ALU.add).then_inc(mx_done, 1)
                    dve.wait_ge(mx_done, n + 1)
                    nc.vector.reduce_max(mcol[:, :], mx[:, :], AX.X).then_inc(mcol_done, 1)
                if m is not None:
                    x1_tile(m, 1, odd)
                if n is not None:
                    dve.wait_ge(mcolT_ready, n + 1)
                    nc.vector.reduce_max(gmax[:, :], BATT[0:1, 8:8 + P], AX.X).then_inc(gmax_done, 1)
                if m is not None:
                    x1_tile(m, 2, odd)
                if n is not None:
                    dve.wait_ge(gmax_spread, n + 1)
                    nc.vector.tensor_scalar(ngmax[:, :], BATT[:, 144:145], -1.0, None, ALU.mult).then_inc(ngmax_done, 1)
                if m is not None:
                    x1_tile(m, 3, odd)
                    dve.wait_ge(x1_done, m * 4 + 4)
                    for t in range(TT):
                        ins = nc.vector.bn_stats(bn1[:, t, :], x1[:, t, :])
                    ins.then_inc(x1_stats, 1)
                    dve.wait_ge(x1_stats, m + 1)
                if n is not None:
                    dve.wait_ge(hc_ready, n + 1)
                    nc.vector.reciprocal(binv[:, :], BATT[:, 152:153]).then_inc(binv_done, 1)
                if m is not None:
                    for t in range(TT):
                        ins = nc.vector.bn_aggr(mv1[:, t, :], bn1[:, t, :])
                    ins.then_inc(x1_mv, 1)
                    dve.wait_ge(x1_mv, m + 1)
                    nc.vector.tensor_scalar(veps1[:, :], mv1[:, :, 1], 1.0 + EPS, EPS * EPS, ALU.mult, ALU.add).then_inc(x1_var, 1)
                if n is not None:
                    dve.wait_ge(binv_done, n + 1)
                    nc.vector.tensor_scalar(hc[:, :], BATT[:, 148:150], binv[:, 0:1], None, ALU.mult).then_inc(hc_done, 1)
                    dve.wait_ge(hc_done, n + 1)
                    dve.wait_ge(w_loaded, 48)
                    dve.wait_ge(wmix_split, n)
                    for k in range(KT):
                        ins = nc.vector.scalar_tensor_tensor(out=w_mix[:, k, :], in0=w_bar[:, k, :], scalar=hc[:, k:k + 1],
                                                             in1=w_enc[:, k, :], op0=ALU.mult, op1=ALU.add)
                    ins.then_inc(wmix_done, 1)
                    dve.wait_ge(wmix_hi, n + 1)
                    nc.vector.tensor_tensor(w_mix_s[1][:, :, :], w_mix[:, :, :], w_mix_s[0][:, :, :].bitcast(f32),
                                            ALU.subtract).then_inc(wmix_split, 1)
                    for t in range(TT):
                        dve.wait_ge(pT_hi, n * 4 + (t + 1))
                        here = slice(t * P, (t + 1) * P)
                        nc.vector.tensor_tensor(probT_s[1][:, :, here], TR[:, t % 2, :].rearrange("p (j i) -> p j i", i=P),
                                                probT_s[0][:, :, here].bitcast(f32), ALU.subtract).then_inc(pT_split, 1)
                if m is not None:
                    dve.wait_ge(x1_rstd, m + 1)
                    dve.wait_ge(hT_ready, m * 2)
                    for t in range(TT):
                        ins = nc.vector.tensor_scalar(h[:, t, :], x1[:, t, :], mv1[:, t, 0:1], rstd1[:, t:t + 1],
                                                      ALU.subtract, ALU.mult)
                    ins.then_inc(h_done, 1)
                if q is not None:
                    normalise(q)

            dve.wait_ge(bias_loaded, 32)
            stats(0)
            variance(0)
            dve.wait_ge(wmid_hi, 1)
            nc.vector.tensor_tensor(w_mid_s[1][:, :, :], w_stage, w_mid_s[0][:, :, :].bitcast(f32),
                                    ALU.subtract).then_inc(wmid_split, 1)
            normalise(0)
            steps(nc.vector, step)

        @block.tensor
        def _(pe):
            THREE = ((0, 0), (1, 0), (0, 1))

            def transposes(bank, sources):
                for i, src in enumerate(sources):
                    ins = nc.tensor.transpose(TR[:, bank, i * P:(i + 1) * P], src, ident[:, :])
                return ins

            def products(out, ks, lhs, rhs):
                steps = [(a, b, k) for a, b in THREE for k in ks]
                for i, (a, b, k) in enumerate(steps):
                    ins = nc.tensor.matmul(out, lhs(a, k), rhs(b, k), start=i == 0, stop=i == len(steps) - 1)
                return ins

            def features(m, t, odd):
                pe.wait_ge(x1_done, m * 4 + max(t - 1, 0))
                here = slice(t * P, (t + 1) * P)
                groups = ([(enc_s[odd], k, w_mix_s, k) for k in range(KT)] + [(hq_s, k, w_mid_s, k) for k in range(KT)]
                          + [(prod_s, k, w_mid_s, KT + k) for k in range(KT)])
                products(X[:, t % 2, 0:D], range(3 * KT),
                         lambda a, i: groups[i][0][a][:, groups[i][1], here],
                         lambda b, i: groups[i][2][b][:, groups[i][3], :]).then_inc(x1_ready, 1)

            def step(m, n, q, odd):
                even = 1 - odd
                if n is not None:
                    pe.wait_ge(enc_done, n + 1)
                    pe.wait_ge(hT_done, n * 2 - 2 if m is not None else 0)
                    pe.wait_ge(pT_split, n * 4)
                    for k in range(KT):
                        transposes(k, [enc[:, t, k * P:(k + 1) * P] for t in range(TT)]).then_inc(encT_ready, 1)
                    pe.wait_ge(cx_loaded, n * 16 + 16)
                    for k in range(KT):
                        pe.wait_ge(encT_copied, n * 2 + (k + 1))
                        pe.wait_ge(ep_copied, n * 2 + (k + 1))
                        transposes(k, [cx[:, t, k * P:(k + 1) * P] for t in range(TT)]).then_inc(cxT_ready, 1)
                if m is not None:
                    pe.wait_ge(cx_split, m + 1)
                    pe.wait_ge(pT_split, m * 4 + 4)
                    pe.wait_ge(hq_split, m * 2)
                    for k in range(KT):
                        cols = slice(k * P, (k + 1) * P)
                        products(HQ[:, k, :], range(TT), lambda a, j: cx_s[a][:, j, cols],
                                 lambda b, j: probT_s[b][:, j, :]).then_inc(hq_ready, 1)
                if n is not None:
                    pe.wait_ge(ep_split, n * 2 + 2)
                    pe.wait_ge(cxT_split, n * 2 + 2)
                    pe.wait_ge(hc_done, n)
                    for t in range(TT):
                        if t < 2:
                            pe.wait_ge(exp_done, n * 4)
                        else:
                            pe.wait_ge(exp_done, n * 4 + (t - 1))
                        here = slice(t * P, (t + 1) * P)
                        products(S[:, t % 2, :], range(KT), lambda a, k: ep_s[a][:, k, here],
                                 lambda b, k: cxT_s[b][:, k, :]).then_inc(s_ready, 1)
                if m is not None:
                    pe.wait_ge(enc_split, m * 2 + 2)
                    pe.wait_ge(hq_split, m * 2 + 2)
                    pe.wait_ge(prod_split, m * 2 + 2)
                    pe.wait_ge(wmix_split, m + 1)
                    pe.wait_ge(wmid_split, 1)
                    features(m, 0, odd)
                if n is not None:
                    pe.wait_ge(exp_done, n * 4 + 3)
                    for t in range(TT):
                        for k in range(KT):
                            ins = nc.tensor.matmul(BATT[:, t:t + 1], encT[even][:, k, t * P:(t + 1) * P],
                                                   columns[:, COL_WSIM + k:COL_WSIM + k + 1], start=k == 0, stop=k == KT - 1)
                    ins.then_inc(r_ready, 1)
                if m is not None:
                    features(m, 1, odd)
                if n is not None:
                    pe.wait_ge(mcol_done, n + 1)
                    nc.tensor.transpose(BATT[0:1, 8:8 + P], mcol[:, :], ident[:, :]).then_inc(mcolT_ready, 1)
                if m is not None:
                    features(m, 2, odd)
                if n is not None:
                    pe.wait_ge(gmax_done, n + 1)
                    nc.tensor.matmul(BATT[:, 144:145], ones[0:1, :], gmax[:, :], start=True, stop=True).then_inc(gmax_spread, 1)
                if m is not None:
                    features(m, 3, odd)
                if n is not None:
                    pe.wait_ge(bexp_done, n + 1)
                    for k in range(KT):
                        for t in range(TT):
                            nc.tensor.matmul(BATT[:, 148 + k:149 + k], enc[:, t, k * P:(k + 1) * P], bexp[:, t:t + 1],
                                             start=t == 0, stop=t == TT - 1)
                    for t in range(TT):
                        ins = nc.tensor.matmul(BATT[:, 152:153], ones[:, :], bexp[:, t:t + 1], start=t == 0, stop=t == TT - 1)
                    ins.then_inc(hc_ready, 1)
                    for t in range(TT):
                        pe.wait_ge(prob_done, n * 4 + (t + 1))
                        if t >= 2:
                            pe.wait_ge(pT_split, n * 4 + (t - 1))
                        else:
                            pe.wait_ge(cxT_split, n * 2 + (t + 1))
                        transposes(t % 2, [prob[:, t, j * P:(j + 1) * P] for j in range(TT)]).then_inc(pT_ready, 1)
                if m is not None:
                    pe.wait_ge(h_done, m + 1)
                    pe.wait_ge(pT_split, m * 4 + 8 if n is not None else m * 4 + 4)
                    for k in range(KT):
                        transposes(k, [h[:, t, k * P:(k + 1) * P] for t in range(TT)]).then_inc(hT_ready, 1)

            steps(nc.tensor, step)



def self_attention_phase(nc, T):
    ident, ident_b, mask, ones = T["ident"], T["ident_b"], T["mask"], T["ones"]
    neg_half, columns, qk_scale = T["neg_half"], T["columns"], T["qk_scale"]
    hT_all, gate_all, self_raw = T["hT_all"], T["gate_all"], T["self_raw"]
    PC = 2 * DH
    U = 2 * TT
    BLOCKS = 13
    CU, CO, CT = PAIRS * U, PAIRS * 2, PAIRS * TT
    order = [(hh, t) for hh in range(2) for t in reversed(range(TT))]

    ctx = ExitStack()
    with ctx:
        sb = lambda name, shape, dt=f32: ctx.enter_context(nc.sbuf_tensor(name, shape, dt))
        split = lambda name, shape: (sb(name + "_hi", shape, f32r), sb(name + "_lo", shape, f32r))
        sem = lambda name: ctx.enter_context(nc.semaphore(name))
        with nc.sbuf_tensor("spare", [P, PAIRS, ROWS], f32) as spare:
            pass
        attnT_s = split("attnT_s", [P, PAIRS, ROWS])
        hT_now = spare[:, 2:2 + KT, :]
        wqkv_s = split("wqkv_s", [P, KT, PAIRS, 3, PC])
        wo_s = split("wo_s", [P, PAIRS, D])
        h_s = split("hT_s", [P, KT, ROWS])
        qT_s = [split(f"qT_s{i}", [P, ROWS]) for i in range(2)]
        kT_s = [split(f"kT_s{i}", [P, ROWS]) for i in range(2)]
        v_s = [split(f"v_s{i}", [P, TT, PC]) for i in range(2)]
        qkv = sb("qkv", [P, TT, 3, PC])
        qk_sq = sb("qk_sq", [P, 2, 2, PC])
        prob = sb("prob_b", [P, 2, ROWS])
        probT_s = [split(f"pT_s{i}", [P, BLOCKS, P]) for i in range(2)]
        scaled = sb("scaled", [P, ROWS])
        ssq = sb("ssq", [P, TT, 2, 2])
        rnorm = [sb(f"rnorm{i}", [P, TT, 2, 2]) for i in range(2)]
        rowmax, nrowmax, rowsum, rinv = (sb(n, [P, U]) for n in ("rowmax_b", "nrowmax_b", "rowsum_b", "rinv_b"))
        bn, mv = sb("bn_b", [P, TT, 6]), sb("mv_b", [P, TT, 2])
        veps, rstd = sb("veps_b", [P, TT]), sb("rstd_b", [P, TT])
        g_max, g_sum, g_inv = (sb(n, [P, TT]) for n in ("g_max", "g_sum", "g_inv"))
        g_exp = sb("g_exp", [P, TT, E])

        A = ctx.enter_context(nc.psum_tensor("psum_project", [P, 3, 512], f32))
        S = ctx.enter_context(nc.psum_tensor("psum_logits", [P, 2, 512], f32))
        PT = ctx.enter_context(nc.psum_tensor("psum_probT", [P, 2, 512], f32))
        O = ctx.enter_context(nc.psum_tensor("psum_attn", [P, 512], f32))

        (w_hi, w_split, wo_hi, wo_split, h_hi, h_split) = map(
            sem, ("sw_hi", "sw_split", "wo_hi", "wo_split", "bh_hi", "bh_split"))
        (proj_ready, qk_copied, v_hi, v_split, sq_done, ssq_sum, ssq_done, norm_pow, k_done) = map(
            sem, ("proj_ready", "qk_copied", "v_hi", "v_split", "sq_done", "ssq_sum", "ssq_done", "norm_pow", "k_done"))
        (qT_ready, qT_hi, qT_split, kT_ready, kT_hi, kT_split) = map(
            sem, ("qT_ready", "qT_hi", "qT_split", "kT_ready", "kT_hi", "kT_split"))
        (s_ready, max_done, nmax_done, exp_done, pT_ready, pT_hi, pT_split) = map(
            sem, ("bs_ready", "bmax_done", "bnmax_done", "bexp_done_b", "bpT_ready", "bpT_hi", "bpT_split"))
        (rinv_done, rinv_wide, rinv_kept, o_ready, o_scaled, o_hi, o_split, wo_ready, wo_copied) = map(
            sem, ("brinv_done", "rinv_wide", "rinv_kept", "o_ready", "o_scaled", "o_hi", "o_split", "wo_ready", "wo_copied"))
        (n_stats, n_mv, n_var, n_rstd, n_done, n_ready, hT_done, hT_kept) = map(
            sem, ("n_stats", "n_mv", "n_var", "n_rstd", "n_done", "n_ready", "bhT_done", "hT_kept"))
        (g_ready, g_max_done, g_sub, g_exp_done, g_sum_done, g_inv_done, g_done) = map(
            sem, ("g_ready", "g_max_done", "g_sub", "g_exp_done", "g_sum_done", "g_inv_done", "g_done"))
        block = ctx.enter_context(nc.Block())

        def pairs(engine, begin, pair, finish, after):
            def chunk(c, more):
                g0 = c * PAIRS if isinstance(c, int) else engine.snap(c * PAIRS)
                pair(c, g0, 0, 0, True, False, True)
                with engine.Fori(0, (PAIRS - 2) // 2) as i:
                    for step in (1, 2):
                        p = engine.snap(i * 2 + step)
                        pair(c, engine.snap(g0 + p), p, step % 2, False, False, True)
                g7 = g0 + (PAIRS - 1) if isinstance(c, int) else engine.snap(g0 + (PAIRS - 1))
                pair(c, g7, PAIRS - 1, 1, False, True, more)
                finish(c, more)

            begin()
            chunk(0, True)
            with engine.Fori(1, CHUNKS - 1) as c:
                chunk(c, True)
            chunk(CHUNKS - 1, False)
            after(CHUNKS - 1)

        def plus(engine, g, n):
            return g + n if isinstance(g, int) else engine.snap(g + n)

        def past(engine, semaphore, count):
            if not (isinstance(count, int) and count <= 0):
                engine.wait_ge(semaphore, count)

        @block.gpsimd
        def _(pool):
            def powers(g, t, odd, heads_split):
                if t == 0:
                    past(pool, exp_done, g * U - U)
                    past(pool, o_split, heads_split)
                pool.wait_ge(ssq_done, g * TT + (t + 1))
                nc.gpsimd.tensor_tensor(rnorm[odd][:, t, :, :], ssq[:, t, :, :],
                                        neg_half[:, 0:4].rearrange("p (a h) -> p a h", h=2), ALU.pow).then_inc(norm_pow, 1)

            def v_low(g, odd):
                pool.wait_ge(v_hi, g + 1)
                nc.gpsimd.tensor_tensor(v_s[odd][1][:, :, :], qkv[:, :, 2, :], v_s[odd][0][:, :, :].bitcast(f32),
                                        ALU.subtract).then_inc(v_split, 1)

            def attn_low(g, p, hh):
                pool.wait_ge(o_hi, g * 2 + (hh + 1))
                rows = slice(hh * DH, (hh + 1) * DH)
                nc.gpsimd.tensor_tensor(attnT_s[1][rows, bass.ds(p, 1), :], scaled[rows, :].unsqueeze(1),
                                        attnT_s[0][rows, bass.ds(p, 1), :].bitcast(f32), ALU.subtract).then_inc(o_split, 1)

            def begin():
                for t in range(TT):
                    powers(0, t, 0, 0)
                v_low(0, 0)

            def pair(c, g, p, odd, start, fresh, more):
                nxt = plus(pool, g, 1)
                if fresh:
                    pool.wait_ge(o_split, g * 2 - 1)
                    attn_low(g - 1, p - 1, 1)
                if more:
                    for t in range(TT):
                        powers(nxt, t, 1 - odd, g * 2 if start or fresh else g * 2 - 1)
                    v_low(nxt, 1 - odd)
                    pool.wait_ge(v_split, g + 2)
                if not start and not fresh:
                    attn_low(g - 1, p - 1, 1)
                past(pool, o_split, g * 2)
                attn_low(g, p, 0)

            def finish(c, more):
                pool.wait_ge(o_split, c * CO + (CO - 1))
                attn_low(c * PAIRS + (PAIRS - 1), PAIRS - 1, 1)
                pool.wait_ge(o_split, c * CO + CO)
                pool.wait_ge(n_var, c + 1)
                nc.gpsimd.tensor_tensor(rstd[:, :], veps[:, :], neg_half[:, 0:TT], ALU.pow).then_inc(n_rstd, 1)

            pairs(nc.gpsimd, begin, pair, finish, lambda c: None)

        @block.scalar
        def _(act):
            def split_h(c):
                past(act, proj_ready, c * CT)
                nc.scalar.activation(h_s[0][:, :, :], hT_all[:, bass.ds(c, 1), :, :].rearrange("p c k n -> p (c k) n"),
                                     ACT.Copy).then_inc(h_hi, 1)

            def from_projection(g, t):
                if t == 0:
                    past(act, qT_ready, g)
                    past(act, kT_ready, g)
                    past(act, v_split, g)
                act.wait_ge(proj_ready, g * TT + (t + 1))
                nc.scalar.activation(qkv[:, t, :, :], A[:, t % 3, 0:3 * PC].rearrange("p (a n) -> p a n", a=3), ACT.Copy).then_inc(qk_copied, 1)
                past(act, ssq_sum, g * TT + (t - 1))
                nc.scalar.activation(qk_sq[:, t % 2, :, :], A[:, t % 3, 0:2 * PC].rearrange("p (a n) -> p a n", a=2),
                                     ACT.Square).then_inc(sq_done, 1)

            def v_high(g, odd):
                past(act, o_ready, g * 2 - 2)
                act.wait_ge(qk_copied, g * TT + TT)
                nc.scalar.activation(v_s[odd][0][:, :, :], qkv[:, :, 2, :], ACT.Copy).then_inc(v_hi, 1)

            def q_high(g, p, odd):
                act.wait_ge(qT_ready, g + 1)
                past(act, s_ready, g * U - U)
                nc.scalar.activation(qT_s[odd][0][:, :], A[:, 1, :], ACT.Copy, scale=qk_scale[:, bass.ds(p, 1)]).then_inc(qT_hi, 1)

            def k_high(g, odd):
                act.wait_ge(kT_ready, g + 1)
                nc.scalar.activation(kT_s[odd][0][:, :], A[:, 2, :], ACT.Copy).then_inc(kT_hi, 1)

            def exponentials(g, u, odd):
                hh, t = order[u]
                past(act, pT_ready, g * U + (u - 1))
                act.wait_ge(nmax_done, g * U + (u + 1))
                n = (t + 1) * P
                nc.scalar.activation(prob[:, u % 2, 0:n], S[:, u % 2, 0:n], ACT.Exp, bias=nrowmax[:, u:u + 1],
                                     scale=rnorm[odd][:, t, 0, hh:hh + 1], accum_out=rowsum[:, u:u + 1]).then_inc(exp_done, 1)

            def probT_high(g, u):
                hh, t = order[u]
                if t == TT - 1:
                    past(act, o_ready, g * 2 + (hh - 1))
                act.wait_ge(pT_ready, g * U + (u + 1))
                nc.scalar.activation(probT_s[hh][0][:, t:4 * t + 1:3, :], PT[:, u % 2, 0:(t + 1) * P]
                                     .rearrange("p (j i) -> p j i", i=P), ACT.Copy).then_inc(pT_hi, 1)

            def keep_inverses(g, hh):
                past(act, o_split, g * 2 + (hh - 1))
                act.wait_ge(rinv_wide, g * 2 + (hh + 1))
                rows = slice(hh * DH, (hh + 1) * DH)
                nc.scalar.activation(scaled[rows, :], A[rows, 0, :], ACT.Copy).then_inc(rinv_kept, 1)

            def attn_high(c, g, p, hh):
                past(act, wo_ready, c * TT)
                act.wait_ge(o_scaled, g * 2 + (hh + 1))
                rows = slice(hh * DH, (hh + 1) * DH)
                nc.scalar.activation(attnT_s[0][rows, bass.ds(p, 1), :], scaled[rows, :].unsqueeze(1), ACT.Copy).then_inc(o_hi, 1)

            def output_transposed(c, k):
                act.wait_ge(n_ready, c * KT + (k + 1))
                nc.scalar.activation(hT_now[:, k, :], O[:, :], ACT.Identity, scale=columns[:, COL_G + k:COL_G + k + 1],
                                     bias=columns[:, COL_B + k:COL_B + k + 1]).then_inc(hT_done, 1)

            def gate_exponentials(c):
                act.wait_ge(g_sub, c + 1)
                nc.scalar.activation(g_exp[:, :, :], g_exp[:, :, :], ACT.Exp).then_inc(g_exp_done, 1)

            def begin():
                for p in range(PAIRS):
                    for i in range(3):
                        ins = nc.scalar.activation(wqkv_s[0][:, :, p, i, :],
                                                   self_raw[:, i * KT:(i + 1) * KT, p * PC:(p + 1) * PC], ACT.Copy)
                    ins.then_inc(w_hi, 1)
                    if p == 0:
                        split_h(0)
                for t in range(TT):
                    from_projection(0, t)
                v_high(0, 0)
                q_high(0, 0, 0)
                nc.scalar.activation(wo_s[0][:, :, :], wo_raw, ACT.Copy).then_inc(wo_hi, 1)
                k_high(0, 0)
                exponentials(0, 0, 0)

            wo_raw = self_raw[:, 3 * KT:, :].rearrange("p a b -> p (a b)").rearrange("p (k d) -> p k d", d=D)

            def pair(c, g, p, odd, start, fresh, more):
                nxt, even, late = plus(act, g, 1), 1 - odd, int(fresh)
                if fresh and more:
                    split_h(plus(act, c, 1))
                for u in range(U):
                    if u < U - 1:
                        exponentials(g, u + 1, odd)
                    elif more and not fresh:
                        exponentials(nxt, 0, even)
                    probT_high(g, u)
                    if more:
                        if u == late:
                            from_projection(nxt, 0)
                            from_projection(nxt, 1)
                        if u == 1 + late:
                            from_projection(nxt, 2)
                        if u == 2 + late:
                            from_projection(nxt, 3)
                        if u == 5 + late:
                            q_high(nxt, 0 if fresh else p + 1, even)
                            k_high(nxt, even)
                    if u == 0 and fresh or u == 3 and not start and not fresh:
                        keep_inverses(g - 1, 1)
                    if u == 1 and fresh or u == 5 and not start and not fresh:
                        attn_high(c, g - 1, p - 1, 1)
                    if u == 4 and more:
                        v_high(nxt, even)
                    if start and not (isinstance(c, int) and c == 0):
                        if u < KT:
                            output_transposed(c - 1, u)
                        if u == 3:
                            gate_exponentials(c - 1)
                    if u == 5:
                        keep_inverses(g, 0)
                    if u == 7:
                        attn_high(c, g, p, 0)

            def finish(c, more):
                g7, nxt = plus(act, c * PAIRS, PAIRS - 1), plus(act, c * PAIRS, PAIRS)
                keep_inverses(g7, 1)
                attn_high(c, g7, PAIRS - 1, 1)
                for t in range(TT):
                    act.wait_ge(wo_ready, c * TT + (t + 1))
                    nc.scalar.activation(spare[:, 0:2, t * P:(t + 1) * P], S[:, t % 2, 0:D].rearrange("p (k n) -> p k n", k=2),
                                         ACT.Copy).then_inc(wo_copied, 1)
                if more:
                    exponentials(nxt, 0, 0)

            def after(c):
                for k in range(KT):
                    output_transposed(c, k)
                gate_exponentials(c)

            pairs(nc.scalar, begin, pair, finish, after)

        @block.vector
        def _(dve):
            wo_raw = self_raw[:, 3 * KT:, :].rearrange("p a b -> p (a b)").rearrange("p (k d) -> p k d", d=D)

            def low(out, whole, high):
                return nc.vector.tensor_tensor(out, whole, high.bitcast(f32), ALU.subtract)

            def split_h(c):
                dve.wait_ge(h_hi, c + 1)
                low(h_s[1][:, :, :], hT_all[:, bass.ds(c, 1), :, :].rearrange("p c k n -> p (c k) n"), h_s[0][:, :, :]).then_inc(h_split, 1)

            def sum_squares(g, t):
                dve.wait_ge(sq_done, g * TT + (t + 1))
                nc.vector.reduce_sum(ssq[:, t, :, :], qk_sq[:, t % 2, :, :].rearrange("p a (h d) -> p a h d", d=DH),
                                     AX.X).then_inc(ssq_sum, 1)
                dve.wait_ge(ssq_sum, g * TT + (t + 1))
                nc.vector.tensor_scalar_add(ssq[:, t, :, :], ssq[:, t, :, :], 1e-12).then_inc(ssq_done, 1)

            def key_norms(g, t, odd):
                dve.wait_ge(norm_pow, g * TT + (t + 1))
                here = qkv[:, t, 1, :].rearrange("p (h d) -> p h d", d=DH)
                nc.vector.tensor_tensor(here, here, rnorm[odd][:, t, 1, :].unsqueeze(2).to_broadcast([P, 2, DH]), ALU.mult).then_inc(k_done, 1)

            def q_low(g, p, odd):
                dve.wait_ge(qT_hi, g + 1)
                nc.vector.scalar_tensor_tensor(out=qT_s[odd][1][:, :], in0=A[:, 1, :], scalar=qk_scale[:, bass.ds(p, 1)],
                                               in1=qT_s[odd][0][:, :].bitcast(f32), op0=ALU.mult, op1=ALU.subtract).then_inc(qT_split, 1)

            def k_low(g, odd):
                dve.wait_ge(kT_hi, g + 1)
                low(kT_s[odd][1][:, :], A[:, 2, :], kT_s[odd][0][:, :]).then_inc(kT_split, 1)

            def maximum(g, u, odd):
                hh, t = order[u]
                dve.wait_ge(s_ready, g * U + (u + 1))
                nc.vector.reduce_max(rowmax[:, u:u + 1], S[:, u % 2, 0:(t + 1) * P], AX.X).then_inc(max_done, 1)
                dve.wait_ge(max_done, g * U + (u + 1))
                nc.vector.scalar_tensor_tensor(out=nrowmax[:, u:u + 1], in0=rowmax[:, u:u + 1], scalar=-1.0,
                                               in1=rnorm[odd][:, t, 0, hh:hh + 1], op0=ALU.mult, op1=ALU.mult).then_inc(nmax_done, 1)

            def probT_low(g, u):
                hh, t = order[u]
                dve.wait_ge(pT_hi, g * U + (u + 1))
                low(probT_s[hh][1][:, t:4 * t + 1:3, :], PT[:, u % 2, 0:(t + 1) * P].rearrange("p (j i) -> p j i", i=P),
                    probT_s[hh][0][:, t:4 * t + 1:3, :]).then_inc(pT_split, 1)

            def inverse(g, hh):
                dve.wait_ge(exp_done, g * U + (hh + 1) * TT)
                half = slice(hh * TT, (hh + 1) * TT)
                nc.vector.reciprocal(rinv[:, half], rowsum[:, half]).then_inc(rinv_done, 1)

            def scale_attention(g, hh):
                rows = slice(hh * DH, (hh + 1) * DH)
                dve.wait_ge(rinv_kept, g * 2 + (hh + 1))
                dve.wait_ge(o_ready, g * 2 + (hh + 1))
                nc.vector.tensor_tensor(scaled[rows, :], O[rows, :], scaled[rows, :], ALU.mult).then_inc(o_scaled, 1)

            def keep_output(c):
                dve.wait_ge(hT_done, c * KT + KT)
                nc.vector.tensor_copy(hT_all[:, bass.ds(c, 1), :, :].rearrange("p c k n -> p (c k) n"), hT_now).then_inc(hT_kept, 1)

            def gate_logits(c):
                dve.wait_ge(g_ready, c + 1)
                logits = O[:, 0:TT * E].rearrange("p (t e) -> p t e", e=E)
                nc.vector.reduce_max(g_max[:, :], logits, AX.X).then_inc(g_max_done, 1)
                dve.wait_ge(g_max_done, c + 1)
                nc.vector.tensor_tensor(g_exp[:, :, :], logits, g_max[:, :].unsqueeze(2).to_broadcast([P, TT, E]), ALU.subtract).then_inc(g_sub, 1)

            def gate_shares(c):
                dve.wait_ge(g_exp_done, c + 1)
                nc.vector.reduce_sum(g_sum[:, :], g_exp[:, :, :], AX.X).then_inc(g_sum_done, 1)
                dve.wait_ge(g_sum_done, c + 1)
                nc.vector.reciprocal(g_inv[:, :], g_sum[:, :]).then_inc(g_inv_done, 1)
                dve.wait_ge(g_inv_done, c + 1)
                nc.vector.tensor_tensor(gate_all[:, bass.ds(c, 1), :, :].rearrange("p c t e -> p (c t) e"), g_exp[:, :, :],
                                        g_inv[:, :].unsqueeze(2).to_broadcast([P, TT, E]), ALU.mult).then_inc(g_done, 1)

            def begin():
                for p in range(PAIRS):
                    dve.wait_ge(w_hi, p + 1)
                    for i in range(3):
                        ins = low(wqkv_s[1][:, :, p, i, :], self_raw[:, i * KT:(i + 1) * KT, p * PC:(p + 1) * PC],
                                  wqkv_s[0][:, :, p, i, :])
                    ins.then_inc(w_split, 1)
                    if p == 0:
                        split_h(0)
                for t in range(TT):
                    sum_squares(0, t)
                q_low(0, 0, 0)
                for t in range(TT):
                    key_norms(0, t, 0)
                dve.wait_ge(wo_hi, 1)
                low(wo_s[1][:, :, :], wo_raw, wo_s[0][:, :, :]).then_inc(wo_split, 1)
                k_low(0, 0)
                maximum(0, 0, 0)
                maximum(0, 1, 0)

            def pair(c, g, p, odd, start, fresh, more):
                nxt, even, late = plus(dve, g, 1), 1 - odd, int(fresh)
                after_chunk = start and not (isinstance(c, int) and c == 0)
                if fresh and more:
                    split_h(plus(dve, c, 1))
                for u in range(U):
                    if u < U - 2:
                        maximum(g, u + 2, odd)
                    elif more and not fresh:
                        maximum(nxt, u + 2 - U, even)
                    if u % TT == TT - 1:
                        inverse(g, u // TT)
                    probT_low(g, u)
                    if more:
                        if u == late:
                            sum_squares(nxt, 0)
                            sum_squares(nxt, 1)
                        if u == 1 + late:
                            sum_squares(nxt, 2)
                        if u == 2 + late:
                            sum_squares(nxt, 3)
                            key_norms(nxt, 0, even)
                            key_norms(nxt, 1, even)
                        if u == 3 + late:
                            key_norms(nxt, 2, even)
                            key_norms(nxt, 3, even)
                        if u == 5 + late:
                            q_low(nxt, 0 if fresh else p + 1, even)
                            k_low(nxt, even)
                    if u == 1 and fresh or u == 4 and not start and not fresh:
                        scale_attention(g - 1, 1)
                    if after_chunk:
                        if u == 2:
                            keep_output(c - 1)
                        if u == 3:
                            gate_logits(c - 1)
                        if u == 4:
                            gate_shares(c - 1)
                    if u == 6:
                        scale_attention(g, 0)

            def finish(c, more):
                g7, nxt = plus(dve, c * PAIRS, PAIRS - 1), plus(dve, c * PAIRS, PAIRS)
                scale_attention(g7, 1)
                for t in range(TT):
                    dve.wait_ge(wo_copied, c * TT + (t + 1))
                    nc.vector.bn_stats(bn[:, t, :], S[:, t % 2, 0:D]).then_inc(n_stats, 1)
                if more:
                    dve.wait_ge(n_stats, c * TT + TT)
                    maximum(nxt, 0, 0)
                else:
                    dve.wait_ge(n_stats, c * TT + TT)
                for t in range(TT):
                    ins = nc.vector.bn_aggr(mv[:, t, :], bn[:, t, :])
                ins.then_inc(n_mv, 1)
                dve.wait_ge(n_mv, c + 1)
                nc.vector.tensor_scalar_add(veps[:, :], mv[:, :, 1], EPS).then_inc(n_var, 1)
                if more:
                    maximum(nxt, 1, 0)
                dve.wait_ge(n_rstd, c + 1)
                for t in range(TT):
                    here = spare[:, 0:2, t * P:(t + 1) * P]
                    ins = nc.vector.tensor_scalar(here, here, mv[:, t, 0:1], rstd[:, t:t + 1], ALU.subtract, ALU.mult)
                ins.then_inc(n_done, 1)

            def after(c):
                keep_output(c)
                gate_logits(c)
                gate_shares(c)

            pairs(nc.vector, begin, pair, finish, after)

        @block.tensor
        def _(pe):
            THREE = ((0, 0), (1, 0), (0, 1))

            def project(g, p, t, inverses_kept=0):
                bank = t % 3
                if t == 0:
                    past(pe, rinv_kept, inverses_kept)
                if t == 1:
                    past(pe, qT_split, g)
                if t == 2:
                    past(pe, kT_split, g)
                if t == 3:
                    pe.wait_ge(sq_done, g * TT + 1)
                steps = [(a, b, k) for a, b in THREE for k in range(KT)]
                for i, (a, b, k) in enumerate(steps):
                    ins = nc.tensor.matmul(A[:, bank, 0:3 * PC], h_s[a][:, k, t * P:(t + 1) * P],
                                           wqkv_s[b][:, k, bass.ds(p, 1), :, :].rearrange("p a b c -> p a (b c)"),
                                           start=i == 0, stop=i == len(steps) - 1)
                ins.then_inc(proj_ready, 1)

            def transpose_q(g):
                pe.wait_ge(qk_copied, g * TT + TT)
                pe.wait_ge(sq_done, g * TT + 2)
                for t in range(TT):
                    ins = nc.tensor.transpose(A[:, 1, t * P:(t + 1) * P], qkv[:, t, 0, :], ident[:, :])
                ins.then_inc(qT_ready, 1)

            def transpose_k(g):
                pe.wait_ge(sq_done, g * TT + 3)
                pe.wait_ge(k_done, g * TT + TT)
                for t in range(TT):
                    ins = nc.tensor.transpose(A[:, 2, t * P:(t + 1) * P], qkv[:, t, 1, :], ident[:, :])
                ins.then_inc(kT_ready, 1)

            def logits(g, u, odd):
                hh, t = order[u]
                if u == 0:
                    pe.wait_ge(qT_split, g + 1)
                    pe.wait_ge(kT_split, g + 1)
                past(pe, exp_done, g * U + (u - 1))
                rows = slice(hh * DH, (hh + 1) * DH)
                n = (t + 1) * P
                for i, (a, b) in enumerate(THREE):
                    nc.tensor.matmul(S[:, u % 2, 0:n], qT_s[odd][a][rows, t * P:(t + 1) * P], kT_s[odd][b][rows, 0:n],
                                     start=i == 0, stop=False, skip_group_check=True)
                nc.tensor.matmul(S[:, u % 2, t * P:n], ident_b[:, :], mask[:, :], start=False, stop=True,
                                 skip_group_check=True).then_inc(s_ready, 1)

            def transpose_probs(g, u):
                t = order[u][1]
                past(pe, pT_split, g * U + (u - 1))
                pe.wait_ge(exp_done, g * U + (u + 1))
                for j in range(t + 1):
                    ins = nc.tensor.transpose(PT[:, u % 2, j * P:(j + 1) * P], prob[:, u % 2, j * P:(j + 1) * P], ident[:, :])
                ins.then_inc(pT_ready, 1)

            def widen_inverses(g, hh, more, projected):
                past(pe, rinv_kept, g * 2 + hh)
                if more:
                    pe.wait_ge(sq_done, projected)
                pe.wait_ge(rinv_done, g * 2 + (hh + 1))
                for t in range(TT):
                    u = order.index((hh, t))
                    ins = nc.tensor.transpose(A[:, 0, t * P:(t + 1) * P], rinv[:, u:u + 1].to_broadcast([P, P]), ident[:, :])
                ins.then_inc(rinv_wide, 1)

            def attend(g, hh, odd, after_gates=None):
                past(pe, o_scaled, g * 2 + hh)
                if after_gates is not None:
                    pe.wait_ge(g_sub, after_gates)
                pe.wait_ge(v_split, g + 1)
                pe.wait_ge(pT_split, g * U + (hh + 1) * TT)
                steps = [(a, b, j) for j in range(TT) for a, b in THREE]
                for i, (a, b, j) in enumerate(steps):
                    probs = probT_s[hh][b][:, 4 * j:3 * j + TT, :].rearrange("p a b -> p (a b)")
                    ins = nc.tensor.matmul(O[:, j * P:ROWS], v_s[odd][a][:, j, :], probs,
                                           start=i == 0, stop=i == len(steps) - 1, skip_group_check=True)
                ins.then_inc(o_ready, 1)

            def output_transposes(c, k):
                if k == 0:
                    pe.wait_ge(o_scaled, c * CO + CO)
                    pe.wait_ge(n_done, c + 1)
                else:
                    pe.wait_ge(hT_done, c * KT + k)
                for t in range(TT):
                    ins = nc.tensor.transpose(O[:, t * P:(t + 1) * P], spare[:, k, t * P:(t + 1) * P], ident[:, :])
                ins.then_inc(n_ready, 1)

            def gates(c):
                pe.wait_ge(hT_done, c * KT + KT)
                for t in range(TT):
                    here = slice(t * P, (t + 1) * P)
                    for k in range(KT):
                        nc.tensor.matmul(O[:, t * E:(t + 1) * E], hT_now[:, k, here], T["gate_w"][:, k, :], start=k == 0, stop=False)
                    ins = nc.tensor.matmul(O[:, t * E:(t + 1) * E], ones[0:1, :], T["gate_b"][:, :], start=False, stop=True)
                ins.then_inc(g_ready, 1)

            def begin():
                pe.wait_ge(w_split, 1)
                pe.wait_ge(h_split, 1)
                for t in range(TT):
                    project(0, 0, t)
                transpose_q(0)
                transpose_k(0)
                pe.wait_ge(w_split, PAIRS)
                logits(0, 0, 0)
                logits(0, 1, 0)

            def pair(c, g, p, odd, start, fresh, more):
                nxt, even, late = plus(pe, g, 1), 1 - odd, int(fresh)
                after_chunk = start and not (isinstance(c, int) and c == 0)
                p_next = 0 if fresh else p + 1
                for u in range(U):
                    if u < U - 2:
                        logits(g, u + 2, odd)
                    elif more and not fresh:
                        logits(nxt, u + 2 - U, even)
                    transpose_probs(g, u)
                    if u == 0 and fresh:
                        widen_inverses(g - 1, 1, False, None)
                        attend(g - 1, 1, even)
                    if more:
                        if u == late:
                            if fresh:
                                pe.wait_ge(h_split, c + 2)
                            project(nxt, p_next, 0, g * 2 if start or fresh else g * 2 - 1)
                            project(nxt, p_next, 1)
                        if u == 1 + late:
                            project(nxt, p_next, 2)
                        if u == 2 + late:
                            project(nxt, p_next, 3)
                        if u == 4 + late:
                            transpose_q(nxt)
                            transpose_k(nxt)
                    if u == 3 and not start and not fresh:
                        widen_inverses(g - 1, 1, more, g * TT + 2 * TT)
                        attend(g - 1, 1, even)
                    if after_chunk:
                        if u < KT:
                            output_transposes(c - 1, u)
                        if u == KT:
                            gates(c - 1)
                    if u == 5:
                        widen_inverses(g, 0, more, g * TT + 2 * TT)
                    if u == 6:
                        attend(g, 0, odd, c if after_chunk else None)

            def finish(c, more):
                g7, nxt = plus(pe, c * PAIRS, PAIRS - 1), plus(pe, c * PAIRS, PAIRS)
                widen_inverses(g7, 1, False, None)
                attend(g7, 1, 1)
                if isinstance(c, int) and c == 0:
                    pe.wait_ge(wo_split, 1)
                pe.wait_ge(exp_done, c * CU + CU)
                pe.wait_ge(o_split, c * CO + CO)
                for t in range(TT):
                    if t >= 2:
                        pe.wait_ge(n_stats, c * TT + (t - 1))
                    steps = [(a, b, p) for a, b in THREE for p in range(PAIRS)]
                    for i, (a, b, p) in enumerate(steps):
                        ins = nc.tensor.matmul(S[:, t % 2, 0:D], attnT_s[a][:, p, t * P:(t + 1) * P], wo_s[b][:, p, :],
                                               start=i == 0, stop=i == len(steps) - 1)
                    ins.then_inc(wo_ready, 1)
                if more:
                    pe.wait_ge(n_stats, c * TT + (TT - 1))
                    logits(nxt, 0, 0)
                    pe.wait_ge(n_stats, c * TT + TT)
                    logits(nxt, 1, 0)

            def after(c):
                for k in range(KT):
                    output_transposes(c, k)
                gates(c)

            pairs(nc.tensor, begin, pair, finish, after)


def experts_phase(nc, T, ln_g, ln_b, w1, b2, w2, x1_dram, out):
    hT_all, gate_all, columns = T["hT_all"], T["gate_all"], T["columns"]
    ident, neg_half = T["ident"], T["neg_half"]
    moe_sum = hT_all[:, :, :, :].rearrange("p c k n -> p c (k n)").rearrange("p c (t d) -> p c t d", d=D)
    KT, FT = D // P, FF // P
    LAST = E - 1

    ctx = ExitStack()
    with ctx:
        sb = lambda name, shape, dt: ctx.enter_context(nc.sbuf_tensor(name, shape, dt))
        sem = lambda name: ctx.enter_context(nc.semaphore(name))
        h_hi = sb("h2T_hi", [P, CHUNKS, KT, ROWS], f32r)
        h_lo = sb("h2T_lo", [P, CHUNKS, KT, ROWS], f32r)
        W1_COLS = KT * FF
        W_COLS = W1_COLS + FT * D
        w_hi = [sb(f"w_hi{i}", [P, W_COLS], f32r) for i in range(2)]
        w_lo = [sb(f"w_lo{i}", [P, W_COLS], f32r) for i in range(2)]
        w_raw = sb("w_raw", [P, W_COLS], f32)
        g_rows, b_rows = sb("g_rows", [P, D], f32), sb("b_rows", [P, D], f32)
        b2_sb = sb("b2_sb", [E, D], f32)
        hid = sb("hid", [P, 2, ROWS], f32)
        hid_hi = sb("hid_hi", [P, 4, ROWS], f32r)
        hid_lo = sb("hid_lo", [P, 4, ROWS], f32r)
        gT = hid[0:E, :, :]
        x1c = w_raw[:, 0:TT * D].rearrange("p (t d) -> p t d", d=D)
        bn = sb("bn2", [P, TT, 6], f32)
        mv = sb("mv2", [P, TT, 2], f32)
        veps = sb("veps2", [P, TT], f32)
        rstd = sb("rstd2", [P, TT], f32)
        H = ctx.enter_context(nc.psum_tensor("psum_hid", [P, 4, 512], f32))
        O = ctx.enter_context(nc.psum_tensor("psum_out", [P, 4, 2, D], f32))

        w_loaded = sem("w_loaded")
        b2_loaded = sem("b2_loaded")
        norm_loaded = sem("norm_loaded")
        w_hi_done = sem("w_hi_done")
        w_split = sem("w_split")
        h_hi_done = sem("h_hi_done")
        h_split = sem("h_split")
        gT_ready = sem("gT_ready")
        gT_copied = sem("gT_copied")
        bias_ready = sem("bias_ready")
        sum_begun = sem("sum_begun")
        hid_ready = sem("hid_ready")
        gelu_done = sem("gelu_done")
        hid_hi_done = sem("hid_hi_done")
        hid_split = sem("hid_split")
        out_used = sem("out_used")
        sum_done = sem("sum_done")
        x1_loaded = sem("x1_loaded")
        stats_done = sem("stats_done")
        mv_done = sem("mv_done")
        var_done = sem("var_done")
        rstd_done = sem("rstd_done")
        norm_step = sem("norm_step")
        y_done = sem("y_done")
        stored = sem("stored")
        block = ctx.enter_context(nc.Block())

        def experts(engine, run):
            run(0, 0, True, False)
            with engine.Fori(0, (E - 2) // 2) as i:
                for step in (1, 2):
                    run(engine.snap(i * 2 + step), step % 2, False, False)
            run(LAST, LAST % 2, False, True)

        def cell(e, c):
            return e * CHUNKS + c

        @block.sync
        def _(sp):
            def load_weights(e, first):
                if not first:
                    sp.wait_ge(w_split, 8 * e)
                sp.dma_start(w_raw[:, 0:W1_COLS].rearrange("p (k f) -> p k f", k=KT),
                             w1[bass.ds(e, 1), :, :].rearrange("e (k p) f -> p (e k) f", p=P)).then_inc(w_loaded, 16)
                sp.dma_start(w_raw[:, W1_COLS:W_COLS].rearrange("p (k f) -> p k f", k=FT),
                             w2[bass.ds(e, 1), :, :].rearrange("e (k p) f -> p (e k) f", p=P)).then_inc(w_loaded, 16)

            load_weights(0, True)
            sp.dma_start(b2_sb[:, :], b2).then_inc(b2_loaded, 16)
            sp.dma_start(g_rows[:, :], ln_g.unsqueeze(0).to_broadcast([P, D])).then_inc(norm_loaded, 16)
            sp.dma_start(b_rows[:, :], ln_b.unsqueeze(0).to_broadcast([P, D])).then_inc(norm_loaded, 16)
            with sp.Fori(1, E) as e:
                load_weights(e, False)
            for c in range(CHUNKS):
                if c:
                    sp.wait_ge(y_done, c)
                    sp.wait_ge(x1_loaded, 16 * c)
                else:
                    sp.wait_ge(w_split, 8 * E)
                sp.dma_start(x1c[:, :, :], x1_dram[c, :, :, :].rearrange("t p d -> p t d")).then_inc(x1_loaded, 16)
                sp.wait_ge(y_done, c + 1)
                sp.dma_start(out[c, :, :].rearrange("(t p) d -> p t d", p=P), moe_sum[:, c, :, :]).then_inc(stored, 16)
            sp.wait_ge(stored, 16 * CHUNKS)

        @block.gpsimd
        def _(pool):
            for c in range(CHUNKS):
                pool.wait_ge(var_done, c + 1)
                nc.gpsimd.tensor_tensor(rstd[:, :], veps[:, :], neg_half[:, 0:TT], ALU.pow).then_inc(rstd_done, 1)

        @block.scalar
        def _(act):
            act.wait_ge(w_loaded, 32)
            for i in range(8):
                nc.scalar.activation(w_hi[0][:, i * 512:(i + 1) * 512], w_raw[:, i * 512:(i + 1) * 512],
                                     ACT.Copy).then_inc(w_hi_done, 1)
            for c in range(CHUNKS):
                nc.scalar.activation(h_hi[:, c, :, :], hT_all[:, c, :, :], ACT.Copy).then_inc(h_hi_done, 1)
                act.wait_ge(gT_ready, c + 1)
                if c >= 2:
                    act.wait_ge(bias_ready, c - 1)
                nc.scalar.activation(gT[:, c % 2, :], H[0:E, c % 4, :], ACT.Copy).then_inc(gT_copied, 1)
            def gelus(e, c, first):
                base = act.snap(cell(e, c) * FT)
                for f in range(FT):
                    act.wait_ge(hid_ready, base + (f + 1))
                    if not first or f >= 2:
                        act.wait_ge(hid_split, base + (f - 1))
                    nc.scalar.activation(hid[:, f % 2, :], H[:, f % 4, :], ACT.Gelu_apprx_tanh,
                                         bias=columns[:, bass.ds(e * FT + (COL_B1 + f), 1)]).then_inc(gelu_done, 1)

            def run(e, odd, first, last):
                if first:
                    gelus(0, 0, True)
                with nc.scalar.Fori(int(first), CHUNKS) as c:
                    gelus(e, c, False)

            experts(nc.scalar, run)

        @block.vector
        def _(dve):
            def split_weights(e, odd, i):
                cols = bass.ds(i * 512, 512)
                nc.vector.tensor_copy(w_hi[odd][:, cols], w_raw[:, cols]).then_inc(w_hi_done, 1)
                dve.wait_ge(w_hi_done, e * 8 + i + 1)
                nc.vector.tensor_tensor(w_lo[odd][:, cols], w_raw[:, cols], w_hi[odd][:, cols].bitcast(f32),
                                        ALU.subtract).then_inc(w_split, 1)

            for i in range(8):
                dve.wait_ge(w_hi_done, i + 1)
                cols = slice(i * 512, (i + 1) * 512)
                nc.vector.tensor_tensor(w_lo[0][:, cols], w_raw[:, cols], w_hi[0][:, cols].bitcast(f32),
                                        ALU.subtract).then_inc(w_split, 1)
            for c in range(CHUNKS):
                dve.wait_ge(h_hi_done, c + 1)
                nc.vector.tensor_tensor(h_lo[:, c, :, :], hT_all[:, c, :, :], h_hi[:, c, :, :].bitcast(f32),
                                        ALU.subtract).then_inc(h_split, 1)
                dve.wait_ge(bias_ready, c + 1)
                dve.wait_ge(h_split, c + 1)
                nc.vector.tensor_copy(moe_sum[:, c, :, :], O[:, c % 2 * 2:c % 2 * 2 + 2, :, :]
                                      .rearrange("p a b d -> p (a b) d")).then_inc(sum_begun, 1)

            def split_hidden(base, f):
                dve.wait_ge(gelu_done, base + (f + 1))
                nc.vector.tensor_copy(hid_hi[:, f % 4, :], hid[:, f % 2, :]).then_inc(hid_hi_done, 1)
                dve.wait_ge(hid_hi_done, base + (f + 1))
                nc.vector.tensor_tensor(hid_lo[:, f % 4, :], hid[:, f % 2, :], hid_hi[:, f % 4, :].bitcast(f32),
                                        ALU.subtract).then_inc(hid_split, 1)

            def slot_free(base, f, begun):
                if begun or f >= 4:
                    dve.wait_ge(out_used, base + (f - 3))

            def add_chunk(e, c, n, first):
                dve.wait_ge(out_used, (n + 1) * FT)
                if not first:
                    dve.wait_ge(sum_done, n - (CHUNKS - 1))
                half = n % 2 * 2
                for t in range(TT):
                    ins = nc.vector.scalar_tensor_tensor(
                        out=moe_sum[:, bass.ds(c, 1), t, :], in0=O[:, bass.ds(half + t // 2, 1), t % 2, :],
                        scalar=gate_all[:, bass.ds(c, 1), t, bass.ds(e, 1)].rearrange("p a b -> p (a b)"),
                        in1=moe_sum[:, bass.ds(c, 1), t, :], op0=ALU.mult, op1=ALU.add)
                ins.then_inc(sum_done, 1)

            def final_norm(c):
                dve.wait_ge(sum_done, cell(LAST, c) + 1)
                for t in range(TT):
                    ins = nc.vector.bn_stats(bn[:, t, :], moe_sum[:, c, t, :])
                ins.then_inc(stats_done, 1)
                dve.wait_ge(stats_done, c + 1)
                for t in range(TT):
                    ins = nc.vector.bn_aggr(mv[:, t, :], bn[:, t, :])
                ins.then_inc(mv_done, 1)
                dve.wait_ge(mv_done, c + 1)
                nc.vector.tensor_scalar_add(veps[:, :], mv[:, :, 1], EPS).then_inc(var_done, 1)
                dve.wait_ge(rstd_done, c + 1)
                for t in range(TT):
                    ins = nc.vector.tensor_scalar(moe_sum[:, c, t, :], moe_sum[:, c, t, :], mv[:, t, 0:1], rstd[:, t:t + 1],
                                                  ALU.subtract, ALU.mult)
                ins.then_inc(norm_step, 1)
                dve.wait_ge(norm_step, 3 * c + 1)
                dve.wait_ge(norm_loaded, 32)
                nc.vector.tensor_tensor(moe_sum[:, c, :, :], moe_sum[:, c, :, :], g_rows[:, :].unsqueeze(1).to_broadcast([P, TT, D]),
                                        ALU.mult).then_inc(norm_step, 1)
                dve.wait_ge(norm_step, 3 * c + 2)
                nc.vector.tensor_tensor(moe_sum[:, c, :, :], moe_sum[:, c, :, :], b_rows[:, :].unsqueeze(1).to_broadcast([P, TT, D]),
                                        ALU.add).then_inc(norm_step, 1)
                dve.wait_ge(norm_step, 3 * c + 3)
                dve.wait_ge(x1_loaded, 16 * (c + 1))
                nc.vector.tensor_tensor(moe_sum[:, c, :, :], moe_sum[:, c, :, :], x1c[:, :, :], ALU.add).then_inc(y_done, 1)

            def run(e, odd, first, last):
                def chunk(c):
                    base = dve.snap(cell(e, c) * FT)
                    for f in range(FT):
                        slot_free(base, f, True)
                        split_hidden(base, f)
                        if f == 1:
                            add_chunk(e, c - 1, dve.snap(cell(e, c - 1)), first)
                        if f == 4 and not last:
                            split_weights(e + 1, 1 - odd, c)
                        if f == 4 and last:
                            final_norm(c - 1)

                for f in range(FT):
                    slot_free(cell(e, 0) * FT, f, not first)
                    split_hidden(cell(e, 0) * FT, f)
                if last:
                    for c in range(1, CHUNKS):
                        chunk(c)
                else:
                    dve.wait_ge(w_loaded, e * 32 + 64)
                    split_weights(e + 1, 1 - odd, 0)
                    with nc.vector.Fori(1, CHUNKS) as c:
                        chunk(c)
                add_chunk(e, CHUNKS - 1, cell(e, CHUNKS - 1), first)

            experts(nc.vector, run)
            final_norm(CHUNKS - 1)

        @block.tensor
        def _(pe):
            def weights1(odd, half, k, f):
                at = k * FF + f * P
                return (w_hi, w_lo)[half][odd][:, at:at + P]

            def weights2(odd, half, f):
                at = W1_COLS + f * D
                return (w_hi, w_lo)[half][odd][:, at:at + D]

            def up(odd, c, f, base):
                if base is not None:
                    pe.wait_ge(gelu_done, base + (f - 3))
                steps = [(a, b, k) for a, b in ((0, 0), (1, 0), (0, 1)) for k in range(KT)]
                for i, (a, b, k) in enumerate(steps):
                    ins = nc.tensor.matmul(H[:, f % 4, :], weights1(odd, a, k, f),
                                           (h_hi, h_lo)[b][:, bass.ds(c, 1), k, :],
                                           start=i == 0, stop=i == len(steps) - 1)
                ins.then_inc(hid_ready, 1)

            def down(odd, f, n):
                pe.wait_ge(hid_split, n * FT + (f + 1))
                half = n % 2 * 2
                for t in range(TT):
                    for i, (a, b) in enumerate(((0, 0), (1, 0), (0, 1))):
                        tokens = (hid_hi, hid_lo)[a][:, f % 4, t * P:(t + 1) * P]
                        ins = nc.tensor.matmul(O[:, bass.ds(half + t // 2, 1), t % 2, :], tokens, weights2(odd, b, f),
                                               start=f == 0 and i == 0 and t % 2 == 0,
                                               stop=f == FT - 1 and i == 2, skip_group_check=True)
                ins.then_inc(out_used, 1)

            pe.wait_ge(b2_loaded, 16)
            for c in range(CHUNKS):
                if c >= 4:
                    pe.wait_ge(gT_copied, c - 3)
                for t in range(TT):
                    ins = nc.tensor.transpose(H[0:E, c % 4, t * P:(t + 1) * P], gate_all[:, c, t, :], ident[:, :])
                ins.then_inc(gT_ready, 1)
                pe.wait_ge(gT_copied, c + 1)
                if c >= 2:
                    pe.wait_ge(sum_begun, c - 1)
                for t in range(TT):
                    ins = nc.tensor.matmul(O[:, c % 2 * 2 + t // 2, t % 2, :], gT[:, c % 2, t * P:(t + 1) * P],
                                           b2_sb[:, :], start=t % 2 == 0, stop=True, skip_group_check=True)
                ins.then_inc(bias_ready, 1)

            pe.wait_ge(w_split, 8)
            pe.wait_ge(h_split, 2)
            pe.wait_ge(sum_begun, CHUNKS)
            up(0, 0, 0, None)
            up(0, 0, 1, None)

            def run(e, odd, first, last):
                def chunk(c, closing, begun):
                    n = pe.snap(cell(e, c))
                    base = pe.snap(n * FT)
                    for f in range(FT):
                        if f < FT - 2:
                            up(odd, c, f + 2, base if begun or f + 2 >= 4 else None)
                        elif not closing:
                            up(odd, c + 1, f + 2 - FT, base + FT)
                        elif not last:
                            if f == FT - 2:
                                pe.wait_ge(w_split, e * 8 + 16)
                            up(1 - odd, 0, f + 2 - FT, base + FT)
                        if f == 0 and begun:
                            pe.wait_ge(sum_done, n - 1)
                        down(odd, f, n)

                if first:
                    chunk(0, False, False)
                    pe.wait_ge(h_split, CHUNKS)
                with nc.tensor.Fori(int(first), CHUNKS - 1) as c:
                    chunk(c, False, True)
                chunk(CHUNKS - 1, True, True)

            experts(nc.tensor, run)


def xattn_ffn_kernel(nc, x, context, w_sim, b_sim, W_qv, b_qv, ln_g, ln_b, Wq, Wk, Wv, q_scale, k_scale, Wo,
                     gate_w, gate_b, w1, b1, w2, b2, out):
    x1_dram = nc.dram_tensor("x1_kept", (CHUNKS, TT, P, D), f32, kind="Internal").ap()
    with ExitStack() as ctx:
        T = {}
        for name, shape, dt in (("hT_all", [P, CHUNKS, KT, ROWS], f32), ("gate_all", [P, CHUNKS, TT, E], f32),
                                ("columns", [P, N_COLS], f32), ("ident", [P, P], f32), ("ident_b", [P, P], bf16),
                                ("mask", [P, P], bf16), ("ones", [P, P], f32), ("neg_half", [P, 8], f32),
                                ("qk_scale", [P, PAIRS], f32), ("gate_w", [P, KT, E], f32), ("gate_b", [1, E], f32)):
            T[name] = ctx.enter_context(nc.sbuf_tensor(name, shape, dt))
        setup_phase(nc, T, w_sim, ln_g, ln_b, q_scale, k_scale, gate_w, gate_b, b1)
        with nc.sbuf_tensor("self_raw", [P, 3 * KT + 2, HEADS * DH], f32) as self_raw:
            T["self_raw"] = self_raw
            cross_attention_phase(nc, T, x, context, W_qv, b_qv, b_sim, Wq, Wk, Wv, Wo, x1_dram)
        self_attention_phase(nc, T)
        experts_phase(nc, T, ln_g, ln_b, w1, b2, w2, x1_dram, out)


_INS = ['x', 'ctx_1024', 'L0_xattn_w_sim', 'L0_xattn_b_sim', 'L0_xattn_W_qv', 'L0_xattn_b_qv', 'L0_ffn_ln_g',
        'L0_ffn_ln_b', 'L0_ffn_Wq', 'L0_ffn_Wk', 'L0_ffn_Wv', 'L0_ffn_q_scale', 'L0_ffn_k_scale', 'L0_ffn_Wo',
        'L0_ffn_gate_w', 'L0_ffn_gate_b', 'L0_ffn_w1', 'L0_ffn_b1', 'L0_ffn_w2', 'L0_ffn_b2']
_OUTS = [((8, 512, 256), 'float32')]


def kernel(**inputs):
    import numpy as _np
    import concourse.bacc as _bacc
    from concourse import mybir as _mybir
    from concourse.bass_utils import run_bass_kernel_spmd as _run

    nc = _bacc.Bacc("TRN2", target_bir_lowering=False, num_devices=1)
    arrays, args = {}, []
    for name in _INS:
        a = _np.ascontiguousarray(inputs[name])
        arrays[f"in_{name}_dram"] = a
        args.append(nc.dram_tensor(f"in_{name}_dram", a.shape, _mybir.dt.from_np(a.dtype), kind="ExternalInput").ap())
    for i, (shape, dtype) in enumerate(_OUTS):
        dt = _mybir.dt.from_np(_np.dtype(dtype))
        args.append(nc.dram_tensor(f"out_{i}_dram", shape, dt, kind="ExternalOutput").ap())
    xattn_ffn_kernel(nc, *args)
    r = _run(nc, [arrays], core_ids=[0])
    got = tuple(r.results[0][f"out_{i}_dram"] for i in range(len(_OUTS)))
    return got[0]
```

```python
from contextlib import ExitStack

import concourse.bass as bass
from concourse import mybir

f32 = mybir.dt.float32
f32r = mybir.dt.float32r
bf16 = mybir.dt.bfloat16
ALU = mybir.AluOpType
ACT = mybir.ActivationFunctionType
AX = mybir.AxisListType

P = 128
CHUNKS, ROWS, D = 8, 512, 256
TT = ROWS // P
KT = D // P
HEADS, DH = 16, 64
PAIRS = HEADS // 2
E, FF = 8, 1024
EPS = 1e-5
QK_SCALE = 10.0
MASKED = -1e30

COL_WSIM, COL_G, COL_B, COL_QS, COL_KS, COL_B1 = 0, 6, 8, 10, 18, 26
N_COLS = COL_B1 + E * FF // P


def load_expert(queue, w_raw, w1, w2, e, loaded):
    queue.dma_start(w_raw[:, 0:KT * FF].rearrange("p (k f) -> p k f", k=KT),
                    w1[bass.ds(e, 1), :, :].rearrange("e (k p) f -> p (e k) f", p=P)).then_inc(loaded, 16)
    queue.dma_start(w_raw[:, KT * FF:].rearrange("p (k f) -> p k f", k=FF // P),
                    w2[bass.ds(e, 1), :, :].rearrange("e (k p) f -> p (e k) f", p=P)).then_inc(loaded, 16)


def setup_phase(nc, T, w_sim, ln_g, ln_b, q_scale, k_scale, gate_w, gate_b, b1):
    ident, ones, neg_half, columns = T["ident"], T["ones"], T["neg_half"], T["columns"]
    ctx = ExitStack()
    with ctx:
        rows = ctx.enter_context(nc.sbuf_tensor("param_rows", [N_COLS, P], f32))
        cols_ps = ctx.enter_context(nc.psum_tensor("psum_columns", [P, 512], f32))
        sem = lambda name: ctx.enter_context(nc.semaphore(name))
        rows_loaded, gate_loaded = sem("rows_loaded"), sem("gate_loaded")
        ident_zero, ident_done, consts_done = sem("ident_zero"), sem("ident_done"), sem("consts_done")
        cols_ready, cols_done = sem("cols_ready"), sem("cols_done")
        block = ctx.enter_context(nc.Block())

        @block.sync
        def _(sp):
            for at, src, n in ((COL_WSIM, w_sim, 6), (COL_G, ln_g, 2), (COL_B, ln_b, 2)):
                sp.dma_start(rows[at:at + n, :], src.rearrange("(r p) -> r p", p=P)).then_inc(rows_loaded, 16)
            for at, src in ((COL_QS, q_scale), (COL_KS, k_scale)):
                sp.dma_start(rows[at:at + PAIRS, :], src.rearrange("(r h) a d -> r (h a d)", h=2)).then_inc(rows_loaded, 16)
            sp.dma_start(rows[COL_B1:N_COLS, :], b1.rearrange("e (f p) -> (e f) p", p=P)).then_inc(rows_loaded, 16)

        @block.gpsimd
        def _(pool):
            nc.gpsimd.memset(ident[:, :], 0.0).then_inc(ident_zero, 1)
            nc.gpsimd.memset(ones[:, :], 1.0).then_inc(consts_done, 1)
            nc.gpsimd.memset(neg_half[:, :], -0.5).then_inc(consts_done, 1)
            nc.gpsimd.memset(T["mask"][:, :], 0.0).then_inc(ident_zero, 1)
            pool.wait_ge(ident_zero, 2)
            nc.gpsimd.affine_select(out=T["mask"][:, :], in_=T["mask"][:, :], compare_op=ALU.is_ge, fill=MASKED,
                                    base=0, pattern=[[-1, P]], channel_multiplier=1).then_inc(ident_done, 1)
            nc.gpsimd.affine_select(out=ident[:, :], in_=ident[:, :], compare_op=ALU.not_equal, fill=1.0,
                                    base=0, pattern=[[-1, P]], channel_multiplier=1).then_inc(ident_done, 1)

        @block.scalar
        def _(act):
            act.dma_start(T["gate_w"][:, :, :], gate_w.rearrange("(k p) e -> p k e", p=P)).then_inc(gate_loaded, 16)
            act.dma_start(T["gate_b"][:, :], gate_b.unsqueeze(0)).then_inc(gate_loaded, 16)
            act.wait_ge(gate_loaded, 32)

        @block.tensor
        def _(pe):
            pe.wait_ge(rows_loaded, 96)
            pe.wait_ge(ident_done, 2)
            nc.tensor.transpose(cols_ps[:, 0:N_COLS], rows[:, :], ident[0:N_COLS, 0:N_COLS]).then_inc(cols_ready, 1)

        @block.vector
        def _(dve):
            dve.wait_ge(cols_ready, 1)
            nc.vector.tensor_copy(columns[:, :], cols_ps[:, 0:N_COLS]).then_inc(cols_done, 1)
            dve.wait_ge(cols_done, 1)
            nc.vector.scalar_tensor_tensor(out=T["qk_scale"][:, :], in0=columns[:, COL_QS:COL_QS + PAIRS],
                                           scalar=QK_SCALE, in1=columns[:, COL_KS:COL_KS + PAIRS],
                                           op0=ALU.mult, op1=ALU.mult).then_inc(cols_done, 1)
            dve.wait_ge(ident_done, 2)
            nc.vector.tensor_copy(T["ident_b"][:, :], ident[:, :]).then_inc(cols_done, 1)
            dve.wait_ge(consts_done, 2)


def cross_attention_phase(nc, T, x, context, W_qv, b_qv, b_sim, Wq, Wk, Wv, Wo, x1_dram):
    ident, ones, neg_half, columns = T["ident"], T["ones"], T["neg_half"], T["columns"]
    hT_all, self_raw = T["hT_all"], T["self_raw"]

    ctx = ExitStack()
    with ctx:
        sb = lambda name, shape, dt=f32: ctx.enter_context(nc.sbuf_tensor(name, shape, dt))
        pair = lambda name, shape: (sb(name + "_hi", shape, f32r), sb(name + "_lo", shape, f32r))
        sem = lambda name: ctx.enter_context(nc.semaphore(name))

        xb = [sb(f"x_biased{i}", [P, TT, D]) for i in range(2)]
        encT = [sb(f"encT{i}", [P, KT, ROWS]) for i in range(2)]
        enc_s = [pair(f"encT_s{i}", [P, KT, ROWS]) for i in range(2)]
        xr = sb("x_raw", [P, TT, D])
        enc = sb("enc", [P, TT, D])
        cx = sb("cx", [P, TT, D])
        cx_s = pair("cx_s", [P, TT, D])
        cxT_s = pair("cxT_s", [P, KT, ROWS])
        ep = sb("ep", [P, KT, ROWS])
        ep_s = pair("ep_s", [P, KT, ROWS])
        prob = sb("prob", [P, TT, ROWS])
        probT_s = pair("probT_s", [P, TT, ROWS])
        hq_s = pair("hq_s", [P, KT, ROWS])
        prod = sb("prod", [P, KT, ROWS])
        prod_s = pair("prod_s", [P, KT, ROWS])
        w_enc = sb("w_enc", [P, KT, D])
        w_bar = sb("w_bar", [P, KT, D])
        w_mid_s = pair("w_mid_s", [P, 2 * KT, D])
        w_mix = sb("w_mix", [P, KT, D])
        w_mix_s = pair("w_mix_s", [P, KT, D])
        x1 = sb("x1_chunk", [P, TT, D])
        h = prod[:, :, :].rearrange("p k n -> p (k n)").rearrange("p (t d) -> p t d", d=D)
        bn = sb("bn", [P, TT, 6])
        mv = sb("mv", [P, TT, 2])
        veps = sb("veps", [P, TT])
        rstd = sb("rstd", [P, TT])
        bn1 = sb("bn1", [P, TT, 6])
        mv1 = sb("mv1", [P, TT, 2])
        veps1 = sb("veps1", [P, TT])
        rstd1 = sb("rstd1", [P, TT])
        rowmax = sb("rowmax", [P, TT])
        nrowmax = sb("nrowmax", [P, TT])
        rowsum = sb("rowsum", [P, TT])
        rinv = sb("rinv", [P, TT])
        mx = sb("mx", [P, TT])
        mcol = sb("mcol", [P, 1])
        gmax = sb("gmax", [1, 1])
        ngmax = sb("ngmax", [P, 1])
        bexp = sb("bexp", [P, TT])
        binv = sb("binv", [P, 1])
        hc = sb("hc", [P, KT])
        bqv_rows = sb("bqv_rows", [P, D])
        bsim = sb("bsim", [P, 1])
        w_stage = prob[:, 0:2, :].rearrange("p a b -> p (a b)").rearrange("p (k d) -> p k d", d=D)

        TR = ctx.enter_context(nc.psum_tensor("psum_transposed", [P, 2, 512], f32))
        S = ctx.enter_context(nc.psum_tensor("psum_scores", [P, 2, 512], f32))
        HQ = ctx.enter_context(nc.psum_tensor("psum_hq", [P, 2, 512], f32))
        X = ctx.enter_context(nc.psum_tensor("psum_x1", [P, 2, 512], f32))
        BATT = S[:, 0, :]

        bias_loaded = sem("bias_loaded")
        cx_loaded, w_loaded, qkv_loaded = sem("cx_loaded"), sem("wqv_loaded"), sem("qkv_loaded")
        x_loaded = sem("x_loaded")
        wmid_hi, wmid_split = sem("wmid_hi"), sem("wmid_split")
        enc_stats, enc_mv, enc_var, enc_rstd, enc_done, xb_done = map(
            sem, ("enc_stats", "enc_mv", "enc_var", "enc_rstd", "enc_done", "xb_done"))
        encT_ready, encT_copied, ep_copied, enc_hi, enc_split, ep_hi, ep_split = map(
            sem, ("encT_ready", "encT_copied", "ep_copied", "enc_hi", "enc_split", "ep_hi", "ep_split"))
        cxT_ready, cxT_hi, cxT_split, cx_hi, cx_split = map(
            sem, ("cxT_ready", "cxT_hi", "cxT_split", "cx_hi", "cx_split"))
        hq_ready, hq_hi, hq_split, prod_done, prod_hi, prod_split = map(
            sem, ("hq_ready", "hq_hi", "hq_split", "prod_done", "prod_hi", "prod_split"))
        s_ready, max_done, nmax_done, exp_done, rinv_done, prob_done = map(
            sem, ("s_ready", "max_done", "nmax_done", "exp_done", "rinv_done", "prob_done"))
        pT_ready, pT_hi, pT_split = map(sem, ("pT_ready", "pT_hi", "pT_split"))
        r_ready, mx_done, mcol_done, mcolT_ready, gmax_done, gmax_spread, ngmax_done, bexp_done = map(
            sem, ("r_ready", "mx_done", "mcol_done", "mcolT_ready", "gmax_done", "gmax_spread", "ngmax_done", "bexp_done"))
        hc_ready, binv_done, hc_done, wmix_done, wmix_hi, wmix_split = map(
            sem, ("hc_ready", "binv_done", "hc_done", "wmix_done", "wmix_hi", "wmix_split"))
        x1_ready, x1_done, x1_stats, x1_mv, x1_var, x1_rstd, h_done, hT_ready, hT_done, x1_stored = map(
            sem, ("x1_ready", "x1_done", "x1_stats", "x1_mv", "x1_var", "x1_rstd", "h_done", "hT_ready", "hT_done", "x1_stored"))
        block = ctx.enter_context(nc.Block())

        def earlier(m):
            return not (isinstance(m, int) and m == 0)

        def steps(engine, step):
            step(None, 0, 1, 1)
            step(0, 1, 2, 0)
            step(1, 2, 3, 1)
            with engine.Fori(1, (CHUNKS - 2) // 2) as i:
                for odd in range(2):
                    m = engine.snap(i * 2 + odd)
                    step(m, m + 1, m + 2, odd)
            step(CHUNKS - 2, CHUNKS - 1, None, 0)
            step(CHUNKS - 1, None, None, 1)

        @block.sync
        def _(sp):
            def load(q):
                sp.wait_ge(enc_done, q)
                sp.wait_ge(xb_done, q)
                sp.dma_start(xr[:, :, :], x[bass.ds(q, 1), :, :].rearrange("c (t p) d -> p (c t) d", p=P)).then_inc(x_loaded, 16)
                sp.wait_ge(cxT_ready, q * 2)
                sp.wait_ge(cx_split, q)
                sp.dma_start(cx[:, :, :], context[bass.ds(q, 1), :, :].rearrange("c (t p) d -> p (c t) d", p=P)).then_inc(cx_loaded, 16)

            load(0)
            with sp.Fori(1, CHUNKS) as q:
                load(q)

        @block.gpsimd
        def _(pool):
            def prepare(q):
                pool.wait_ge(enc_var, q + 1)
                nc.gpsimd.tensor_tensor(rstd[:, :], veps[:, :], neg_half[:, 0:TT], ALU.pow).then_inc(enc_rstd, 1)

            def with_bias(q, odd, first):
                pool.wait_ge(x_loaded, q * 16 + 16)
                if not first:
                    pool.wait_ge(x1_done, q * 4 - 4)
                nc.gpsimd.tensor_tensor(xb[odd][:, :, :], xr[:, :, :],
                                        bqv_rows[:, :].unsqueeze(1).to_broadcast([P, TT, D]), ALU.add).then_inc(xb_done, 1)

            def step(m, n, q, odd):
                if m is not None:
                    for k in range(KT):
                        pool.wait_ge(prod_hi, m * 2 + (k + 1))
                        nc.gpsimd.tensor_tensor(prod_s[1][:, k, :], prod[:, k, :], prod_s[0][:, k, :].bitcast(f32),
                                                ALU.subtract).then_inc(prod_split, 1)
                if n is not None:
                    pool.wait_ge(cx_hi, n + 1)
                    nc.gpsimd.tensor_tensor(cx_s[1][:, :, :], cx[:, :, :], cx_s[0][:, :, :].bitcast(f32),
                                            ALU.subtract).then_inc(cx_split, 1)
                if q is not None:
                    prepare(q)
                if m is not None:
                    pool.wait_ge(x1_var, m + 1)
                    nc.gpsimd.tensor_tensor(rstd1[:, :], veps1[:, :], neg_half[:, 0:TT], ALU.pow).then_inc(x1_rstd, 1)
                    pool.dma_start(x1_dram[bass.ds(m, 1), :, :, :].rearrange("c t p d -> p (c t) d"),
                                   x1[:, :, :]).then_inc(x1_stored, 16)
                if q is not None:
                    with_bias(q, odd, m is None)

            prepare(0)
            pool.wait_ge(bias_loaded, 32)
            with_bias(0, 0, True)
            steps(nc.gpsimd, step)
            pool.wait_ge(x1_stored, 16 * CHUNKS)

        @block.scalar
        def _(act):
            act.dma_start(bqv_rows[:, :], b_qv.unsqueeze(0).to_broadcast([P, D])).then_inc(bias_loaded, 16)
            act.dma_start(bsim[:, :], b_sim.unsqueeze(0).to_broadcast([P, 1])).then_inc(bias_loaded, 16)
            act.dma_start(w_enc[:, :, :], W_qv[0:D, :].rearrange("(k p) d -> p k d", p=P)).then_inc(w_loaded, 16)
            act.dma_start(w_bar[:, :, :], W_qv[3 * D:4 * D, :].rearrange("(k p) d -> p k d", p=P)).then_inc(w_loaded, 16)
            act.dma_start(w_stage, W_qv[D:3 * D, :].rearrange("(k p) d -> p k d", p=P)).then_inc(w_loaded, 16)
            for i, w in enumerate((Wq, Wk, Wv)):
                act.dma_start(self_raw[:, i * KT:(i + 1) * KT, :], w.rearrange("(k p) n -> p k n", p=P)).then_inc(qkv_loaded, 16)
            act.dma_start(self_raw[:, 3 * KT:, :].rearrange("p a b -> p (a b)").rearrange("p (k d) -> p k d", d=D),
                          Wo.rearrange("(k p) d -> p k d", p=P)).then_inc(qkv_loaded, 16)

            def keep_hT(m):
                for k in range(KT):
                    act.wait_ge(hT_ready, m * 2 + (k + 1))
                    nc.scalar.activation(hT_all[:, bass.ds(m, 1), k, :], TR[:, k, :].unsqueeze(1), ACT.Identity,
                                         scale=columns[:, COL_G + k:COL_G + k + 1],
                                         bias=columns[:, COL_B + k:COL_B + k + 1]).then_inc(hT_done, 1)

            def probT_high(n, t):
                act.wait_ge(hq_ready, n * 2)
                act.wait_ge(pT_ready, n * 4 + (t + 1))
                nc.scalar.activation(probT_s[0][:, :, t * P:(t + 1) * P],
                                     TR[:, t % 2, :].rearrange("p (j i) -> p j i", i=P), ACT.Copy).then_inc(pT_hi, 1)

            def step(m, n, q, odd):
                if n is not None:
                    for k in range(KT):
                        act.wait_ge(cxT_ready, n * 2 + (k + 1))
                        act.wait_ge(s_ready, n * 4)
                        nc.scalar.activation(cxT_s[0][:, k, :], TR[:, k, :], ACT.Copy).then_inc(cxT_hi, 1)
                    for k in range(KT):
                        act.wait_ge(encT_ready, n * 2 + (k + 1))
                        act.wait_ge(x1_ready, n * 4 - 4 if m is not None else 0)
                        act.wait_ge(prod_done, n * 2 - 2 if m is not None else 0)
                        nc.scalar.activation(encT[1 - odd][:, k, :], TR[:, k, :], ACT.Copy).then_inc(encT_copied, 1)
                        act.wait_ge(ep_split, n * 2)
                        nc.scalar.activation(ep[:, k, :], TR[:, k, :], ACT.Identity,
                                             scale=columns[:, COL_WSIM + 4 + k:COL_WSIM + 5 + k],
                                             bias=columns[:, COL_WSIM + 2 + k:COL_WSIM + 3 + k]).then_inc(ep_copied, 1)
                if m is None:
                    act.wait_ge(w_loaded, 48)
                    nc.scalar.activation(w_mid_s[0][:, :, :], w_stage, ACT.Copy).then_inc(wmid_hi, 1)

                def context_hi():
                    act.wait_ge(cx_loaded, n * 16 + 16)
                    act.wait_ge(hq_ready, n * 2)
                    nc.scalar.activation(cx_s[0][:, :, :], cx[:, :, :], ACT.Copy).then_inc(cx_hi, 1)

                if m is not None:
                    for k in range(KT):
                        act.wait_ge(hq_ready, m * 2 + (k + 1))
                        act.wait_ge(x1_ready, m * 4)
                        nc.scalar.activation(hq_s[0][:, k, :], HQ[:, k, :], ACT.Copy).then_inc(hq_hi, 1)
                        if k == 0 and earlier(m):
                            keep_hT(m - 1)
                        act.wait_ge(prod_done, m * 2 + (k + 1))
                        nc.scalar.activation(prod_s[0][:, k, :], prod[:, k, :], ACT.Copy).then_inc(prod_hi, 1)
                if m is not None:
                    act.wait_ge(wmix_done, m + 1)
                    act.wait_ge(x1_ready, m * 4)
                    nc.scalar.activation(w_mix_s[0][:, :, :], w_mix[:, :, :], ACT.Copy).then_inc(wmix_hi, 1)
                if n is not None:
                    for t in range(TT):
                        act.wait_ge(nmax_done, n * 4 + (t + 1))
                        if m is None and t == 0:
                            act.wait_ge(wmid_split, 1)
                        act.wait_ge(pT_ready, n * 4)
                        nc.scalar.activation(prob[:, t, :], S[:, t % 2, :], ACT.Exp, bias=nrowmax[:, t:t + 1],
                                             accum_out=rowsum[:, t:t + 1]).then_inc(exp_done, 1)
                    context_hi()
                    probT_high(n, 0)
                    probT_high(n, 1)
                    act.wait_ge(ngmax_done, n + 1)
                    act.wait_ge(hc_ready, n)
                    nc.scalar.activation(bexp[:, :], mx[:, :], ACT.Exp, bias=ngmax[:, 0:1]).then_inc(bexp_done, 1)
                    probT_high(n, 2)
                    probT_high(n, 3)

            steps(nc.scalar, step)
            keep_hT(CHUNKS - 1)
            act.wait_ge(qkv_loaded, 64)

        @block.vector
        def _(dve):
            def stats(q):
                dve.wait_ge(x_loaded, q * 16 + 16)
                for t in range(TT):
                    ins = nc.vector.bn_stats(bn[:, t, :], xr[:, t, :])
                ins.then_inc(enc_stats, 1)
                dve.wait_ge(enc_stats, q + 1)

            def variance(q):
                for t in range(TT):
                    ins = nc.vector.bn_aggr(mv[:, t, :], bn[:, t, :])
                ins.then_inc(enc_mv, 1)
                dve.wait_ge(enc_mv, q + 1)
                dve.wait_ge(enc_rstd, q)
                nc.vector.tensor_scalar_add(veps[:, :], mv[:, :, 1], EPS).then_inc(enc_var, 1)

            def normalise(q):
                dve.wait_ge(enc_rstd, q + 1)
                dve.wait_ge(hc_ready, q)
                dve.wait_ge(encT_ready, q * 2)
                for t in range(TT):
                    ins = nc.vector.tensor_scalar(enc[:, t, :], xr[:, t, :], mv[:, t, 0:1], rstd[:, t:t + 1],
                                                  ALU.subtract, ALU.mult)
                ins.then_inc(enc_done, 1)

            def x1_tile(m, t, odd):
                dve.wait_ge(x1_ready, m * 4 + (t + 1))
                if t == 0:
                    dve.wait_ge(xb_done, m + 1)
                    dve.wait_ge(x1_stored, m * 16)
                    dve.wait_ge(h_done, m)
                nc.vector.tensor_tensor(x1[:, t, :], X[:, t % 2, 0:D], xb[odd][:, t, :], ALU.add).then_inc(x1_done, 1)

            def probT_low(n, t):
                dve.wait_ge(pT_hi, n * 4 + (t + 1))
                here = slice(t * P, (t + 1) * P)
                nc.vector.tensor_tensor(probT_s[1][:, :, here], TR[:, t % 2, :].rearrange("p (j i) -> p j i", i=P),
                                        probT_s[0][:, :, here].bitcast(f32), ALU.subtract).then_inc(pT_split, 1)

            def make_h(m):
                dve.wait_ge(x1_rstd, m + 1)
                dve.wait_ge(prod_split, m * 2 + 2)
                for t in range(TT):
                    ins = nc.vector.tensor_scalar(h[:, t, :], x1[:, t, :], mv1[:, t, 0:1], rstd1[:, t:t + 1],
                                                  ALU.subtract, ALU.mult)
                ins.then_inc(h_done, 1)

            def mix_weights(m):
                dve.wait_ge(hc_done, m + 1)
                dve.wait_ge(w_loaded, 48)
                dve.wait_ge(wmix_split, m)
                for k in range(KT):
                    ins = nc.vector.scalar_tensor_tensor(out=w_mix[:, k, :], in0=w_bar[:, k, :], scalar=hc[:, k:k + 1],
                                                         in1=w_enc[:, k, :], op0=ALU.mult, op1=ALU.add)
                ins.then_inc(wmix_done, 1)

            def low_weights(m):
                dve.wait_ge(wmix_hi, m + 1)
                nc.vector.tensor_tensor(w_mix_s[1][:, :, :], w_mix[:, :, :], w_mix_s[0][:, :, :].bitcast(f32),
                                        ALU.subtract).then_inc(wmix_split, 1)

            def split_enc(n, k, even):
                dve.wait_ge(encT_copied, n * 2 + (k + 1))
                nc.vector.tensor_copy(enc_s[even][0][:, k, :], encT[even][:, k, :]).then_inc(enc_hi, 1)
                dve.wait_ge(enc_hi, n * 2 + (k + 1))
                nc.vector.tensor_tensor(enc_s[even][1][:, k, :], encT[even][:, k, :], enc_s[even][0][:, k, :].bitcast(f32),
                                        ALU.subtract).then_inc(enc_split, 1)

            def step(m, n, q, odd):
                even = 1 - odd
                if n is not None:
                    for k in range(KT):
                        dve.wait_ge(cxT_hi, n * 2 + (k + 1))
                        nc.vector.tensor_tensor(cxT_s[1][:, k, :], TR[:, k, :], cxT_s[0][:, k, :].bitcast(f32),
                                                ALU.subtract).then_inc(cxT_split, 1)
                if m is not None and earlier(m):
                    make_h(m - 1)
                if n is not None:
                    for k in range(KT):
                        dve.wait_ge(ep_copied, n * 2 + (k + 1))
                        dve.wait_ge(s_ready, n * 4)
                        nc.vector.tensor_copy(ep_s[0][:, k, :], ep[:, k, :]).then_inc(ep_hi, 1)
                        dve.wait_ge(ep_hi, n * 2 + (k + 1))
                        nc.vector.tensor_tensor(ep_s[1][:, k, :], ep[:, k, :], ep_s[0][:, k, :].bitcast(f32),
                                                ALU.subtract).then_inc(ep_split, 1)
                if m is None:
                    dve.wait_ge(bias_loaded, 32)
                    dve.wait_ge(wmid_hi, 1)
                    nc.vector.tensor_tensor(w_mid_s[1][:, :, :], w_stage, w_mid_s[0][:, :, :].bitcast(f32),
                                            ALU.subtract).then_inc(wmid_split, 1)
                if m is not None:
                    mix_weights(m)
                    for k in range(KT):
                        dve.wait_ge(hT_ready, m * 2)
                        dve.wait_ge(hq_hi, m * 2 + (k + 1))
                        nc.vector.tensor_tensor(prod[:, k, :], HQ[:, k, :], encT[odd][:, k, :], ALU.mult).then_inc(prod_done, 1)
                        nc.vector.tensor_tensor(hq_s[1][:, k, :], HQ[:, k, :], hq_s[0][:, k, :].bitcast(f32),
                                                ALU.subtract).then_inc(hq_split, 1)
                if m is not None and n is None:
                    low_weights(m)
                if n is not None:
                    for t in range(TT + 1):
                        if t == 2 and m is not None:
                            low_weights(m)
                        if t < TT:
                            dve.wait_ge(s_ready, n * 4 + (t + 1))
                            nc.vector.reduce_max(rowmax[:, t:t + 1], S[:, t % 2, :], AX.X).then_inc(max_done, 1)
                            dve.wait_ge(max_done, n * 4 + (t + 1))
                            nc.vector.tensor_scalar(nrowmax[:, t:t + 1], rowmax[:, t:t + 1], -1.0, None, ALU.mult).then_inc(nmax_done, 1)
                        if t:
                            u = t - 1
                            dve.wait_ge(exp_done, n * 4 + (u + 1))
                            nc.vector.reciprocal(rinv[:, u:u + 1], rowsum[:, u:u + 1]).then_inc(rinv_done, 1)
                            dve.wait_ge(rinv_done, n * 4 + (u + 1))
                            nc.vector.tensor_scalar(prob[:, u, :], prob[:, u, :], rinv[:, u:u + 1], None, ALU.mult).then_inc(prob_done, 1)
                if q is not None:
                    stats(q)
                if m is not None:
                    x1_tile(m, 0, odd)
                if q is not None:
                    variance(q)
                if n is not None:
                    dve.wait_ge(r_ready, n + 1)
                    dve.wait_ge(bexp_done, n)
                    nc.vector.scalar_tensor_tensor(out=mx[:, :], in0=BATT[:, 0:TT], scalar=bsim[:, 0:1], in1=rowmax[:, :],
                                                   op0=ALU.add, op1=ALU.add).then_inc(mx_done, 1)
                    dve.wait_ge(mx_done, n + 1)
                    nc.vector.reduce_max(mcol[:, :], mx[:, :], AX.X).then_inc(mcol_done, 1)
                    probT_low(n, 0)
                    split_enc(n, 0, even)
                if m is not None:
                    x1_tile(m, 1, odd)
                if n is not None:
                    dve.wait_ge(mcolT_ready, n + 1)
                    nc.vector.reduce_max(gmax[:, :], BATT[0:1, 8:8 + P], AX.X).then_inc(gmax_done, 1)
                    probT_low(n, 1)
                    split_enc(n, 1, even)
                if m is not None:
                    x1_tile(m, 2, odd)
                if n is not None:
                    dve.wait_ge(gmax_spread, n + 1)
                    nc.vector.tensor_scalar(ngmax[:, :], BATT[:, 144:145], -1.0, None, ALU.mult).then_inc(ngmax_done, 1)
                if n is not None:
                    probT_low(n, 2)
                if m is not None:
                    x1_tile(m, 3, odd)
                    dve.wait_ge(x1_done, m * 4 + 4)
                    for t in range(TT):
                        ins = nc.vector.bn_stats(bn1[:, t, :], x1[:, t, :])
                    ins.then_inc(x1_stats, 1)
                    dve.wait_ge(x1_stats, m + 1)
                if q is not None:
                    normalise(q)
                if n is not None:
                    probT_low(n, 3)
                    dve.wait_ge(hc_ready, n + 1)
                    nc.vector.reciprocal(binv[:, :], BATT[:, 152:153]).then_inc(binv_done, 1)
                if m is not None:
                    for t in range(TT):
                        ins = nc.vector.bn_aggr(mv1[:, t, :], bn1[:, t, :])
                    ins.then_inc(x1_mv, 1)
                    dve.wait_ge(x1_mv, m + 1)
                    nc.vector.tensor_scalar(veps1[:, :], mv1[:, :, 1], 1.0 + EPS, EPS * EPS, ALU.mult, ALU.add).then_inc(x1_var, 1)
                if n is not None:
                    dve.wait_ge(binv_done, n + 1)
                    nc.vector.tensor_scalar(hc[:, :], BATT[:, 148:150], binv[:, 0:1], None, ALU.mult).then_inc(hc_done, 1)

            stats(0)
            variance(0)
            normalise(0)
            steps(nc.vector, step)
            make_h(CHUNKS - 1)

        @block.tensor
        def _(pe):
            THREE = ((0, 0), (1, 0), (0, 1))

            def transposes(bank, sources):
                for i, src in enumerate(sources):
                    ins = nc.tensor.transpose(TR[:, bank, i * P:(i + 1) * P], src, ident[:, :])
                return ins

            def products(out, ks, lhs, rhs):
                steps = [(a, b, k) for a, b in THREE for k in ks]
                for i, (a, b, k) in enumerate(steps):
                    ins = nc.tensor.matmul(out, lhs(a, k), rhs(b, k), start=i == 0, stop=i == len(steps) - 1)
                return ins

            def features(m, t, odd):
                pe.wait_ge(x1_done, m * 4 + max(t - 1, 0))
                here = slice(t * P, (t + 1) * P)
                groups = ([(enc_s[odd], k, w_mix_s, k) for k in range(KT)] + [(hq_s, k, w_mid_s, k) for k in range(KT)]
                          + [(prod_s, k, w_mid_s, KT + k) for k in range(KT)])
                products(X[:, t % 2, 0:D], range(3 * KT),
                         lambda a, i: groups[i][0][a][:, groups[i][1], here],
                         lambda b, i: groups[i][2][b][:, groups[i][3], :]).then_inc(x1_ready, 1)

            def transpose_probs(m, n, t):
                if t >= 2:
                    pe.wait_ge(pT_split, n * 4 + (t - 1))
                elif m is not None and earlier(m):
                    pe.wait_ge(hT_done, m * 2)
                else:
                    pe.wait_ge(ep_copied, n * 2 + (t + 1))
                pe.wait_ge(prob_done, n * 4 + (t + 1))
                transposes(t % 2, [prob[:, t, j * P:(j + 1) * P] for j in range(TT)]).then_inc(pT_ready, 1)

            def transpose_h(m):
                pe.wait_ge(h_done, m + 1)
                for k in range(KT):
                    transposes(k, [h[:, t, k * P:(k + 1) * P] for t in range(TT)]).then_inc(hT_ready, 1)

            def step(m, n, q, odd):
                even = 1 - odd
                if n is not None:
                    pe.wait_ge(pT_split, n * 4)
                    pe.wait_ge(cx_loaded, n * 16 + 16)
                    for k in range(KT):
                        transposes(k, [cx[:, t, k * P:(k + 1) * P] for t in range(TT)]).then_inc(cxT_ready, 1)
                    pe.wait_ge(enc_done, n + 1)
                    for k in range(KT):
                        pe.wait_ge(cxT_split, n * 2 + (k + 1))
                        transposes(k, [enc[:, t, k * P:(k + 1) * P] for t in range(TT)]).then_inc(encT_ready, 1)
                if m is not None:
                    pe.wait_ge(cx_split, m + 1)
                    pe.wait_ge(pT_split, m * 4 + 4)
                    pe.wait_ge(hq_split, m * 2)
                    for k in range(KT):
                        cols = slice(k * P, (k + 1) * P)
                        products(HQ[:, k, :], range(TT), lambda a, j: cx_s[a][:, j, cols],
                                 lambda b, j: probT_s[b][:, j, :]).then_inc(hq_ready, 1)
                        if k == 0 and earlier(m):
                            if n is not None:
                                pe.wait_ge(ep_copied, n * 2 + 2)
                            transpose_h(m - 1)
                if n is not None:
                    pe.wait_ge(ep_split, n * 2 + 2)
                    pe.wait_ge(cxT_split, n * 2 + 2)
                    pe.wait_ge(hc_done, n)
                    for t in range(TT):
                        if t < 2:
                            pe.wait_ge(exp_done, n * 4)
                        else:
                            pe.wait_ge(exp_done, n * 4 + (t - 1))
                        here = slice(t * P, (t + 1) * P)
                        products(S[:, t % 2, :], range(KT), lambda a, k: ep_s[a][:, k, here],
                                 lambda b, k: cxT_s[b][:, k, :]).then_inc(s_ready, 1)
                if m is not None:
                    pe.wait_ge(enc_split, m * 2 + 2)
                    pe.wait_ge(hq_split, m * 2 + 2)
                    pe.wait_ge(prod_split, m * 2 + 2)
                    pe.wait_ge(wmix_split, m + 1)
                    pe.wait_ge(wmid_split, 1)
                    features(m, 0, odd)
                if n is not None:
                    pe.wait_ge(exp_done, n * 4 + 3)
                    for t in range(TT):
                        for k in range(KT):
                            ins = nc.tensor.matmul(BATT[:, t:t + 1], encT[even][:, k, t * P:(t + 1) * P],
                                                   columns[:, COL_WSIM + k:COL_WSIM + k + 1], start=k == 0, stop=k == KT - 1)
                    ins.then_inc(r_ready, 1)
                    transpose_probs(m, n, 0)
                if m is not None:
                    features(m, 1, odd)
                if n is not None:
                    pe.wait_ge(mcol_done, n + 1)
                    nc.tensor.transpose(BATT[0:1, 8:8 + P], mcol[:, :], ident[:, :]).then_inc(mcolT_ready, 1)
                    transpose_probs(m, n, 1)
                if m is not None:
                    features(m, 2, odd)
                if n is not None:
                    pe.wait_ge(gmax_done, n + 1)
                    nc.tensor.matmul(BATT[:, 144:145], ones[0:1, :], gmax[:, :], start=True, stop=True).then_inc(gmax_spread, 1)
                    transpose_probs(m, n, 2)
                if m is not None:
                    features(m, 3, odd)
                if n is not None:
                    pe.wait_ge(bexp_done, n + 1)
                    for k in range(KT):
                        for t in range(TT):
                            nc.tensor.matmul(BATT[:, 148 + k:149 + k], enc[:, t, k * P:(k + 1) * P], bexp[:, t:t + 1],
                                             start=t == 0, stop=t == TT - 1)
                    for t in range(TT):
                        ins = nc.tensor.matmul(BATT[:, 152:153], ones[:, :], bexp[:, t:t + 1], start=t == 0, stop=t == TT - 1)
                    ins.then_inc(hc_ready, 1)
                    transpose_probs(m, n, 3)

            steps(nc.tensor, step)
            pe.wait_ge(hT_done, CHUNKS * 2 - 2)
            transpose_h(CHUNKS - 1)



def self_attention_phase(nc, T, w1, w2):
    ident, ident_b, mask, ones = T["ident"], T["ident_b"], T["mask"], T["ones"]
    neg_half, columns, qk_scale = T["neg_half"], T["columns"], T["qk_scale"]
    hT_all, gate_all, self_raw = T["hT_all"], T["gate_all"], T["self_raw"]
    PC = 2 * DH
    U = 2 * TT
    BLOCKS = 13
    CO, CT = PAIRS * 2, PAIRS * TT
    order = [(hh, t) for hh in range(2) for t in reversed(range(TT))]

    ctx = ExitStack()
    with ctx:
        sb = lambda name, shape, dt=f32: ctx.enter_context(nc.sbuf_tensor(name, shape, dt))
        split = lambda name, shape: (sb(name + "_hi", shape, f32r), sb(name + "_lo", shape, f32r))
        sem = lambda name: ctx.enter_context(nc.semaphore(name))
        with nc.sbuf_tensor("spare", [P, PAIRS, ROWS], f32) as spare:
            pass
        attnT_s = split("attnT_s", [P, PAIRS, ROWS])
        hT_now = spare[:, 2:2 + KT, :]
        with nc.sbuf_tensor("w_raw_early", [P, KT * FF + FF // P * D], f32) as w_raw_early:
            T["w_raw_early"] = w_raw_early
        wqkv_s = split("wqkv_s", [P, KT, PAIRS, 3, PC])
        wo_s = split("wo_s", [P, PAIRS, D])
        h_s = split("hT_s", [P, KT, ROWS])
        qT_s = [split(f"qT_s{i}", [P, ROWS]) for i in range(2)]
        kT_s = [split(f"kT_s{i}", [P, ROWS]) for i in range(2)]
        v_s = [split(f"v_s{i}", [P, TT, PC]) for i in range(2)]
        qkv = sb("qkv", [P, TT, 3, PC])
        qk_sq = sb("qk_sq", [P, 2, 2, PC])
        prob = sb("prob_b", [P, 2, ROWS])
        probT_s = [split(f"pT_s{i}", [P, BLOCKS, P]) for i in range(2)]
        scaled = sb("scaled", [P, ROWS])
        ssq = sb("ssq", [P, TT, 2, 2])
        rnorm = [sb(f"rnorm{i}", [P, TT, 2, 2]) for i in range(2)]
        rowmax, nrowmax, rowsum, rinv = (sb(n, [P, U]) for n in ("rowmax_b", "nrowmax_b", "rowsum_b", "rinv_b"))
        bn, mv = sb("bn_b", [P, TT, 6]), sb("mv_b", [P, TT, 2])
        veps, rstd = sb("veps_b", [P, TT]), sb("rstd_b", [P, TT])
        g_max, g_sum, g_inv = (sb(n, [P, TT]) for n in ("g_max", "g_sum", "g_inv"))
        g_exp = sb("g_exp", [P, TT, E])

        A = ctx.enter_context(nc.psum_tensor("psum_project", [P, 3, 512], f32))
        S = ctx.enter_context(nc.psum_tensor("psum_logits", [P, 2, 512], f32))
        PT = ctx.enter_context(nc.psum_tensor("psum_probT", [P, 2, 512], f32))
        O = ctx.enter_context(nc.psum_tensor("psum_attn", [P, 512], f32))

        expert_loaded = sem("expert_loaded")
        (w_hi, w_split, wo_hi, wo_split, h_hi, h_split) = map(
            sem, ("sw_hi", "sw_split", "wo_hi", "wo_split", "bh_hi", "bh_split"))
        (proj_ready, qk_copied, v_hi, v_split, sq_done, ssq_sum, ssq_done, norm_pow, k_done) = map(
            sem, ("proj_ready", "qk_copied", "v_hi", "v_split", "sq_done", "ssq_sum", "ssq_done", "norm_pow", "k_done"))
        (qT_ready, qT_hi, qT_split, kT_ready, kT_hi, kT_split) = map(
            sem, ("qT_ready", "qT_hi", "qT_split", "kT_ready", "kT_hi", "kT_split"))
        (s_ready, max_done, nmax_done, exp_done, pT_ready, pT_hi, pT_split) = map(
            sem, ("bs_ready", "bmax_done", "bnmax_done", "bexp_done_b", "bpT_ready", "bpT_hi", "bpT_split"))
        (rinv_done, rinv_wide, rinv_kept, o_ready, o_scaled, o_hi, o_split, wo_ready, wo_copied) = map(
            sem, ("brinv_done", "rinv_wide", "rinv_kept", "o_ready", "o_scaled", "o_hi", "o_split", "wo_ready", "wo_copied"))
        (n_stats, n_mv, n_var, n_rstd, n_done, n_ready, hT_done, hT_kept) = map(
            sem, ("n_stats", "n_mv", "n_var", "n_rstd", "n_done", "n_ready", "bhT_done", "hT_kept"))
        (g_ready, g_max_done, g_sub, g_exp_done, g_sum_done, g_inv_done, g_done) = map(
            sem, ("g_ready", "g_max_done", "g_sub", "g_exp_done", "g_sum_done", "g_inv_done", "g_done"))
        wo_banks = A[:, 0, 0:D], O[:, 0:D]
        block = ctx.enter_context(nc.Block())

        def pairs(engine, begin, pair, finish, after):
            def chunk(c, more):
                g0 = c * PAIRS if isinstance(c, int) else engine.snap(c * PAIRS)
                pair(c, g0, 0, 0, True, False, True, True)
                with engine.Fori(0, 2) as i:
                    for step in (1, 2):
                        p = engine.snap(i * 2 + step)
                        pair(c, engine.snap(g0 + p), p, step % 2, False, False, True, True)
                for p in range(5, PAIRS):
                    fresh = p == PAIRS - 1
                    pair(c, plus(engine, g0, p), p, p % 2, False, fresh, more or not fresh, p < PAIRS - 2)
                finish(c, more)

            begin()
            chunk(0, True)
            with engine.Fori(1, CHUNKS - 1) as c:
                chunk(c, True)
            chunk(CHUNKS - 1, False)
            after(CHUNKS - 1)

        def plus(engine, g, n):
            return g + n if isinstance(g, int) else engine.snap(g + n)

        def past(engine, semaphore, count):
            if not (isinstance(count, int) and count <= 0):
                engine.wait_ge(semaphore, count)

        @block.sync
        def _(sp):
            sp.wait_ge(proj_ready, CHUNKS * CT)
            load_expert(sp, w_raw_early, w1, w2, 0, expert_loaded)
            sp.wait_ge(expert_loaded, 32)

        @block.gpsimd
        def _(pool):
            def powers(g, t, odd, heads_split):
                if t == 0:
                    past(pool, exp_done, g * U - U)
                    past(pool, o_split, heads_split)
                pool.wait_ge(ssq_done, g * TT + (t + 1))
                nc.gpsimd.tensor_tensor(rnorm[odd][:, t, :, :], ssq[:, t, :, :],
                                        neg_half[:, 0:4].rearrange("p (a h) -> p a h", h=2), ALU.pow).then_inc(norm_pow, 1)

            def v_low(g, odd):
                pool.wait_ge(v_hi, g + 1)
                nc.gpsimd.tensor_tensor(v_s[odd][1][:, :, :], qkv[:, :, 2, :], v_s[odd][0][:, :, :].bitcast(f32),
                                        ALU.subtract).then_inc(v_split, 1)

            def attn_low(g, p, hh):
                pool.wait_ge(o_hi, g * 2 + (hh + 1))
                rows = slice(hh * DH, (hh + 1) * DH)
                nc.gpsimd.tensor_tensor(attnT_s[1][rows, bass.ds(p, 1), :], scaled[rows, :].unsqueeze(1),
                                        attnT_s[0][rows, bass.ds(p, 1), :].bitcast(f32), ALU.subtract).then_inc(o_split, 1)

            def begin():
                for t in range(TT):
                    powers(0, t, 0, 0)
                v_low(0, 0)

            def pair(c, g, p, odd, start, fresh, more, ahead):
                nxt = plus(pool, g, 1)
                if fresh:
                    pool.wait_ge(o_split, g * 2 - 1)
                    attn_low(g - 1, p - 1, 1)
                if more:
                    for t in range(TT):
                        powers(nxt, t, 1 - odd, g * 2 if start or fresh else g * 2 - 1)
                    v_low(nxt, 1 - odd)
                    pool.wait_ge(v_split, g + 2)
                if not start and not fresh:
                    attn_low(g - 1, p - 1, 1)
                past(pool, o_split, g * 2)
                attn_low(g, p, 0)

            def finish(c, more):
                pool.wait_ge(o_split, c * CO + CO)
                pool.wait_ge(n_var, c + 1)
                nc.gpsimd.tensor_tensor(rstd[:, :], veps[:, :], neg_half[:, 0:TT], ALU.pow).then_inc(n_rstd, 1)

            pairs(nc.gpsimd, begin, pair, finish, lambda c: None)

        @block.scalar
        def _(act):
            def split_h(c):
                past(act, proj_ready, c * CT)
                nc.scalar.activation(h_s[0][:, :, :], hT_all[:, bass.ds(c, 1), :, :].rearrange("p c k n -> p (c k) n"),
                                     ACT.Copy).then_inc(h_hi, 1)

            def from_projection(g, t):
                if t == 0:
                    past(act, qT_ready, g)
                    past(act, kT_ready, g)
                    past(act, v_split, g)
                act.wait_ge(proj_ready, g * TT + (t + 1))
                nc.scalar.activation(qkv[:, t, :, :], A[:, t % 3, 0:3 * PC].rearrange("p (a n) -> p a n", a=3), ACT.Copy).then_inc(qk_copied, 1)
                past(act, ssq_sum, g * TT + (t - 1))
                nc.scalar.activation(qk_sq[:, t % 2, :, :], A[:, t % 3, 0:2 * PC].rearrange("p (a n) -> p a n", a=2),
                                     ACT.Square).then_inc(sq_done, 1)

            def v_high(g, odd):
                past(act, o_ready, g * 2 - 2)
                act.wait_ge(qk_copied, g * TT + TT)
                nc.scalar.activation(v_s[odd][0][:, :, :], qkv[:, :, 2, :], ACT.Copy).then_inc(v_hi, 1)

            def q_high(g, p, odd):
                act.wait_ge(qT_ready, g + 1)
                past(act, s_ready, g * U - U)
                nc.scalar.activation(qT_s[odd][0][:, :], A[:, 1, :], ACT.Copy, scale=qk_scale[:, bass.ds(p, 1)]).then_inc(qT_hi, 1)

            def k_high(g, odd):
                act.wait_ge(kT_ready, g + 1)
                nc.scalar.activation(kT_s[odd][0][:, :], A[:, 2, :], ACT.Copy).then_inc(kT_hi, 1)

            def exponentials(g, u, odd):
                hh, t = order[u]
                past(act, pT_ready, g * U + (u - 1))
                act.wait_ge(nmax_done, g * U + (u + 1))
                n = (t + 1) * P
                nc.scalar.activation(prob[:, u % 2, 0:n], S[:, u % 2, 0:n], ACT.Exp, bias=nrowmax[:, u:u + 1],
                                     scale=rnorm[odd][:, t, 0, hh:hh + 1], accum_out=rowsum[:, u:u + 1]).then_inc(exp_done, 1)

            def probT_high(g, u):
                hh, t = order[u]
                if t == TT - 1:
                    past(act, o_ready, g * 2 + (hh - 1))
                act.wait_ge(pT_ready, g * U + (u + 1))
                nc.scalar.activation(probT_s[hh][0][:, t:4 * t + 1:3, :], PT[:, u % 2, 0:(t + 1) * P]
                                     .rearrange("p (j i) -> p j i", i=P), ACT.Copy).then_inc(pT_hi, 1)

            def keep_inverses(g, hh):
                past(act, o_split, g * 2 + (1 if hh else -1))
                act.wait_ge(rinv_wide, g * 2 + (hh + 1))
                rows = slice(hh * DH, (hh + 1) * DH)
                nc.scalar.activation(scaled[rows, :], A[rows, 0, :], ACT.Copy).then_inc(rinv_kept, 1)

            def attn_high(c, g, p, hh):
                past(act, wo_ready, c * TT)
                act.wait_ge(o_scaled, g * 2 + (hh + 1))
                rows = slice(hh * DH, (hh + 1) * DH)
                nc.scalar.activation(attnT_s[0][rows, bass.ds(p, 1), :], scaled[rows, :].unsqueeze(1), ACT.Copy).then_inc(o_hi, 1)

            def output_transposed(c, k):
                act.wait_ge(n_ready, c * KT + (k + 1))
                nc.scalar.activation(hT_now[:, k, :], O[:, :], ACT.Identity, scale=columns[:, COL_G + k:COL_G + k + 1],
                                     bias=columns[:, COL_B + k:COL_B + k + 1]).then_inc(hT_done, 1)

            def gate_exponentials(c):
                act.wait_ge(g_sub, c + 1)
                nc.scalar.activation(g_exp[:, :, :], g_exp[:, :, :], ACT.Exp).then_inc(g_exp_done, 1)

            def begin():
                for p in range(PAIRS):
                    for i in range(3):
                        ins = nc.scalar.activation(wqkv_s[0][:, :, p, i, :],
                                                   self_raw[:, i * KT:(i + 1) * KT, p * PC:(p + 1) * PC], ACT.Copy)
                    ins.then_inc(w_hi, 1)
                    if p == 0:
                        split_h(0)
                for t in range(TT):
                    from_projection(0, t)
                v_high(0, 0)
                q_high(0, 0, 0)
                nc.scalar.activation(wo_s[0][:, :, :], wo_raw, ACT.Copy).then_inc(wo_hi, 1)
                k_high(0, 0)
                exponentials(0, 0, 0)

            wo_raw = self_raw[:, 3 * KT:, :].rearrange("p a b -> p (a b)").rearrange("p (k d) -> p k d", d=D)

            def pair(c, g, p, odd, start, fresh, more, ahead):
                nxt, even, late = plus(act, g, 1), 1 - odd, int(fresh)
                if fresh and more:
                    split_h(plus(act, c, 1))
                for u in range(U):
                    if u < U - 1:
                        exponentials(g, u + 1, odd)
                    elif more and not fresh:
                        exponentials(nxt, 0, even)
                    probT_high(g, u)
                    if more:
                        for tiles in (((), (0, 1), (2,), (3,)) if fresh else ((0, 1, 2), (3,)) if start else ((1, 2), (3,)))[u:u + 1]:
                            for tile in tiles:
                                from_projection(nxt, tile)
                        if u == (7 if fresh else 4):
                            q_high(nxt, 0 if fresh else p + 1, even)
                            k_high(nxt, even)
                    if u == 0 and fresh or u == 2 and not start and not fresh:
                        keep_inverses(g - 1, 1)
                    if u == 1 and fresh or u == 4 and not start and not fresh:
                        attn_high(c, g - 1, p - 1, 1)
                    if u == (4 if fresh else 3) and more:
                        v_high(nxt, even)
                    if start and not (isinstance(c, int) and c == 0):
                        if u < KT:
                            output_transposed(c - 1, u)
                        if u == 3:
                            gate_exponentials(c - 1)
                    if u == 5:
                        keep_inverses(g, 0)
                    if u == 7:
                        attn_high(c, g, p, 0)
                        if ahead:
                            from_projection(plus(act, g, 2), 0)

            def finish(c, more):
                g7, nxt = plus(act, c * PAIRS, PAIRS - 1), plus(act, c * PAIRS, PAIRS)
                keep_inverses(g7, 1)
                if more:
                    exponentials(nxt, 0, 0)
                attn_high(c, g7, PAIRS - 1, 1)
                for t in range(TT):
                    act.wait_ge(wo_ready, c * TT + (t + 1))
                    nc.scalar.activation(spare[:, 0:2, t * P:(t + 1) * P], wo_banks[t % 2].rearrange("p (k n) -> p k n", k=2),
                                         ACT.Copy).then_inc(wo_copied, 1)

            def after(c):
                for k in range(KT):
                    output_transposed(c, k)
                gate_exponentials(c)

            pairs(nc.scalar, begin, pair, finish, after)

        @block.vector
        def _(dve):
            wo_raw = self_raw[:, 3 * KT:, :].rearrange("p a b -> p (a b)").rearrange("p (k d) -> p k d", d=D)

            def low(out, whole, high):
                return nc.vector.tensor_tensor(out, whole, high.bitcast(f32), ALU.subtract)

            def split_h(c):
                dve.wait_ge(h_hi, c + 1)
                low(h_s[1][:, :, :], hT_all[:, bass.ds(c, 1), :, :].rearrange("p c k n -> p (c k) n"), h_s[0][:, :, :]).then_inc(h_split, 1)

            def sum_squares(g, t):
                dve.wait_ge(sq_done, g * TT + (t + 1))
                nc.vector.reduce_sum(ssq[:, t, :, :], qk_sq[:, t % 2, :, :].rearrange("p a (h d) -> p a h d", d=DH),
                                     AX.X).then_inc(ssq_sum, 1)
                dve.wait_ge(ssq_sum, g * TT + (t + 1))
                nc.vector.tensor_scalar_add(ssq[:, t, :, :], ssq[:, t, :, :], 1e-12).then_inc(ssq_done, 1)

            def key_norms(g, t, odd):
                dve.wait_ge(norm_pow, g * TT + (t + 1))
                here = qkv[:, t, 1, :].rearrange("p (h d) -> p h d", d=DH)
                nc.vector.tensor_tensor(here, here, rnorm[odd][:, t, 1, :].unsqueeze(2).to_broadcast([P, 2, DH]), ALU.mult).then_inc(k_done, 1)

            def q_low(g, p, odd):
                dve.wait_ge(qT_hi, g + 1)
                nc.vector.scalar_tensor_tensor(out=qT_s[odd][1][:, :], in0=A[:, 1, :], scalar=qk_scale[:, bass.ds(p, 1)],
                                               in1=qT_s[odd][0][:, :].bitcast(f32), op0=ALU.mult, op1=ALU.subtract).then_inc(qT_split, 1)

            def k_low(g, odd):
                dve.wait_ge(kT_hi, g + 1)
                low(kT_s[odd][1][:, :], A[:, 2, :], kT_s[odd][0][:, :]).then_inc(kT_split, 1)

            def maximum(g, u, odd):
                hh, t = order[u]
                dve.wait_ge(s_ready, g * U + (u + 1))
                nc.vector.reduce_max(rowmax[:, u:u + 1], S[:, u % 2, 0:(t + 1) * P], AX.X).then_inc(max_done, 1)
                dve.wait_ge(max_done, g * U + (u + 1))
                nc.vector.scalar_tensor_tensor(out=nrowmax[:, u:u + 1], in0=rowmax[:, u:u + 1], scalar=-1.0,
                                               in1=rnorm[odd][:, t, 0, hh:hh + 1], op0=ALU.mult, op1=ALU.mult).then_inc(nmax_done, 1)

            def probT_low(g, u):
                hh, t = order[u]
                dve.wait_ge(pT_hi, g * U + (u + 1))
                low(probT_s[hh][1][:, t:4 * t + 1:3, :], PT[:, u % 2, 0:(t + 1) * P].rearrange("p (j i) -> p j i", i=P),
                    probT_s[hh][0][:, t:4 * t + 1:3, :]).then_inc(pT_split, 1)

            def inverse(g, hh):
                dve.wait_ge(exp_done, g * U + (hh + 1) * TT)
                half = slice(hh * TT, (hh + 1) * TT)
                nc.vector.reciprocal(rinv[:, half], rowsum[:, half]).then_inc(rinv_done, 1)

            def scale_attention(g, hh):
                rows = slice(hh * DH, (hh + 1) * DH)
                dve.wait_ge(rinv_kept, g * 2 + (hh + 1))
                dve.wait_ge(o_ready, g * 2 + (hh + 1))
                nc.vector.tensor_tensor(scaled[rows, :], O[rows, :], scaled[rows, :], ALU.mult).then_inc(o_scaled, 1)

            def keep_output(c):
                dve.wait_ge(hT_done, c * KT + KT)
                nc.vector.tensor_copy(hT_all[:, bass.ds(c, 1), :, :].rearrange("p c k n -> p (c k) n"), hT_now).then_inc(hT_kept, 1)

            def gate_logits(c):
                dve.wait_ge(g_ready, c + 1)
                logits = O[:, 0:TT * E].rearrange("p (t e) -> p t e", e=E)
                nc.vector.reduce_max(g_max[:, :], logits, AX.X).then_inc(g_max_done, 1)
                dve.wait_ge(g_max_done, c + 1)
                nc.vector.tensor_tensor(g_exp[:, :, :], logits, g_max[:, :].unsqueeze(2).to_broadcast([P, TT, E]), ALU.subtract).then_inc(g_sub, 1)

            def gate_shares(c):
                dve.wait_ge(g_exp_done, c + 1)
                nc.vector.reduce_sum(g_sum[:, :], g_exp[:, :, :], AX.X).then_inc(g_sum_done, 1)
                dve.wait_ge(g_sum_done, c + 1)
                nc.vector.reciprocal(g_inv[:, :], g_sum[:, :]).then_inc(g_inv_done, 1)
                dve.wait_ge(g_inv_done, c + 1)
                nc.vector.tensor_tensor(gate_all[:, bass.ds(c, 1), :, :].rearrange("p c t e -> p (c t) e"), g_exp[:, :, :],
                                        g_inv[:, :].unsqueeze(2).to_broadcast([P, TT, E]), ALU.mult).then_inc(g_done, 1)

            def begin():
                for p in range(PAIRS):
                    dve.wait_ge(w_hi, p + 1)
                    for i in range(3):
                        ins = low(wqkv_s[1][:, :, p, i, :], self_raw[:, i * KT:(i + 1) * KT, p * PC:(p + 1) * PC],
                                  wqkv_s[0][:, :, p, i, :])
                    ins.then_inc(w_split, 1)
                    if p == 0:
                        split_h(0)
                for t in range(TT):
                    sum_squares(0, t)
                q_low(0, 0, 0)
                for t in range(TT):
                    key_norms(0, t, 0)
                dve.wait_ge(wo_hi, 1)
                low(wo_s[1][:, :, :], wo_raw, wo_s[0][:, :, :]).then_inc(wo_split, 1)
                k_low(0, 0)
                maximum(0, 0, 0)
                maximum(0, 1, 0)

            def pair(c, g, p, odd, start, fresh, more, ahead):
                nxt, even, late = plus(dve, g, 1), 1 - odd, int(fresh)
                after_chunk = start and not (isinstance(c, int) and c == 0)
                if fresh and more:
                    split_h(plus(dve, c, 1))
                for u in range(U):
                    if u < U - 2:
                        maximum(g, u + 2, odd)
                    elif more and not fresh:
                        maximum(nxt, u + 2 - U, even)
                    if u % TT == TT - 1:
                        inverse(g, u // TT)
                    probT_low(g, u)
                    if more:
                        for tiles in (((), (0, 1), (2,), (3,)) if fresh else ((0, 1), (2, 3)))[u:u + 1]:
                            for tile in tiles:
                                sum_squares(nxt, tile)
                        for tiles in (((), (), (), (0, 1), (2, 3)) if fresh else ((), (0, 1), (2, 3)))[u:u + 1]:
                            for tile in tiles:
                                key_norms(nxt, tile, even)
                        if u == (7 if fresh else 4):
                            q_low(nxt, 0 if fresh else p + 1, even)
                            k_low(nxt, even)
                    if u == 1 and fresh or u == 3 and not start and not fresh:
                        scale_attention(g - 1, 1)
                    if after_chunk:
                        if u == 2:
                            keep_output(c - 1)
                        if u == 3:
                            gate_logits(c - 1)
                        if u == 4:
                            gate_shares(c - 1)
                    if u == 6:
                        scale_attention(g, 0)

            def finish(c, more):
                g7, nxt = plus(dve, c * PAIRS, PAIRS - 1), plus(dve, c * PAIRS, PAIRS)
                if more:
                    maximum(nxt, 0, 0)
                scale_attention(g7, 1)
                dve.wait_ge(o_hi, c * CO + CO)
                low(attnT_s[1][DH:P, PAIRS - 1, :], scaled[DH:P, :], attnT_s[0][DH:P, PAIRS - 1, :]).then_inc(o_split, 1)
                for t in range(TT):
                    dve.wait_ge(wo_copied, c * TT + (t + 1))
                    nc.vector.bn_stats(bn[:, t, :], wo_banks[t % 2]).then_inc(n_stats, 1)
                dve.wait_ge(n_stats, c * TT + TT)
                if more:
                    maximum(nxt, 1, 0)
                for t in range(TT):
                    ins = nc.vector.bn_aggr(mv[:, t, :], bn[:, t, :])
                ins.then_inc(n_mv, 1)
                dve.wait_ge(n_mv, c + 1)
                nc.vector.tensor_scalar_add(veps[:, :], mv[:, :, 1], EPS).then_inc(n_var, 1)
                dve.wait_ge(n_rstd, c + 1)
                for t in range(TT):
                    here = spare[:, 0:2, t * P:(t + 1) * P]
                    ins = nc.vector.tensor_scalar(here, here, mv[:, t, 0:1], rstd[:, t:t + 1], ALU.subtract, ALU.mult)
                ins.then_inc(n_done, 1)

            def after(c):
                keep_output(c)
                gate_logits(c)
                gate_shares(c)

            pairs(nc.vector, begin, pair, finish, after)

        @block.tensor
        def _(pe):
            THREE = ((0, 0), (1, 0), (0, 1))

            def project(g, p, t, inverses_kept=0, stats_made=0):
                bank = t % 3
                if t == 0:
                    past(pe, rinv_kept, inverses_kept)
                    past(pe, n_stats, stats_made)
                if t == 1:
                    past(pe, qT_split, g)
                if t == 2:
                    past(pe, kT_split, g)
                if t == 3:
                    pe.wait_ge(sq_done, g * TT + 1)
                steps = [(a, b, k) for a, b in THREE for k in range(KT)]
                for i, (a, b, k) in enumerate(steps):
                    ins = nc.tensor.matmul(A[:, bank, 0:3 * PC], h_s[a][:, k, t * P:(t + 1) * P],
                                           wqkv_s[b][:, k, bass.ds(p, 1), :, :].rearrange("p a b c -> p a (b c)"),
                                           start=i == 0, stop=i == len(steps) - 1)
                ins.then_inc(proj_ready, 1)

            def transpose_q(g):
                pe.wait_ge(qk_copied, g * TT + TT)
                pe.wait_ge(sq_done, g * TT + 2)
                for t in range(TT):
                    ins = nc.tensor.transpose(A[:, 1, t * P:(t + 1) * P], qkv[:, t, 0, :], ident[:, :])
                ins.then_inc(qT_ready, 1)

            def transpose_k(g):
                pe.wait_ge(sq_done, g * TT + 3)
                pe.wait_ge(k_done, g * TT + TT)
                for t in range(TT):
                    ins = nc.tensor.transpose(A[:, 2, t * P:(t + 1) * P], qkv[:, t, 1, :], ident[:, :])
                ins.then_inc(kT_ready, 1)

            def logits(g, u, odd):
                hh, t = order[u]
                if u == 0:
                    pe.wait_ge(qT_split, g + 1)
                    pe.wait_ge(kT_split, g + 1)
                past(pe, exp_done, g * U + (u - 1))
                rows = slice(hh * DH, (hh + 1) * DH)
                n = (t + 1) * P
                for i, (a, b) in enumerate(THREE):
                    nc.tensor.matmul(S[:, u % 2, 0:n], qT_s[odd][a][rows, t * P:(t + 1) * P], kT_s[odd][b][rows, 0:n],
                                     start=i == 0, stop=False, skip_group_check=True)
                nc.tensor.matmul(S[:, u % 2, t * P:n], ident_b[:, :], mask[:, :], start=False, stop=True,
                                 skip_group_check=True).then_inc(s_ready, 1)

            def transpose_probs(g, u):
                t = order[u][1]
                past(pe, pT_split, g * U + (u - 1))
                pe.wait_ge(exp_done, g * U + (u + 1))
                for j in range(t + 1):
                    ins = nc.tensor.transpose(PT[:, u % 2, j * P:(j + 1) * P], prob[:, u % 2, j * P:(j + 1) * P], ident[:, :])
                ins.then_inc(pT_ready, 1)

            def widen_inverses(g, hh, more, projected):
                past(pe, rinv_kept, g * 2 + hh)
                if more:
                    pe.wait_ge(sq_done, projected)
                pe.wait_ge(rinv_done, g * 2 + (hh + 1))
                for t in range(TT):
                    u = order.index((hh, t))
                    ins = nc.tensor.transpose(A[:, 0, t * P:(t + 1) * P], rinv[:, u:u + 1].to_broadcast([P, P]), ident[:, :])
                ins.then_inc(rinv_wide, 1)

            def attend(g, hh, odd, after_gates=None):
                past(pe, o_scaled, g * 2 + hh)
                if after_gates is not None:
                    pe.wait_ge(g_sub, after_gates)
                pe.wait_ge(v_split, g + 1)
                pe.wait_ge(pT_split, g * U + (hh + 1) * TT)
                steps = [(a, b, j) for j in range(TT) for a, b in THREE]
                for i, (a, b, j) in enumerate(steps):
                    probs = probT_s[hh][b][:, 4 * j:3 * j + TT, :].rearrange("p a b -> p (a b)")
                    ins = nc.tensor.matmul(O[:, j * P:ROWS], v_s[odd][a][:, j, :], probs,
                                           start=i == 0, stop=i == len(steps) - 1, skip_group_check=True)
                ins.then_inc(o_ready, 1)

            def output_transposes(c, k):
                if k == 0:
                    pe.wait_ge(n_stats, c * TT + TT)
                    pe.wait_ge(n_done, c + 1)
                else:
                    pe.wait_ge(hT_done, c * KT + k)
                for t in range(TT):
                    ins = nc.tensor.transpose(O[:, t * P:(t + 1) * P], spare[:, k, t * P:(t + 1) * P], ident[:, :])
                ins.then_inc(n_ready, 1)

            def gates(c):
                pe.wait_ge(hT_done, c * KT + KT)
                for t in range(TT):
                    here = slice(t * P, (t + 1) * P)
                    for k in range(KT):
                        nc.tensor.matmul(O[:, t * E:(t + 1) * E], hT_now[:, k, here], T["gate_w"][:, k, :], start=k == 0, stop=False)
                    ins = nc.tensor.matmul(O[:, t * E:(t + 1) * E], ones[0:1, :], T["gate_b"][:, :], start=False, stop=True)
                ins.then_inc(g_ready, 1)

            def begin():
                pe.wait_ge(w_split, 1)
                pe.wait_ge(h_split, 1)
                for t in range(TT):
                    project(0, 0, t)
                transpose_q(0)
                transpose_k(0)
                pe.wait_ge(w_split, PAIRS)
                logits(0, 0, 0)
                logits(0, 1, 0)

            def pair(c, g, p, odd, start, fresh, more, ahead):
                nxt, even, late = plus(pe, g, 1), 1 - odd, int(fresh)
                after_chunk = start and not (isinstance(c, int) and c == 0)
                p_next = 0 if fresh else p + 1
                for u in range(U):
                    if u < U - 2:
                        logits(g, u + 2, odd)
                    elif more and not fresh:
                        logits(nxt, u + 2 - U, even)
                    transpose_probs(g, u)
                    if u == 0 and fresh:
                        widen_inverses(g - 1, 1, False, None)
                        attend(g - 1, 1, even)
                    if more:
                        if u == late and fresh:
                            pe.wait_ge(h_split, c + 2)
                        if u == late and (start or fresh):
                            project(nxt, p_next, 0, g * 2, c * TT if after_chunk else 0)
                            project(nxt, p_next, 1)
                        if u == 2 * late:
                            project(nxt, p_next, 2)
                        if u == 1 + 2 * late:
                            project(nxt, p_next, 3)
                        if u == 3 + 2 * late:
                            transpose_q(nxt)
                            transpose_k(nxt)
                    if u == 2 and not start and not fresh:
                        widen_inverses(g - 1, 1, more, g * TT + 2 * TT)
                        attend(g - 1, 1, even)
                    if after_chunk:
                        if u < KT:
                            output_transposes(c - 1, u)
                        if u == KT:
                            gates(c - 1)
                    if u == 4 + late:
                        widen_inverses(g, 0, more, g * TT + 2 * TT)
                    if u == 5 + late:
                        attend(g, 0, odd, c if after_chunk else None)
                    if u >= U - 2 and ahead:
                        project(plus(pe, g, 2), p + 2, u + 2 - U, g * 2 + 1)

            def finish(c, more):
                g7, nxt = plus(pe, c * PAIRS, PAIRS - 1), plus(pe, c * PAIRS, PAIRS)
                widen_inverses(g7, 1, False, None)
                attend(g7, 1, 1)
                if more:
                    logits(nxt, 0, 0)
                    logits(nxt, 1, 0)
                if isinstance(c, int) and c == 0:
                    pe.wait_ge(wo_split, 1)
                pe.wait_ge(o_split, c * CO + (CO - 2))
                pe.wait_ge(rinv_kept, c * CO + CO)
                for t in range(TT):
                    if t >= 2:
                        pe.wait_ge(n_stats, c * TT + (t - 1))
                    steps = [(a, b, p) for p in range(PAIRS) for a, b in THREE]
                    for i, (a, b, p) in enumerate(steps):
                        if t == 0 and i == len(steps) - len(THREE):
                            pe.wait_ge(o_split, c * CO + CO)
                        if t == 1 and i == 0:
                            pe.wait_ge(o_scaled, c * CO + CO)
                        ins = nc.tensor.matmul(wo_banks[t % 2], attnT_s[a][:, p, t * P:(t + 1) * P], wo_s[b][:, p, :],
                                               start=i == 0, stop=i == len(steps) - 1)
                    ins.then_inc(wo_ready, 1)

            def after(c):
                for k in range(KT):
                    output_transposes(c, k)
                gates(c)

            pairs(nc.tensor, begin, pair, finish, after)


def experts_phase(nc, T, ln_g, ln_b, w1, b2, w2, x1_dram, out):
    hT_all, gate_all, columns = T["hT_all"], T["gate_all"], T["columns"]
    ident, neg_half = T["ident"], T["neg_half"]
    moe_sum = hT_all[:, :, :, :].rearrange("p c k n -> p c (k n)").rearrange("p c (t d) -> p c t d", d=D)
    KT, FT = D // P, FF // P
    LAST = E - 1

    ctx = ExitStack()
    with ctx:
        sb = lambda name, shape, dt: ctx.enter_context(nc.sbuf_tensor(name, shape, dt))
        sem = lambda name: ctx.enter_context(nc.semaphore(name))
        w_first = T["w_raw_early"]
        W1_COLS = KT * FF
        W_COLS = W1_COLS + FT * D
        w_hi = [sb(f"w_hi{i}", [P, W_COLS], f32r) for i in range(2)]
        w_raw = sb("w_raw", [P, W_COLS], f32)
        w_lo = [sb(f"w_lo{i}", [P, W_COLS], f32r) for i in range(2)]
        h_hi = sb("h2T_hi", [P, CHUNKS, KT, ROWS], f32r)
        h_lo = sb("h2T_lo", [P, CHUNKS, KT, ROWS], f32r)
        g_rows, b_rows = sb("g_rows", [P, D], f32), sb("b_rows", [P, D], f32)
        b2_sb = sb("b2_sb", [E, D], f32)
        hid = sb("hid", [P, 2, ROWS], f32)
        hid_hi = sb("hid_hi", [P, 4, ROWS], f32r)
        hid_lo = sb("hid_lo", [P, 4, ROWS], f32r)
        g_now = sb("g_now", [P, TT, E], f32)
        gT = sb("gT", [E, TT, P], f32)
        x1c = w_raw[:, 0:TT * D].rearrange("p (t d) -> p t d", d=D)
        bn = sb("bn2", [P, TT, 6], f32)
        mv = sb("mv2", [P, TT, 2], f32)
        veps = sb("veps2", [P, TT], f32)
        rstd = sb("rstd2", [P, TT], f32)
        H = ctx.enter_context(nc.psum_tensor("psum_hid", [P, 4, 512], f32))
        O = ctx.enter_context(nc.psum_tensor("psum_out", [P, 4, 2, D], f32))

        w_loaded = sem("w_loaded")
        b2_loaded = sem("b2_loaded")
        norm_loaded = sem("norm_loaded")
        w_hi_done = sem("w_hi_done")
        w_split = sem("w_split")
        h_hi_done = sem("h_hi_done")
        h_split = sem("h_split")
        g_copied = sem("g_copied")
        gT_ready = sem("gT_ready")
        gT_copied = sem("gT_copied")
        bias_ready = sem("bias_ready")
        sum_begun = sem("sum_begun")
        hid_ready = sem("hid_ready")
        gelu_done = sem("gelu_done")
        hid_hi_done = sem("hid_hi_done")
        hid_split = sem("hid_split")
        out_used = sem("out_used")
        sum_done = sem("sum_done")
        x1_loaded = sem("x1_loaded")
        stats_done = sem("stats_done")
        mv_done = sem("mv_done")
        var_done = sem("var_done")
        rstd_done = sem("rstd_done")
        norm_done = sem("norm_done")
        norm_step = sem("norm_step")
        y_done = sem("y_done")
        stored = sem("stored")
        block = ctx.enter_context(nc.Block())

        def experts(engine, run):
            run(0, 0, True, False)
            with engine.Fori(0, (E - 2) // 2) as i:
                for step in (1, 2):
                    run(engine.snap(i * 2 + step), step % 2, False, False)
            run(LAST, LAST % 2, False, True)

        def scale_and_add(engine, ops, c):
            here = moe_sum[:, c, :, :]
            engine.wait_ge(norm_done, c + 1)
            engine.wait_ge(norm_loaded, 32)
            ops.tensor_tensor(here, here, g_rows[:, :].unsqueeze(1).to_broadcast([P, TT, D]), ALU.mult).then_inc(norm_step, 1)
            engine.wait_ge(norm_step, 2 * c + 1)
            ops.tensor_tensor(here, here, b_rows[:, :].unsqueeze(1).to_broadcast([P, TT, D]), ALU.add).then_inc(norm_step, 1)
            engine.wait_ge(norm_step, 2 * c + 2)
            engine.wait_ge(x1_loaded, 16 * (c + 1))
            ops.tensor_tensor(here, here, x1c[:, :, :], ALU.add).then_inc(y_done, 1)

        def out_half(n):
            return n % 2 * 2

        def cell(e, c):
            return e * CHUNKS + c

        @block.sync
        def _(sp):
            sp.dma_start(b2_sb[:, :], b2).then_inc(b2_loaded, 16)
            sp.dma_start(g_rows[:, :], ln_g.unsqueeze(0).to_broadcast([P, D])).then_inc(norm_loaded, 16)
            sp.dma_start(b_rows[:, :], ln_b.unsqueeze(0).to_broadcast([P, D])).then_inc(norm_loaded, 16)
            with sp.Fori(1, E) as e:
                sp.wait_ge(w_split, 8 * e)
                load_expert(sp, w_raw, w1, w2, e, w_loaded)
            for c in range(CHUNKS):
                if c:
                    sp.wait_ge(y_done, c)
                    sp.wait_ge(x1_loaded, 16 * c)
                else:
                    sp.wait_ge(w_split, 8 * E)
                sp.dma_start(x1c[:, :, :], x1_dram[c, :, :, :].rearrange("t p d -> p t d")).then_inc(x1_loaded, 16)
                sp.wait_ge(y_done, c + 1)
                sp.dma_start(out[c, :, :].rearrange("(t p) d -> p t d", p=P), moe_sum[:, c, :, :]).then_inc(stored, 16)
            sp.wait_ge(stored, 16 * CHUNKS)

        @block.gpsimd
        def _(pool):
            for c in range(CHUNKS):
                pool.wait_ge(var_done, c + 1)
                nc.gpsimd.tensor_tensor(rstd[:, :], veps[:, :], neg_half[:, 0:TT], ALU.pow).then_inc(rstd_done, 1)
                if c < CHUNKS - 1:
                    scale_and_add(pool, nc.gpsimd, c)

        @block.scalar
        def _(act):
            def tokens_high(c):
                nc.scalar.activation(h_hi[:, bass.ds(c, 1), :, :], hT_all[:, bass.ds(c, 1), :, :], ACT.Copy).then_inc(h_hi_done, 1)
                if not (isinstance(c, int) and c == 0):
                    act.wait_ge(gT_ready, c)
                nc.scalar.activation(g_now[:, :, :], gate_all[:, bass.ds(c, 1), :, :].rearrange("p c t e -> p (c t) e"),
                                     ACT.Copy).then_inc(g_copied, 1)

            def gates_copied(c):
                if not (isinstance(c, int) and c == 0):
                    act.wait_ge(bias_ready, c)
                act.wait_ge(gT_ready, c + 1)
                nc.scalar.activation(gT[:, :, :], O[0:E, bass.ds(out_half(c), 1), :, :].rearrange("p o a d -> p (o a d)")
                                     .rearrange("p (t n) -> p t n", t=TT), ACT.Copy).then_inc(gT_copied, 1)

            tokens_high(0)
            gates_copied(0)
            for i in range(8):
                nc.scalar.activation(w_hi[0][:, i * 512:(i + 1) * 512], w_first[:, i * 512:(i + 1) * 512],
                                     ACT.Copy).then_inc(w_hi_done, 1)

            def gelus(e, c, first, ahead=False):
                base = act.snap(cell(e, c) * FT)
                for f in range(FT):
                    act.wait_ge(hid_ready, base + (f + 1))
                    if not first or f >= 2:
                        act.wait_ge(hid_split, base + (f - 1))
                    nc.scalar.activation(hid[:, f % 2, :], H[:, f % 4, :], ACT.Gelu_apprx_tanh,
                                         bias=columns[:, bass.ds(e * FT + (COL_B1 + f), 1)]).then_inc(gelu_done, 1)
                    if ahead and f == 0:
                        tokens_high(act.snap(c + 1))
                    if ahead and f == 3:
                        gates_copied(act.snap(c + 1))

            def run(e, odd, first, last):
                if first:
                    gelus(0, 0, True, True)
                    with nc.scalar.Fori(1, CHUNKS - 1) as c:
                        gelus(e, c, False, True)
                    gelus(e, CHUNKS - 1, False)
                else:
                    with nc.scalar.Fori(0, CHUNKS) as c:
                        gelus(e, c, False)

            experts(nc.scalar, run)

        @block.vector
        def _(dve):
            def split_weights(e, odd, i):
                cols = bass.ds(i * 512, 512)
                nc.vector.tensor_copy(w_hi[odd][:, cols], w_raw[:, cols]).then_inc(w_hi_done, 1)
                dve.wait_ge(w_hi_done, e * 8 + i + 1)
                nc.vector.tensor_tensor(w_lo[odd][:, cols], w_raw[:, cols], w_hi[odd][:, cols].bitcast(f32),
                                        ALU.subtract).then_inc(w_split, 1)

            def tokens_low(c):
                dve.wait_ge(h_hi_done, c + 1)
                nc.vector.tensor_tensor(h_lo[:, bass.ds(c, 1), :, :], hT_all[:, bass.ds(c, 1), :, :],
                                        h_hi[:, bass.ds(c, 1), :, :].bitcast(f32), ALU.subtract).then_inc(h_split, 1)

            def begin_sum(c):
                dve.wait_ge(h_split, c + 1)
                dve.wait_ge(bias_ready, c + 1)
                nc.vector.tensor_copy(moe_sum[:, bass.ds(c, 1), :, :].rearrange("p c (a t) d -> p (c a) t d", a=2),
                                      O[:, bass.ds(out_half(c), 2), :, :]).then_inc(sum_begun, 1)

            tokens_low(0)
            begin_sum(0)
            for i in range(8):
                dve.wait_ge(w_hi_done, i + 1)
                cols = slice(i * 512, (i + 1) * 512)
                nc.vector.tensor_tensor(w_lo[0][:, cols], w_first[:, cols], w_hi[0][:, cols].bitcast(f32),
                                        ALU.subtract).then_inc(w_split, 1)

            def split_hidden(base, f):
                dve.wait_ge(gelu_done, base + (f + 1))
                nc.vector.tensor_copy(hid_hi[:, f % 4, :], hid[:, f % 2, :]).then_inc(hid_hi_done, 1)
                dve.wait_ge(hid_hi_done, base + (f + 1))
                nc.vector.tensor_tensor(hid_lo[:, f % 4, :], hid[:, f % 2, :], hid_hi[:, f % 4, :].bitcast(f32),
                                        ALU.subtract).then_inc(hid_split, 1)

            def slot_free(base, f, begun):
                if begun or f >= 4:
                    dve.wait_ge(out_used, base + (f - 3))

            def add_chunk(e, c, n, first):
                dve.wait_ge(out_used, (n + 1) * FT)
                if first:
                    dve.wait_ge(sum_begun, n + 1)
                if not first:
                    dve.wait_ge(sum_done, n - (CHUNKS - 1))
                half = n % 2 * 2
                for t in range(TT):
                    ins = nc.vector.scalar_tensor_tensor(
                        out=moe_sum[:, bass.ds(c, 1), t, :], in0=O[:, bass.ds(half + t // 2, 1), t % 2, :],
                        scalar=gate_all[:, bass.ds(c, 1), t, bass.ds(e, 1)].rearrange("p a b -> p (a b)"),
                        in1=moe_sum[:, bass.ds(c, 1), t, :], op0=ALU.mult, op1=ALU.add)
                ins.then_inc(sum_done, 1)

            def final_stats(c):
                dve.wait_ge(sum_done, cell(LAST, c) + 1)
                for t in range(TT):
                    ins = nc.vector.bn_stats(bn[:, t, :], moe_sum[:, c, t, :])
                ins.then_inc(stats_done, 1)
                dve.wait_ge(stats_done, c + 1)
                for t in range(TT):
                    ins = nc.vector.bn_aggr(mv[:, t, :], bn[:, t, :])
                ins.then_inc(mv_done, 1)
                dve.wait_ge(mv_done, c + 1)
                nc.vector.tensor_scalar_add(veps[:, :], mv[:, :, 1], EPS).then_inc(var_done, 1)

            def final_norm(c):
                dve.wait_ge(rstd_done, c + 1)
                for t in range(TT):
                    ins = nc.vector.tensor_scalar(moe_sum[:, c, t, :], moe_sum[:, c, t, :], mv[:, t, 0:1], rstd[:, t:t + 1],
                                                  ALU.subtract, ALU.mult)
                ins.then_inc(norm_done, 1)

            def run(e, odd, first, last):
                def chunk(c, ahead):
                    base = dve.snap(cell(e, c) * FT)
                    for f in range(FT):
                        slot_free(base, f, True)
                        split_hidden(base, f)
                        if f == 1:
                            add_chunk(e, c - 1, dve.snap(cell(e, c - 1)), first)
                        if f == 4 and not last:
                            split_weights(e + 1, 1 - odd, c)
                        if f == 3 and last:
                            final_stats(c - 1)
                        if f == 5 and last:
                            final_norm(c - 1)
                        if ahead and f == 2:
                            tokens_low(dve.snap(c + 1))
                        if ahead and f == 5:
                            begin_sum(dve.snap(c + 1))

                for f in range(FT):
                    slot_free(cell(e, 0) * FT, f, not first)
                    split_hidden(cell(e, 0) * FT, f)
                    if first and f == 2:
                        tokens_low(1)
                    if first and f == 5:
                        begin_sum(1)
                if last:
                    for c in range(1, CHUNKS):
                        chunk(c, False)
                else:
                    dve.wait_ge(w_loaded, e * 32 + 32)
                    split_weights(e + 1, 1 - odd, 0)
                    with nc.vector.Fori(1, CHUNKS - first) as c:
                        chunk(c, first)
                    if first:
                        chunk(CHUNKS - 1, False)
                add_chunk(e, CHUNKS - 1, cell(e, CHUNKS - 1), first)

            experts(nc.vector, run)
            final_stats(CHUNKS - 1)
            final_norm(CHUNKS - 1)
            scale_and_add(dve, nc.vector, CHUNKS - 1)

        @block.tensor
        def _(pe):
            def weights1(odd, half, k, f):
                at = k * FF + f * P
                return (w_hi, w_lo)[half][odd][:, at:at + P]

            def weights2(odd, half, f):
                at = W1_COLS + f * D
                return (w_hi, w_lo)[half][odd][:, at:at + D]

            def up(odd, c, f, base):
                if base is not None:
                    pe.wait_ge(gelu_done, base + (f - 3))
                steps = [(a, b, k) for a, b in ((0, 0), (1, 0), (0, 1)) for k in range(KT)]
                for i, (a, b, k) in enumerate(steps):
                    ins = nc.tensor.matmul(H[:, f % 4, :], weights1(odd, a, k, f),
                                           (h_hi, h_lo)[b][:, bass.ds(c, 1), k, :],
                                           start=i == 0, stop=i == len(steps) - 1)
                ins.then_inc(hid_ready, 1)

            def down(odd, f, n):
                pe.wait_ge(hid_split, n * FT + (f + 1))
                half = n % 2 * 2
                for t in range(TT):
                    for i, (a, b) in enumerate(((0, 0), (1, 0), (0, 1))):
                        tokens = (hid_hi, hid_lo)[a][:, f % 4, t * P:(t + 1) * P]
                        ins = nc.tensor.matmul(O[:, bass.ds(half + t // 2, 1), t % 2, :], tokens, weights2(odd, b, f),
                                               start=f == 0 and i == 0 and t % 2 == 0,
                                               stop=f == FT - 1 and i == 2, skip_group_check=True)
                ins.then_inc(out_used, 1)

            def gates_transposed(half):
                for t in range(TT):
                    ins = nc.tensor.transpose(O[0:E, half, t // 2, t % 2 * P:(t % 2 + 1) * P], g_now[:, t, :], ident[:, :])
                ins.then_inc(gT_ready, 1)

            def biases(half):
                for t in range(TT):
                    ins = nc.tensor.matmul(O[:, half + t // 2, t % 2, :], gT[:, t, :], b2_sb[:, :],
                                           start=t % 2 == 0, stop=True, skip_group_check=True)
                ins.then_inc(bias_ready, 1)

            pe.wait_ge(g_copied, 1)
            gates_transposed(0)
            pe.wait_ge(b2_loaded, 16)
            pe.wait_ge(gT_copied, 1)
            biases(0)
            pe.wait_ge(w_split, 4)
            pe.wait_ge(h_split, 1)
            up(0, 0, 0, None)
            up(0, 0, 1, None)
            pe.wait_ge(w_split, 8)

            def run(e, odd, first, last):
                def chunk(c, closing, begun, half_after=None):
                    n = pe.snap(cell(e, c))
                    base = pe.snap(n * FT)
                    for f in range(FT):
                        if f < FT - 2:
                            up(odd, c, f + 2, base if begun or f + 2 >= 4 else None)
                        elif not closing:
                            if first and f == FT - 2:
                                pe.wait_ge(h_split, c + 2)
                            up(odd, c + 1, f + 2 - FT, base + FT)
                        elif not last:
                            if f == FT - 2:
                                pe.wait_ge(w_split, e * 8 + 16)
                            up(1 - odd, 0, f + 2 - FT, base + FT)
                        if f == 0 and begun and not first:
                            pe.wait_ge(sum_done, n - 1)
                        if f == 0 and first:
                            pe.wait_ge(sum_begun, c + 1)
                        if first and not closing and f == 2:
                            pe.wait_ge(g_copied, c + 2)
                            if begun:
                                pe.wait_ge(sum_done, c)
                        if first and not closing and f == 4:
                            pe.wait_ge(gT_copied, c + 2)
                        down(odd, f, n)
                        if first and not closing and f == 2:
                            gates_transposed(half_after)
                        if first and not closing and f == 4:
                            biases(half_after)

                if first:
                    chunk(0, False, False, out_half(1))
                    with nc.tensor.Fori(0, (CHUNKS - 2) // 2) as i:
                        for step in (1, 2):
                            chunk(pe.snap(i * 2 + step), False, True, out_half(step + 1))
                else:
                    with nc.tensor.Fori(0, CHUNKS - 1) as c:
                        chunk(c, False, True)
                chunk(CHUNKS - 1, True, True)

            experts(nc.tensor, run)


def xattn_ffn_kernel(nc, x, context, w_sim, b_sim, W_qv, b_qv, ln_g, ln_b, Wq, Wk, Wv, q_scale, k_scale, Wo,
                     gate_w, gate_b, w1, b1, w2, b2, out):
    x1_dram = nc.dram_tensor("x1_kept", (CHUNKS, TT, P, D), f32, kind="Internal").ap()
    with ExitStack() as ctx:
        T = {}
        for name, shape, dt in (("hT_all", [P, CHUNKS, KT, ROWS], f32), ("gate_all", [P, CHUNKS, TT, E], f32),
                                ("columns", [P, N_COLS], f32), ("ident", [P, P], f32), ("ident_b", [P, P], bf16),
                                ("mask", [P, P], bf16), ("ones", [P, P], f32), ("neg_half", [P, 8], f32),
                                ("qk_scale", [P, PAIRS], f32), ("gate_w", [P, KT, E], f32), ("gate_b", [1, E], f32)):
            T[name] = ctx.enter_context(nc.sbuf_tensor(name, shape, dt))
        setup_phase(nc, T, w_sim, ln_g, ln_b, q_scale, k_scale, gate_w, gate_b, b1)
        with nc.sbuf_tensor("self_raw", [P, 3 * KT + 2, HEADS * DH], f32) as self_raw:
            T["self_raw"] = self_raw
            cross_attention_phase(nc, T, x, context, W_qv, b_qv, b_sim, Wq, Wk, Wv, Wo, x1_dram)
        self_attention_phase(nc, T, w1, w2)
        experts_phase(nc, T, ln_g, ln_b, w1, b2, w2, x1_dram, out)


_INS = ['x', 'ctx_1024', 'L0_xattn_w_sim', 'L0_xattn_b_sim', 'L0_xattn_W_qv', 'L0_xattn_b_qv', 'L0_ffn_ln_g',
        'L0_ffn_ln_b', 'L0_ffn_Wq', 'L0_ffn_Wk', 'L0_ffn_Wv', 'L0_ffn_q_scale', 'L0_ffn_k_scale', 'L0_ffn_Wo',
        'L0_ffn_gate_w', 'L0_ffn_gate_b', 'L0_ffn_w1', 'L0_ffn_b1', 'L0_ffn_w2', 'L0_ffn_b2']
_OUTS = [((8, 512, 256), 'float32')]


def kernel(**inputs):
    import numpy as _np
    import concourse.bacc as _bacc
    from concourse import mybir as _mybir
    from concourse.bass_utils import run_bass_kernel_spmd as _run

    nc = _bacc.Bacc("TRN2", target_bir_lowering=False, num_devices=1)
    arrays, args = {}, []
    for name in _INS:
        a = _np.ascontiguousarray(inputs[name])
        arrays[f"in_{name}_dram"] = a
        args.append(nc.dram_tensor(f"in_{name}_dram", a.shape, _mybir.dt.from_np(a.dtype), kind="ExternalInput").ap())
    for i, (shape, dtype) in enumerate(_OUTS):
        dt = _mybir.dt.from_np(_np.dtype(dtype))
        args.append(nc.dram_tensor(f"out_{i}_dram", shape, dt, kind="ExternalOutput").ap())
    xattn_ffn_kernel(nc, *args)
    r = _run(nc, [arrays], core_ids=[0])
    got = tuple(r.results[0][f"out_{i}_dram"] for i in range(len(_OUTS)))
    return got[0]
```
